# Optimizing a Trainium2 kernel written in Bass

```python
import numpy as np
import jax
import jax.numpy as jnp

def _softmax(x, axis=-1):
    return jax.nn.softmax(x, axis=axis)

def _gelu(x):
    return jax.nn.gelu(x, approximate=True)

def _silu(x):
    return jax.nn.silu(x)

def _sigmoid(x):
    return jax.nn.sigmoid(x)

def _layernorm(x, axis=-1, eps=1e-05):
    m = jnp.mean(x, axis=axis, keepdims=True)
    v = jnp.var(x, axis=axis, keepdims=True)
    return (x - m) / jnp.sqrt(v + eps)

def _scatter_add(tgt, idx, src, axis=0):
    return tgt.at[idx].add(src)

def _segment_sum(src, seg, n):
    return jax.ops.segment_sum(src, seg, n)
kernel_name = 'mk_gnn_preln_d2_gnn_r16_4a58ac'

def setup_inputs(seed: int=0):
    np.random.seed(seed)
    _w = jnp.asarray

    def _rec_inputs():
        import jax
        import jax.numpy as jnp
        _gk = jax.random.key(seed)
        x = -8.776e-05 + 1 * jax.random.normal(jax.random.fold_in(_gk, 1), (5000, 64), jnp.float32)
        _s = jax.random.randint(jax.random.fold_in(_gk, 2), (80000,), 0, 5000, jnp.int32)
        _d = jax.random.randint(jax.random.fold_in(_gk, 3), (80000,), 0, 5000, jnp.int32)
        _loop = jnp.arange(5000, dtype=jnp.int32)
        src = jnp.concatenate([_s, _d, _loop])
        dst = jnp.concatenate([_d, _s, _loop])
        _o = jnp.argsort(dst, stable=True)
        src = src[_o]
        dst = dst[_o]
        edge_attr_64 = 2.93046e-05 + 1.00006 * jax.random.normal(jax.random.fold_in(_gk, 12), (165000, 64), jnp.float32)
        edge_weight = jax.random.uniform(jax.random.fold_in(_gk, 14), (165000,), jnp.float32, 0.0, 1)
        return (x, src, dst, edge_attr_64, edge_weight)
    x, src, dst, edge_attr_64, edge_weight = _rec_inputs()

    def _L0_gnn_setup():
        import jax, jax.numpy as jnp
        import numpy as np
        N, E, D, L = (5000, 80000, 64, 4)
        EPS = 1e-07
        LN_EPS = 1e-05

        def _ln(h, g, b):
            mu = h.mean(-1, keepdims=True)
            var = ((h - mu) ** 2).mean(-1, keepdims=True)
            return (h - mu) / jnp.sqrt(var + LN_EPS) * g + b

        def _genconv(x, src, dst, ea, W1, b1, lg, lb, W2, b2, t):
            m = jax.nn.relu(x[src] + ea) + EPS
            logits = m * t
            mx = jax.ops.segment_max(logits, dst, num_segments=N)
            e = jnp.exp(logits - mx[dst])
            denom = jax.ops.segment_sum(e, dst, num_segments=N)
            alpha = e / denom[dst]
            agg = jax.ops.segment_sum(m * alpha, dst, num_segments=N)
            h = agg + x
            h = h @ W1 + b1
            h = jax.nn.relu(_ln(h, lg, lb))
            return h @ W2 + b2
        key = jax.random.key(seed)
        ks = jax.random.split(key, 10)
        g = lambda k, shape: jax.random.normal(k, shape, jnp.float32) * 0.05
        return {'x': jax.random.normal(ks[0], (N, D), jnp.float32), 'edge_index': jax.random.randint(ks[1], (2, E), 0, N), 'edge_attr': jax.random.normal(ks[2], (E, D), jnp.float32), 'encW': g(ks[3], (D, D)), 'encb': jnp.zeros((D,), jnp.float32), 'eencW': g(ks[4], (D, D)), 'eencb': jnp.zeros((D,), jnp.float32), 'convW1': g(ks[5], (L, D, 2 * D)), 'convb1': jnp.zeros((L, 2 * D), jnp.float32), 'convLnG': jnp.ones((L, 2 * D), jnp.float32), 'convLnB': jnp.zeros((L, 2 * D), jnp.float32), 'convW2': g(ks[6], (L, 2 * D, D)), 'convb2': jnp.zeros((L, D), jnp.float32), 't': jnp.ones((L,), jnp.float32), 'normG': jnp.ones((L, D), jnp.float32), 'normB': jnp.zeros((L, D), jnp.float32), 'linW': g(ks[7], (D, D)), 'linb': jnp.zeros((D,), jnp.float32)}
    _L0_gnn_all = _L0_gnn_setup()
    _L0_gnn_in = {k: v for k, v in _L0_gnn_all.items() if k in ('encW', 'encb', 'eencW', 'eencb', 'convW1', 'convb1', 'convLnG', 'convLnB', 'convW2', 'convb2', 't', 'normG', 'normB', 'linW', 'linb')}
    del _L0_gnn_all

    def _L1_gnn_setup():
        import jax, jax.numpy as jnp
        import numpy as np
        N_NODES = 6250
        N_EDGES = 62500
        D_FEAT = 64
        key = jax.random.key(seed)
        k1, k2, k3, k4 = jax.random.split(key, 4)
        feat = jax.random.normal(k1, (N_NODES, D_FEAT), dtype=jnp.float32)
        edge_weight = jax.random.uniform(k2, (N_EDGES,), dtype=jnp.float32)
        edge_src = jax.random.randint(k3, (N_EDGES,), 0, N_NODES, dtype=jnp.int64)
        edge_dst = jax.random.randint(k4, (N_EDGES,), 0, N_NODES, dtype=jnp.int64)
        return {'feat': feat, 'edge_weight': edge_weight, 'edge_src': edge_src, 'edge_dst': edge_dst}
    _L1_gnn_all = _L1_gnn_setup()
    _L1_gnn_in = {k: v for k, v in _L1_gnn_all.items() if k in ()}
    del _L1_gnn_all
    return {'x': x, 'src': src, 'dst': dst, 'edge_attr_64': edge_attr_64, 'edge_weight': edge_weight, 'L0_gnn_encW': _L0_gnn_in['encW'], 'L0_gnn_encb': _L0_gnn_in['encb'], 'L0_gnn_eencW': _L0_gnn_in['eencW'], 'L0_gnn_eencb': _L0_gnn_in['eencb'], 'L0_gnn_convW1': _L0_gnn_in['convW1'], 'L0_gnn_convb1': _L0_gnn_in['convb1'], 'L0_gnn_convLnG': _L0_gnn_in['convLnG'], 'L0_gnn_convLnB': _L0_gnn_in['convLnB'], 'L0_gnn_convW2': _L0_gnn_in['convW2'], 'L0_gnn_convb2': _L0_gnn_in['convb2'], 'L0_gnn_t': _L0_gnn_in['t'], 'L0_gnn_normG': _L0_gnn_in['normG'], 'L0_gnn_normB': _L0_gnn_in['normB'], 'L0_gnn_linW': _L0_gnn_in['linW'], 'L0_gnn_linb': _L0_gnn_in['linb']}

def reference(x, src, dst, edge_attr_64, edge_weight, L0_gnn_encW, L0_gnn_encb, L0_gnn_eencW, L0_gnn_eencb, L0_gnn_convW1, L0_gnn_convb1, L0_gnn_convLnG, L0_gnn_convLnB, L0_gnn_convW2, L0_gnn_convb2, L0_gnn_t, L0_gnn_normG, L0_gnn_normB, L0_gnn_linW, L0_gnn_linb):
    import jax
    import jax.numpy as jnp

    def _L0_gnn_ref(x, edge_index, edge_attr, encW, encb, eencW, eencb, convW1, convb1, convLnG, convLnB, convW2, convb2, t, normG, normB, linW, linb):
        import jax, jax.numpy as jnp
        import numpy as np
        N, E, D, L = (5000, 80000, 64, 4)
        EPS = 1e-07
        LN_EPS = 1e-05

        def _ln(h, g, b):
            mu = h.mean(-1, keepdims=True)
            var = ((h - mu) ** 2).mean(-1, keepdims=True)
            return (h - mu) / jnp.sqrt(var + LN_EPS) * g + b

        def _genconv(x, src, dst, ea, W1, b1, lg, lb, W2, b2, t):
            m = jax.nn.relu(x[src] + ea) + EPS
            logits = m * t
            mx = jax.ops.segment_max(logits, dst, num_segments=N)
            e = jnp.exp(logits - mx[dst])
            denom = jax.ops.segment_sum(e, dst, num_segments=N)
            alpha = e / denom[dst]
            agg = jax.ops.segment_sum(m * alpha, dst, num_segments=N)
            h = agg + x
            h = h @ W1 + b1
            h = jax.nn.relu(_ln(h, lg, lb))
            return h @ W2 + b2
        src, dst = (edge_index[0], edge_index[1])
        x = x @ encW + encb
        ea = edge_attr @ eencW + eencb
        x = _genconv(x, src, dst, ea, convW1[0], convb1[0], convLnG[0], convLnB[0], convW2[0], convb2[0], t[0])
        for i in range(1, L):
            h = jax.nn.relu(_ln(x, normG[i], normB[i]))
            h = _genconv(h, src, dst, ea, convW1[i], convb1[i], convLnG[i], convLnB[i], convW2[i], convb2[i], t[i])
            x = x + h
        x = jax.nn.relu(_ln(x, normG[0], normB[0]))
        return x @ linW + linb

    def _L1_gnn_ref(feat, edge_weight, edge_src, edge_dst):
        import jax, jax.numpy as jnp
        import numpy as np
        N_NODES = 6250
        N_EDGES = 62500
        D_FEAT = 64
        msgs = feat[edge_dst] * edge_weight[:, None]
        out = jax.ops.segment_sum(msgs, edge_src, num_segments=feat.shape[0])
        return out
    edge_index = jnp.stack([src, dst])
    h = jnp.maximum(_layernorm(x, axis=-1), 0.0)
    x = x + _L0_gnn_ref(h, edge_index, edge_attr_64, L0_gnn_encW, L0_gnn_encb, L0_gnn_eencW, L0_gnn_eencb, L0_gnn_convW1, L0_gnn_convb1, L0_gnn_convLnG, L0_gnn_convLnB, L0_gnn_convW2, L0_gnn_convb2, L0_gnn_t, L0_gnn_normG, L0_gnn_normB, L0_gnn_linW, L0_gnn_linb)
    h = jnp.maximum(_layernorm(x, axis=-1), 0.0)
    x = x + _L1_gnn_ref(h, edge_weight, src, dst)
    return x

_drawn_inputs = setup_inputs


def setup_inputs(seed=0):
    import zlib

    import numpy as np

    out = dict(_drawn_inputs(seed))
    spreads = {'L0_gnn_encb': (0.0, 0.1),
     'L0_gnn_eencb': (0.0, 0.1),
     'L0_gnn_convb1': (0.0, 0.1),
     'L0_gnn_convLnG': (1.0, 0.2),
     'L0_gnn_convLnB': (0.0, 0.1),
     'L0_gnn_convb2': (0.0, 0.1),
     'L0_gnn_t': (1.0, 0.2),
     'L0_gnn_normG': (1.0, 0.2),
     'L0_gnn_normB': (0.0, 0.1),
     'L0_gnn_linb': (0.0, 0.1)}
    factors = {}
    for name, (base, spread) in spreads.items():
        noise = np.random.default_rng([zlib.crc32(name.encode()), seed]).standard_normal(out[name].shape)
        drawn = base * np.exp(spread * noise) if base else spread * noise
        out[name] = jnp.asarray(drawn.astype(out[name].dtype))
    for name, factor in factors.items():
        out[name] = (out[name] * factor).astype(out[name].dtype)
    return out
```

```python
from contextlib import ExitStack

import concourse.bass as bass
from concourse import mybir

F32 = mybir.dt.float32
BF16 = mybir.dt.bfloat16
I32 = mybir.dt.int32
ALU = mybir.AluOpType
ACT = mybir.ActivationFunctionType
AX_X = mybir.AxisListType.X

P = 128
N, D, E, L = 5000, 64, 165000, 4
D2 = 2 * D
NT = N // 125
NPAD = P * NT
K = 12
W = P * K
NW = 54
HALF = NW * W
EPAD = 2 * HALF
GT = 4
NG = K // GT
GC = GT * P
B_REAL = E - HALF - (NW - 1) * W
B_PARTS = B_REAL // K
FLAT = EPAD // P
FLAT_REAL = E - (P - 1) * FLAT
TILES = EPAD // P
BIG = float(2.0 ** 126)
EPS = 1e-7
LN_EPS = 1e-5
NC_CHUNK = 5
CT = NT // NC_CHUNK
ACCS = 8
BATCH = ACCS // 2
TRASH = NPAD
assert B_PARTS * K == B_REAL and NPAD == 5120 and FLAT * P == EPAD


class Chain:

    def __init__(self, eng, sem, base=0):
        self.eng, self.sem, self.base, self.n = eng, sem, base, 0

    def __call__(self, ins):
        self.n += 1
        ins.then_inc(self.sem, 1)
        self.eng.wait_ge(self.sem, self.base + self.n)


def layer_norm(v, link, out, x, tmp, stats, width, act_signals):
    n = x.shape[1]
    mean, var, inv = stats[:, 0, 0:n], stats[:, 1, 0:n], stats[:, 2, 0:n]
    centred, squared, rooted, count = act_signals
    link(v.tensor_reduce(mean, x, AX_X, ALU.add))
    link(v.tensor_scalar(mean, mean, 1.0 / width, None, ALU.mult))
    v.tensor_tensor(out, x, mean.unsqueeze(2).broadcast_to([P, n, width]), ALU.subtract).then_inc(centred, 1)
    v.wait_ge(squared, count)
    link(v.tensor_reduce(var, tmp, AX_X, ALU.add))
    v.tensor_scalar(var, var, 1.0 / width, LN_EPS, ALU.mult, ALU.add).then_inc(centred, 1)
    v.wait_ge(rooted, count)
    link(v.reciprocal(inv, var))
    link(v.tensor_tensor(out, out, inv.unsqueeze(2).broadcast_to([P, n, width]), ALU.mult))


def layer_norm_scalar(a, out, tmp, stats, n, act_signals):
    centred, squared, rooted, count = act_signals
    a.wait_ge(centred, 2 * count - 1)
    a.activation(tmp, out, ACT.Square).then_inc(squared, 1)
    a.wait_ge(centred, 2 * count)
    a.activation(stats[:, 1, 0:n], stats[:, 1, 0:n], ACT.Sqrt).then_inc(rooted, 1)


def gnn(nc, x, src, dst, edge_attr, edge_weight, encW, encb, eencW, eencb, W1, b1, lnG, lnB, W2, b2,
        t, normG, normB, linW, linb, out):
    def dram(name, shape, dt=F32):
        return nc.dram_tensor(name, shape, dt).ap()

    src_win = dram("src_win", [NW, P, 2 * K], I32)
    dst_win = dram("dst_win", [NW, P, 2 * K], I32)
    wgt_win = dram("wgt_win", [NW, P, 2 * K])
    src_flat = dram("src_flat", [EPAD])
    dst_tab = dram("dst_tab", [TILES + 1, P])
    run_pen = dram("run_pen", [EPAD + 16], BF16)
    cnt_tab = dram("cnt_tab", [NPAD])
    attr_t = dram("attr_t", [NW, P, W])
    h_tab = dram("h_tab", [NPAD, D])
    sums = dram("sums", [EPAD + P, D2])
    acc = [dram(f"acc{i}", [NPAD + P, D]) for i in range(ACCS)]
    ZROW = EPAD

    with ExitStack() as whole:
        def sb(name, shape, dt=F32, ctx=whole):
            return ctx.enter_context(nc.sbuf_tensor(name, shape, dt))[tuple([slice(None)] * len(shape))]

        def sem(name):
            return whole.enter_context(nc.semaphore(name))

        ident = sb("ident", [P, P])
        ones = sb("ones", [P, P])
        attrW = sb("attrW", [P, P])
        attrB = sb("attrB", [P, 1])
        last_idx = sb("last_idx", [P, NT], I32)
        win_hot = sb("win_hot", [P, NW])
        patch_i = sb("patch_i", [P, 2], I32)
        cpen = sb("cpen", [1, 1])
        x_acc = sb("x_acc", [P, NT, D])
        h_cur = sb("h_cur", [P, NT, D])
        W1s = sb("W1s", [D, L, D2])
        W2s = sb("W2s", [D2, L, D])
        b1s = sb("b1s", [P, L, D2])
        lnGs = sb("lnGs", [P, L, D2])
        lnBs = sb("lnBs", [P, L, D2])
        b2s = sb("b2s", [P, L, D])
        nGs = sb("nGs", [P, L, D])
        nBs = sb("nBs", [P, L, D])
        ts = sb("ts", [P, L])
        linWs = sb("linWs", [D, D])
        linbs = sb("linbs", [P, D])
        stats = sb("stats", [P, 3, NT])

        ps = [whole.enter_context(nc.psum_tensor(f"ps{i}", [P, 512], F32))[:, :] for i in range(8)]

        with ExitStack() as c:
            s_list = sb("s_list", [P, NW, 2, K], I32, c)
            d_list = sb("d_list", [P, NW, 2, K], I32, c)
            w_list = sb("w_list", [P, NW, 2, K], F32, c)
            dflat_i = sb("dflat_i", [P, FLAT], I32, c)
            sflat_i = sb("sflat_i", [P, FLAT], I32, c)
            dflat = sb("dflat", [P, FLAT], F32, c)
            sflat = sb("sflat", [P, FLAT], F32, c)
            dprev = sb("dprev", [P, FLAT], F32, c)
            pen = sb("pen", [P, FLAT], BF16, c)
            padrow = sb("padrow", [1, P], F32, c)
            tlast = sb("tlast", [1, TILES], F32, c)
            tlast_b = sb("tlast_b", [P, TILES], F32, c)
            junk = sb("junk", [P, TILES], F32, c)
            node_i = sb("node_i", [P, NT], I32, c)
            node = sb("node", [P, NT], F32, c)
            cnt_t = sb("cnt_t", [P, NT], F32, c)
            cnt_i = sb("cnt_i", [P, NT], I32, c)
            cnt_r = sb("cnt_r", [P, NT], F32, c)
            before = sb("before", [P, NT], F32, c)
            rows = sb("rows", [P, NT, P], F32, c)
            b_first_i = sb("b_first_i", [P, 1], I32, c)
            b_first = sb("b_first", [P, 1], F32, c)
            b_cnt = sb("b_cnt", [P, 1], F32, c)
            b_last = sb("b_last", [P, 2], F32, c)
            win_i = sb("win_i", [P, NW], I32, c)
            win_f = sb("win_f", [P, NW], F32, c)
            win_le = sb("win_le", [P, NW], F32, c)
            pen_end = sb("pen_end", [1, 16], BF16, c)
            cpen_b = sb("cpen_b", [1, 1], BF16, c)
            zero = sb("zero", [P, (NT + 1) * D], F32, c)
            encWs = sb("encWs", [D, D], F32, c)
            encbs = sb("encbs", [P, D], F32, c)
            xn = sb("xn", [P, NT, D], F32, c)
            xnT = sb("xnT", [D, 2, 512], F32, c)
            ea = [sb(f"ea{i}", [P, 2, K, D], F32, c) for i in range(2)]
            eaT = [sb(f"eaT{i}", [P, W], F32, c) for i in range(2)]

            cleared, pool_made, id_made = sem("cleared"), sem("pool_made"), sem("id_made")
            in_dst, in_src, in_lists, in_par, in_x, in_enc, in_bfirst = (
                sem(f"in_{n}") for n in ("dst", "src", "lists", "par", "x", "enc", "bfirst"))
            in_prev, in_tlast, in_rows, in_cnt, in_cpen = (
                sem(f"in_{n}") for n in ("prev", "tlast", "rows", "cnt", "cpen"))
            out_lists, out_dst, out_pen, out_src, out_zero, out_cnt = (
                sem(f"out_{n}") for n in ("lists", "dst", "pen", "src", "zero", "cnt"))
            dst_f, src_f, pen_f, tlast_ps, bcnt_ok, bcnt_ps, tiles_ok, cnt_ok = (
                sem(f"has_{n}") for n in ("dstf", "srcf", "penf", "tlastps", "bcnt", "bcntps", "tiles", "cnt"))
            tlast_sb, xn_ok, xnT_ps, xnT_sb, enc_ps, enc_sb= (
                sem(f"has_{n}") for n in ("tlastsb", "xn", "xnTps", "xnTsb", "encps", "encsb"))
            ln0 = tuple(sem(f"ln0_{n}") for n in ("centred", "squared", "rooted")) + (1,)
            set_step, in_attrw = sem("set_step"), sem("in_attrw")
            ea_in = [sem("ea_in0"), sem("ea_in1")]
            ea_out = [sem("ea_out0"), sem("ea_out1")]
            eaT_ps, eaT_sb = sem("eaT_ps"), sem("eaT_sb")
            N_CLEAR = 10

            with nc.Block() as block:
                @block.sync
                def _(sp):
                    def load(w, b, parts=P):
                        for h in range(2):
                            n = parts if h else P
                            flat = edge_attr[bass.ds(h * HALF + w * W, n * K), :]
                            sp.dma_start(ea[b][0:n, h, :, :], flat.rearrange("(p k) f -> p k f", k=K)
                                         ).then_inc(ea_in[b], 16)

                    def store(w, b):
                        sp.wait_ge(eaT_sb, NG * (w + 1))
                        sp.dma_start(attr_t[w], eaT[b][:, :]).then_inc(ea_out[b], 16)

                    load(0, 0)
                    load(1, 1)
                    with sp.Fori(0, NW // 2 - 2) as i:
                        for b in range(2):
                            sp.wait_ge(eaT_ps, NG * (2 * i + b + 1))
                            load(2 * i + 2 + b, b)
                            store(2 * i + b, b)
                    sp.wait_ge(eaT_ps, NG * (NW - 3))
                    load(NW - 2, 0)
                    store(NW - 4, 0)
                    sp.wait_ge(eaT_ps, NG * (NW - 2))
                    load(NW - 1, 1, B_PARTS)
                    store(NW - 3, 1)
                    store(NW - 2, 0)
                    store(NW - 1, 1)
                    for b in range(2):
                        sp.wait_ge(ea_out[b], 16 * (NW // 2))

                @block.gpsimd
                def _(g):
                    g.iota(node_i[:, :], [[1, NT]], 0, NT).then_inc(pool_made, 1)
                    g.iota(win_i[:, :], [[W, NW]], HALF, 0).then_inc(pool_made, 1)
                    g.wait_ge(cleared, N_CLEAR)
                    g.affine_select(out=ident[:, :], in_=ident[:, :], compare_op=ALU.not_equal, fill=1.0, base=0,
                                    pattern=[[-1, P]], channel_multiplier=1).then_inc(id_made, 1)
                    real = (P - 1) * FLAT
                    for dest, flat, done in ((dflat_i, dst, in_dst), (sflat_i, src, in_src)):
                        g.dma_start(dest[0:P - 1, :], flat[0:real].rearrange("(p i) -> p i", i=FLAT)).then_inc(done, 16)
                        g.dma_start(dest[P - 1:P, 0:FLAT_REAL], flat[real:E].unsqueeze(0)).then_inc(done, 16)
                    g.dma_start(b_first_i[:, :], dst[HALF:HALF + 1].partition_broadcast(P)).then_inc(in_bfirst, 16)
                    g.dma_start(attrW[0:D, 0:D], eencW).then_inc(in_attrw, 16)
                    g.dma_start(attrW[D:D2, D:D2], eencW).then_inc(in_attrw, 16)
                    g.dma_start(sums[ZROW:ZROW + P, :], zero[:, 0:D2]).then_inc(out_zero, 16)
                    for a in acc:
                        g.dma_start(a.rearrange("(p t) d -> p (t d)", p=P), zero[:, :]).then_inc(out_zero, 16)

                    dst_flat = dst_tab.rearrange("a b -> (a b)")
                    g.wait_ge(dst_f, 1)
                    g.dma_start(dst_flat[0:EPAD].rearrange("(p i) -> p i", i=FLAT), dflat[:, :]).then_inc(out_dst, 16)
                    g.dma_start(dst_tab[TILES:TILES + 1, :], padrow[:, :]).then_inc(out_dst, 16)
                    g.wait_ge(out_dst, 32)
                    g.dma_start(dprev[0:1, 1:FLAT], dst_flat[0:FLAT - 1].unsqueeze(0)).then_inc(in_prev, 16)
                    g.dma_start(dprev[1:P, :], dst_flat[FLAT - 1:FLAT - 1 + (P - 1) * FLAT]
                                .rearrange("(p i) -> p i", i=FLAT)).then_inc(in_prev, 16)
                    g.dma_start(tlast[:, :], dst_tab[0:TILES, P - 1:P].rearrange("a b -> b a"),
                                allow_slow_non_contiguous=True).then_inc(in_tlast, 16)
                    g.wait_ge(src_f, 1)
                    g.dma_start(src_flat.rearrange("(p i) -> p i", i=FLAT), sflat[:, :]).then_inc(out_src, 16)
                    g.wait_ge(pen_f, 1)
                    g.dma_start(run_pen[0:EPAD].rearrange("(p i) -> p i", i=FLAT), pen[:, :]).then_inc(out_pen, 16)
                    g.dma_start(run_pen[EPAD:EPAD + 16].unsqueeze(0), pen_end[:, :]).then_inc(out_pen, 16)
                    g.wait_ge(out_pen, 32)
                    g.dma_start(cpen_b[:, :], run_pen[HALF:HALF + 1].unsqueeze(0)).then_inc(in_cpen, 16)

                    g.wait_ge(tiles_ok, 1)
                    for t in range(NT):
                        g.indirect_dma_start(rows[:, t, :], None, dst_tab[:, :], bass.IndirectOffsetOnAxis(
                            ap=cnt_i[:, t:t + 1], axis=0)).then_inc(in_rows, 16)
                    g.wait_ge(cnt_ok, 1)
                    g.dma_start(cnt_tab.rearrange("(p t) -> p t", t=NT), cnt_r[:, :]).then_inc(out_cnt, 16)
                    g.wait_ge(out_cnt, 16)
                    g.dma_start(before[0:1, 1:NT], cnt_tab[0:NT - 1].unsqueeze(0)).then_inc(in_cnt, 16)
                    g.dma_start(before[1:P, :], cnt_tab[NT - 1:NT - 1 + (P - 1) * NT]
                                .rearrange("(p t) -> p t", t=NT)).then_inc(in_cnt, 16)
                    g.wait_ge(out_src, 16)
                    g.wait_ge(in_attrw, 32)
                    g.wait_ge(out_zero, 16 * (1 + ACCS))

                @block.scalar
                def _(a):
                    a.wait_ge(cleared, N_CLEAR)
                    with nc.allow_non_contiguous_dma("lists and columns of parameters, once"):
                        for dest, flat in ((s_list, src), (d_list, dst), (w_list, edge_weight)):
                            a.dma_start(dest[:, :, 0, :], flat[0:HALF].rearrange("(w p k) -> p w k", p=P, k=K)
                                        ).then_inc(in_lists, 16)
                            a.dma_start(dest[:, 0:NW - 1, 1, :], flat[HALF:HALF + (NW - 1) * W]
                                        .rearrange("(w p k) -> p w k", p=P, k=K)).then_inc(in_lists, 16)
                            a.dma_start(dest[0:B_PARTS, NW - 1, 1, :], flat[HALF + (NW - 1) * W:E]
                                        .rearrange("(p k) -> p k", k=K)).then_inc(in_lists, 16)
                        a.dma_start(attrB[0:D, :], eencb.unsqueeze(1)).then_inc(in_par, 16)
                        a.dma_start(attrB[D:D2, :], eencb.unsqueeze(1)).then_inc(in_par, 16)
                    a.dma_start(h_cur[0:N // NT, :, :].rearrange("p t d -> p (t d)"),
                                x.rearrange("(p t) d -> p (t d)", t=NT)).then_inc(in_x, 16)
                    a.dma_start(encWs[:, :], encW).then_inc(in_enc, 16)
                    a.dma_start(encbs[:, :], encb.partition_broadcast(P)).then_inc(in_enc, 16)
                    a.dma_start(W1s[:, :, :], W1.rearrange("l k m -> k l m")).then_inc(in_par, 16)
                    a.dma_start(W2s[:, :, :], W2.rearrange("l k m -> k l m")).then_inc(in_par, 16)
                    for dest, v in ((b1s, b1), (lnGs, lnG), (lnBs, lnB), (b2s, b2)):
                        a.dma_start(dest.rearrange("p l d -> p (l d)"),
                                    v.rearrange("l d -> (l d)").partition_broadcast(P)).then_inc(in_par, 16)
                    for dest, v in ((nGs, normG), (nBs, normB)):
                        a.dma_start(dest[:, 0:L - 1, :].rearrange("p l d -> p (l d)"),
                                    v[1:L, :].rearrange("l d -> (l d)").partition_broadcast(P)).then_inc(in_par, 16)
                        a.dma_start(dest[:, L - 1, :], v[0, :].partition_broadcast(P)).then_inc(in_par, 16)
                    a.dma_start(ts[:, :], t.partition_broadcast(P)).then_inc(in_par, 16)
                    a.dma_start(linWs[:, :], linW).then_inc(in_par, 16)
                    a.dma_start(linbs[:, :], linb.partition_broadcast(P)).then_inc(in_par, 16)
                    layer_norm_scalar(a, xn[:, :, :], x_acc[:, :, :], stats, NT, ln0)
                    for k in range(NC_CHUNK):
                        for half in range(2):
                            a.wait_ge(xnT_ps, 2 * k + half + 1)
                            if k and not half:
                                a.wait_ge(enc_ps, k)
                            a.activation(xnT[:, half, :], ps[4 + half][0:D, :], ACT.Copy).then_inc(xnT_sb, 1)
                    def empty(i, b):
                        for gr in range(NG):
                            a.wait_ge(eaT_ps, NG * (2 * i + b) + gr + 1)
                            a.activation(eaT[b][:, gr * GC:(gr + 1) * GC], ps[1 + gr][:, :], ACT.Copy
                                         ).then_inc(eaT_sb, 1)

                    empty(0, 0)
                    empty(0, 1)
                    with a.Fori(1, NW // 2) as i:
                        for b in range(2):
                            a.wait_ge(ea_out[b], 16 * i)
                            empty(i, b)
                    a.wait_ge(in_lists, 16 * 9)
                    for win, lst in ((src_win, s_list), (dst_win, d_list), (wgt_win, w_list)):
                        a.dma_start(win.rearrange("w p x -> p w x"), lst.rearrange("p w h k -> p w (h k)")
                                    ).then_inc(out_lists, 16)
                    a.wait_ge(out_lists, 48)
                    a.wait_ge(in_par, 16 * 15)

                @block.tensor
                def _(pe):
                    pe.wait_ge(cleared, N_CLEAR)
                    pe.wait_ge(id_made, 1)
                    pe.wait_ge(in_tlast, 16)
                    for i in range(3):
                        cols = slice(i * TILES // 3, (i + 1) * TILES // 3)
                        pe.matmul(ps[1 + i][:, 0:TILES // 3], ones[0:1, :], tlast[:, cols],
                                  start=True, stop=True).then_inc(tlast_ps, 1)
                    pe.wait_ge(bcnt_ok, 1)
                    pe.matmul(ps[0][:, 0:1], ones[:, :], b_cnt[:, :], start=True, stop=True).then_inc(bcnt_ps, 1)
                    pe.wait_ge(xn_ok, 1)
                    pe.wait_ge(in_enc, 32)
                    for k in range(NC_CHUNK):
                        if k:
                            pe.wait_ge(xnT_sb, 2 * k)
                        for i in range(CT):
                            ins = pe.matmul(ps[4 + i // GT][0:D, i % GT * P:(i % GT + 1) * P], xn[:, k * CT + i, :],
                                            ident[:, :], start=True, stop=True)
                            if i % GT == GT - 1:
                                ins.then_inc(xnT_ps, 1)
                        pe.wait_ge(xnT_sb, 2 * k + 2)
                        if k:
                            pe.wait_ge(enc_sb, k)
                        for i in range(CT):
                            ins = pe.matmul(ps[6][:, i * D:(i + 1) * D], xnT[:, i // GT, i % GT * P:(i % GT + 1) * P],
                                            encWs[:, :], start=True, stop=True)
                        ins.then_inc(enc_ps, 1)
                    pe.wait_ge(tlast_sb, 3)

                    def window(i, b):
                        pe.wait_ge(ea_in[b], 32 * (i + 1))
                        for gr in range(NG):
                            if not (isinstance(i, int) and i == 0 and b == 0):
                                pe.wait_ge(eaT_sb, NG * (2 * i + b) + gr - NG + 1)
                            for j in range(GT):
                                for h in range(2):
                                    ins = pe.matmul(ps[1 + gr][h * D:(h + 1) * D, j * P:(j + 1) * P],
                                                    ea[b][:, h, gr * GT + j, :], ident[:, :], start=True, stop=True)
                            ins.then_inc(eaT_ps, 1)

                    window(0, 0)
                    window(0, 1)
                    with pe.Fori(1, NW // 2) as i:
                        window(i, 0)
                        window(i, 1)

                @block.vector
                def _(v):
                    for buf, value in ((ident[:, :], 0.0), (ones[:, :], 1.0), (attrW[:, :], 0.0),
                                       (dflat_i[:, :], 8191), (sflat_i[:, :], 0), (s_list[:, NW - 1, 1, :], 0),
                                       (d_list[:, NW - 1, 1, :], 0), (w_list[:, NW - 1, 1, :], 0.0),
                                       (h_cur[:, :, :], 0.0), (zero[:, :], 0.0)):
                        v.memset(buf, value).then_inc(cleared, 1)
                    link = Chain(v, set_step)
                    v.memset(padrow[:, :], 8191.0)
                    v.memset(dprev[:, :], -1.0)
                    v.memset(before[:, :], 0.0)
                    link(v.memset(pen_end[:, :], -BIG))
                    v.wait_ge(in_dst, 32)
                    v.wait_ge(cleared, N_CLEAR)
                    v.tensor_copy(dflat[:, :], dflat_i[:, :]).then_inc(dst_f, 1)
                    v.wait_ge(dst_f, 1)
                    v.wait_ge(in_bfirst, 16)
                    link(v.tensor_copy(b_first[:, :], b_first_i[:, :]))
                    v.tensor_scalar(junk[:, :], dflat[:, :], b_first[:, 0:1], None, ALU.is_le, ALU.add,
                                    accum_out=b_cnt[:, :]).then_inc(bcnt_ok, 1)
                    v.wait_ge(in_src, 32)
                    v.tensor_copy(sflat[:, :], sflat_i[:, :]).then_inc(src_f, 1)
                    v.wait_ge(in_prev, 32)
                    v.wait_ge(bcnt_ok, 1)
                    link(v.tensor_tensor(junk[:, :], dflat[:, :], dprev[:, :], ALU.is_equal))
                    v.tensor_scalar(pen[:, :], junk[:, :], -0.5, 2.0 * BIG, ALU.add, ALU.mult).then_inc(pen_f, 1)
                    v.wait_ge(pen_f, 1)

                    v.wait_ge(in_x, 16)
                    layer_norm(v, link, xn[:, :, :], h_cur[:, :, :], x_acc[:, :, :], stats, D, ln0)
                    v.tensor_scalar(xn[:, :, :], xn[:, :, :], 0.0, None, ALU.max).then_inc(xn_ok, 1)

                    for i in range(3):
                        v.wait_ge(tlast_ps, i + 1)
                        v.tensor_copy(tlast_b[:, i * TILES // 3:(i + 1) * TILES // 3], ps[1 + i][:, 0:TILES // 3]
                                      ).then_inc(tlast_sb, 1)
                    v.wait_ge(pool_made, 2)
                    v.tensor_copy(node[:, :], node_i[:, :])
                    link(v.tensor_copy(win_f[:, :], win_i[:, :]))
                    v.wait_ge(tlast_sb, 3)
                    for n in range(NT):
                        link(v.tensor_scalar(junk[:, :], tlast_b[:, :], node[:, n:n + 1], None, ALU.is_le, ALU.add,
                                             accum_out=cnt_t[:, n:n + 1]))
                        if n % CT == 0:
                            k = n // CT
                            v.wait_ge(enc_ps, k + 1)
                            v.tensor_tensor(h_cur[:, k * CT:(k + 1) * CT, :], ps[6].rearrange("p (t d) -> p t d", d=D),
                                            encbs.unsqueeze(1).broadcast_to([P, CT, D]), ALU.add).then_inc(enc_sb, 1)
                    v.wait_ge(enc_sb, NC_CHUNK)
                    v.tensor_copy(cnt_i[:, :], cnt_t[:, :]).then_inc(tiles_ok, 1)
                    v.memset(x_acc[:, :, :], 0.0)

                    v.wait_ge(bcnt_ps, 1)
                    v.tensor_scalar(b_last[:, 0:1], ps[0][:, 0:1], -1.0, None, ALU.add)
                    link(v.tensor_scalar(b_last[:, 1:2], ps[0][:, 0:1], -1.0 - W, None, ALU.add))
                    v.tensor_copy(patch_i[:, 0:1], b_last[:, 0:1])
                    v.tensor_scalar(win_le[:, :], win_f[:, :], b_last[:, 0:1], None, ALU.is_le)
                    link(v.tensor_scalar(win_hot[:, :], win_f[:, :], b_last[:, 1:2], None, ALU.is_gt))
                    link(v.tensor_tensor(win_hot[:, :], win_hot[:, :], win_le[:, :], ALU.mult))
                    v.wait_ge(in_cpen, 16)
                    link(v.tensor_copy(cpen[:, :], cpen_b[:, :]))

                    v.wait_ge(in_rows, 16 * NT)
                    for n in range(NT):
                        link(v.tensor_scalar(junk[:, 0:P], rows[:, n, :], node[:, n:n + 1], None, ALU.is_le, ALU.add,
                                             accum_out=cnt_r[:, n:n + 1]))
                    v.scalar_tensor_tensor(out=cnt_r[:, :], in0=cnt_t[:, :], scalar=float(P), in1=cnt_r[:, :],
                                           op0=ALU.mult, op1=ALU.add).then_inc(cnt_ok, 1)
                    v.wait_ge(cnt_ok, 1)
                    v.wait_ge(in_cnt, 32)
                    link(v.tensor_tensor(before[:, :], cnt_r[:, :], before[:, :], ALU.is_gt))
                    link(v.scalar_tensor_tensor(out=cnt_t[:, :], in0=cnt_r[:, :], scalar=-1.0 - ZROW, in1=before[:, :],
                                                op0=ALU.add, op1=ALU.mult))
                    link(v.tensor_scalar(cnt_t[:, :], cnt_t[:, :], float(ZROW), None, ALU.add))
                    link(v.tensor_copy(last_idx[:, :], cnt_t[:, :]))

        with ExitStack() as c:
            xg = [sb(f"xg{i}", [P, K, 2, D], F32, c) for i in range(2)]
            at = [sb(f"at{i}", [P, W], F32, c) for i in range(2)]
            idx = [sb(f"idx{i}", [P, 2, K], I32, c) for i in range(2)]
            rp = [sb(f"rp{i}", [P, W + 1], BF16, c) for i in range(2)]
            keep = [sb(f"keep{i}", [P, W], BF16, c) for i in range(2)]
            u = [sb(f"u{i}", [P, W], F32, c) for i in range(2)]
            lg = [sb(f"lg{i}", [P, W], F32, c) for i in range(2)]
            runmax = sb("runmax", [P, W], F32, c)
            segmax = sb("segmax", [P, W], F32, c)
            ex = sb("ex", [P, W + 1], F32, c)
            uex = sb("uex", [P, W], F32, c)
            den = [sb(f"den{i}", [P, W], F32, c) for i in range(2)]
            num = [sb(f"num{i}", [P, W], F32, c) for i in range(2)]
            st_all = sb("st_all", [P, 2, 2, K, D2], F32, c)
            st = [st_all[:, i, :, :, :] for i in range(2)]
            carry = sb("carry", [P, 4], F32, c)
            start2 = sb("start2", [P, 2], F32, c)
            wmax = sb("wmax", [P, NW], F32, c)
            wjunk = sb("wjunk", [P, NW], F32, c)
            tcur = sb("tcur", [P, 2], F32, c)
            W1c = sb("W1c", [D, D2], F32, c)
            W2c = sb("W2c", [D2, D], F32, c)
            prow = sb("prow", [1, 4, D2], F32, c)
            pdiff = sb("pdiff", [1, 2, D], F32, c)
            pmax = sb("pmax", [1, D], F32, c)
            pold = sb("pold", [1, 2, D], F32, c)
            pnew = sb("pnew", [1, 2, D], F32, c)
            ptmp = sb("ptmp", [1, 2, D], F32, c)
            dn = st_all.rearrange("p b h k c -> p (b h k) c")[:, 0:NT, :]
            hin = sb("hin", [P, CT, D], F32, c)
            ntmp = sb("ntmp", [P, CT, D], F32, c)
            hinT = sb("hinT", [D, CT * P], F32, c)
            y = sb("y", [P, CT, D2], F32, c)
            y2 = sb("y2", [P, CT, D2], F32, c)
            zT = sb("zT", [D2, CT * P], F32, c)

            at_in, xg_in, idx_in, rp_in, st_out = (
                [sem(f"{n}{i}") for i in range(2)] for n in ("at_in", "xg_in", "idx_in", "rp_in", "st_out"))
            z_ps, u_ok, l_ok, diff_ok, ex_ok, max_ok, sums_ok, back_ps, back_sb = (
                sem(n) for n in ("z_ps", "u_ok", "l_ok", "diff_ok", "ex_ok", "max_ok", "sums_ok", "back_ps", "back_sb"))
            dve_step, node_step, tcur_ok, gather_go = (
                sem(n) for n in ("dve_step", "node_step", "tcur_ok", "gather_go"))
            carry_ok, prow_ps, pold_in, pdiff_ok, pexp_ok, pnew_ok, patched = (
                sem(n) for n in ("carry_ok", "prow_ps", "pold_in", "pdiff_ok", "pexp_ok", "pnew_ok", "patched"))
            dn_in = [sem(f"dn_in{i}") for i in range(NC_CHUNK)]
            hin_ok, hinT_ps, hinT_sb, y_ps, z_ok, zr_ok, zT_ps, zT_sb, o_ps, hn_ok, h_ok, tab_out = (
                sem(n) for n in ("hin_ok", "hinT_ps", "hinT_sb", "y_ps", "z_ok", "zr_ok", "zT_ps", "zT_sb", "o_ps",
                                 "hn_ok", "h_ok", "tab_out"))
            lnY = tuple(sem(f"lnY_{n}") for n in ("centred", "squared", "rooted"))
            lnX = tuple(sem(f"lnX_{n}") for n in ("centred", "squared", "rooted"))
            BU = 2 * NG
            Z0, U0, L0, M0, S0, BP0, BS0 = 2 * NG, NG, 2, 2, 2, 2 * BU, 3
            PAIRS = NW // 2

            with nc.Block() as block:
                @block.sync
                def _(sp):
                    last = sp.value_load(patch_i[0:1, 0:1], min_val=HALF, max_val=EPAD - 1)

                    def load(g, w, b):
                        sp.wait_ge(z_ps, NG * g + NG - NG * 2 + Z0)
                        sp.dma_start(idx[b].rearrange("p h k -> p (h k)"), src_win[w]).then_inc(idx_in[b], 16)
                        sp.dma_start(at[b][:, :], attr_t[w]).then_inc(at_in[b], 16)
                        sp.wait_ge(max_ok, g + 1)
                        sp.wait_ge(l_ok, g + 1)
                        for h in range(2):
                            sp.dma_start(rp[b][h * D:(h + 1) * D, :], run_pen[bass.ds(h * HALF + w * W, W + 1)]
                                         .partition_broadcast(D)).then_inc(rp_in[b], 16)

                    sums_v = sums[0:EPAD, :].rearrange("(h w p k) c -> h w p (k c)", h=2, w=NW, p=P)

                    def store(g, w, b):
                        sp.wait_ge(back_sb, BU * (g + 1) + BS0)
                        for h in range(2):
                            sp.dma_start(sums_v[h, w], st[b][:, h, :, :].rearrange("p k c -> p (k c)")
                                         ).then_inc(st_out[b], 16)

                    def store_nodes(k):
                        sp.dma_start(h_tab.rearrange("(p t) d -> p t d", t=NT)[:, k * CT:(k + 1) * CT, :],
                                     h_cur[:, k * CT:(k + 1) * CT, :]).then_inc(tab_out, 16)

                    for k in range(NC_CHUNK):
                        store_nodes(k)
                    load(0, 0, 0)
                    load(1, 1, 1)
                    with sp.Fori(0, L) as l:
                        with sp.Fori(0, PAIRS - 1) as i:
                            for b in range(2):
                                load(l * NW + 2 * i + 2 + b, 2 * i + 2 + b, b)
                                store(l * NW + 2 * i + b, 2 * i + b, b)
                        for b in range(2):
                            store(l * NW + NW - 2 + b, NW - 2 + b, b)
                        for b in range(2):
                            sp.wait_ge(st_out[b], 32 * PAIRS * (l + 1) + 32)
                        sp.dma_start(pold.rearrange("p a d -> p (a d)"), sums[bass.ds(last, 1), :]).then_inc(pold_in, 16)
                        for b in range(2):
                            load((l + 1) * NW + b, b, b)
                        sp.wait_ge(pnew_ok, l + 1)
                        sp.dma_start(sums[bass.ds(last, 1), :], pnew.rearrange("p a d -> p (a d)")).then_inc(patched, 16)
                        for k in range(NC_CHUNK):
                            sp.wait_ge(h_ok, NC_CHUNK * l + k + 1)
                            store_nodes(k)
                    sp.wait_ge(tab_out, 16 * NC_CHUNK * (L + 1))
                    for b in range(2):
                        sp.wait_ge(idx_in[b], 16 * (PAIRS * L + 1))
                        sp.wait_ge(at_in[b], 16 * (PAIRS * L + 1))
                        sp.wait_ge(rp_in[b], 32 * (PAIRS * L + 1))

                @block.gpsimd
                def _(g_):
                    def window(g, i, l, b):
                        g_.wait_ge(z_ps, NG * g + NG - NG * 2 + Z0)
                        g_.sem_inc(gather_go, 1)
                        g_.wait_ge(idx_in[b], 16 * (l * PAIRS + i + 1))
                        g_.sem_inc(gather_go, 1)
                        for k in range(K):
                            for h in range(2):
                                g_.indirect_dma_start(xg[b][:, k, h, :], None, h_tab[:, :], bass.IndirectOffsetOnAxis(
                                    ap=idx[b][:, h, k:k + 1], axis=0)).then_inc(xg_in[b], 16)

                    with g_.Fori(0, L) as l:
                        g_.wait_ge(tab_out, 16 * NC_CHUNK * (l + 1))
                        g_.sem_inc(gather_go, 1)
                        with g_.Fori(0, PAIRS) as i:
                            for b in range(2):
                                window(l * NW + 2 * i + b, i, l, b)
                        g_.wait_ge(patched, 16 * (l + 1))
                        g_.sem_inc(gather_go, 1)
                        for t_ in range(NT):
                            g_.indirect_dma_start(dn[:, t_, :], None, sums[:, :], bass.IndirectOffsetOnAxis(
                                ap=last_idx[:, t_:t_ + 1], axis=0)).then_inc(dn_in[t_ // CT], 16)

                @block.tensor
                def _(pe):
                    pe.sem_inc(z_ps, Z0)
                    pe.sem_inc(back_ps, BP0)

                    def forward(g, i, l, b):
                        pe.wait_ge(at_in[b], 16 * (l * PAIRS + i + 1))
                        pe.wait_ge(xg_in[b], 32 * K * (l * PAIRS + i + 1))
                        for gr in range(NG):
                            pe.wait_ge(u_ok, NG * g + gr + 1 - NG + U0)
                            pe.matmul(ps[gr][:, :], attrW[:, :], at[b][:, gr * GC:(gr + 1) * GC], start=True, stop=True)
                            for j in range(GT):
                                ins = pe.matmul(ps[gr][:, j * P:(j + 1) * P],
                                                xg[b][:, gr * GT + j, :, :].rearrange("p h d -> p (h d)"), ident[:, :],
                                                start=False, stop=True, skip_group_check=True)
                            ins.then_inc(z_ps, 1)

                    def back(g, b):
                        pe.wait_ge(sums_ok, g + 1 + S0)
                        for r in range(BU):
                            gr, s_ = r // 2, r % 2
                            pe.wait_ge(back_sb, BU * g + r + 1 - 3 + BS0)
                            sum_v = (den, num)[s_][b].rearrange("c (p k) -> c k p", k=K)
                            for j in range(GT):
                                ins = pe.matmul(ps[3 + r % 3][:, j * P:(j + 1) * P], sum_v[:, gr * GT + j, :],
                                                ident[:, :], start=True, stop=True)
                            ins.then_inc(back_ps, 1)

                    with pe.Fori(0, L) as l:
                        g0 = l * NW
                        forward(g0, 0, l, 0)
                        with pe.Fori(0, PAIRS - 1) as i:
                            forward(g0 + 2 * i + 1, i, l, 1)
                            back(g0 + 2 * i, 0)
                            forward(g0 + 2 * i + 2, i + 1, l, 0)
                            back(g0 + 2 * i + 1, 1)
                        forward(g0 + NW - 1, PAIRS - 1, l, 1)
                        back(g0 + NW - 2, 0)
                        back(g0 + NW - 1, 1)

                        pe.wait_ge(carry_ok, l + 1)
                        pe.wait_ge(back_sb, BU * (g0 + NW) + BS0)
                        for j in range(4):
                            ins = pe.matmul(ps[3][0:1, j * P:(j + 1) * P], carry[:, j:j + 1], ident[:, :],
                                            start=True, stop=True)
                        ins.then_inc(prow_ps, 1)
                        for k in range(NC_CHUNK):
                            n = NC_CHUNK * l + k + 1
                            pe.wait_ge(hin_ok, n)
                            pe.wait_ge(u_ok, NG * (g0 + NW) + U0)
                            for j in range(CT):
                                ins = pe.matmul(ps[j // GT][0:D, j % GT * P:(j % GT + 1) * P], hin[:, j, :], ident[:, :],
                                                start=True, stop=True)
                            ins.then_inc(hinT_ps, 1)
                            pe.wait_ge(hinT_sb, n)
                            for j in range(CT):
                                ins = pe.matmul(ps[6 + j // GT][:, j % GT * P:(j % GT + 1) * P],
                                                hinT[:, j * P:(j + 1) * P], W1c[:, :], start=True, stop=True)
                            ins.then_inc(y_ps, 1)
                            pe.wait_ge(zr_ok, n)
                            for j in range(CT):
                                ins = pe.matmul(ps[j // GT][:, j % GT * P:(j % GT + 1) * P], y[:, j, :], ident[:, :],
                                                start=True, stop=True)
                            ins.then_inc(zT_ps, 1)
                            pe.wait_ge(zT_sb, n)
                            for j in range(CT):
                                ins = pe.matmul(ps[2][:, j * D:(j + 1) * D], zT[:, j * P:(j + 1) * P], W2c[:, :],
                                                start=True, stop=True)
                            ins.then_inc(o_ps, 1)

                @block.scalar
                def _(a):
                    a.sem_inc(u_ok, U0)
                    a.sem_inc(l_ok, L0)
                    a.sem_inc(back_sb, BS0)
                    for b in range(2):
                        a.sem_inc(st_out[b], 32)

                    def logits(g, i, l, b):
                        a.wait_ge(sums_ok, g + 1 - 2 + S0)
                        a.wait_ge(rp_in[b], 32 * (l * PAIRS + i + 1))
                        a.activation(keep[b][:, :], rp[b][:, 0:W], ACT.Relu, scale=1.0 / BIG)
                        for gr in range(NG):
                            a.wait_ge(z_ps, NG * g + gr + 1 + Z0)
                            a.activation(u[b].rearrange("c (p k) -> c k p", k=K)[:, gr * GT:(gr + 1) * GT, :],
                                         ps[gr].rearrange("c (k p) -> c k p", p=P), ACT.Relu, bias=attrB[:, 0:1]
                                         ).then_inc(u_ok, 1)
                        a.wait_ge(u_ok, NG * (g + 1) + U0)
                        a.activation(lg[b][:, :], u[b][:, :], ACT.Identity, bias=tcur[:, 1:2], scale=tcur[:, 0:1]
                                     ).then_inc(l_ok, 1)

                    def empty(g, i, l, b):
                        a.wait_ge(st_out[b], 32 * (l * PAIRS + i) + 32)
                        for r in range(BU):
                            gr, s_ = r // 2, r % 2
                            a.wait_ge(back_ps, BU * g + r + 1 + BP0)
                            a.activation(st[b].rearrange("p h k c -> p k h c")[:, gr * GT:(gr + 1) * GT, :,
                                                                               s_ * D:(s_ + 1) * D],
                                         ps[3 + r % 3].rearrange("p (k h c) -> p k h c", k=GT, h=2), ACT.Copy
                                         ).then_inc(back_sb, 1)

                    def exponentials(g):
                        a.wait_ge(diff_ok, g + 1)
                        a.activation(ex[:, :], ex[:, :], ACT.Exp, scale=-1.0).then_inc(ex_ok, 1)

                    with a.Fori(0, L) as l:
                        g0 = l * NW
                        a.wait_ge(tcur_ok, l + 1)
                        logits(g0, 0, l, 0)
                        exponentials(g0)
                        with a.Fori(0, PAIRS - 1) as i:
                            logits(g0 + 2 * i + 1, i, l, 1)
                            empty(g0 + 2 * i, i, l, 0)
                            exponentials(g0 + 2 * i + 1)
                            logits(g0 + 2 * i + 2, i + 1, l, 0)
                            empty(g0 + 2 * i + 1, i, l, 1)
                            exponentials(g0 + 2 * i + 2)
                        logits(g0 + NW - 1, PAIRS - 1, l, 1)
                        empty(g0 + NW - 2, PAIRS - 1, l, 0)
                        exponentials(g0 + NW - 1)
                        empty(g0 + NW - 1, PAIRS - 1, l, 1)

                        a.wait_ge(pdiff_ok, l + 1)
                        a.activation(pdiff[:, :, :], pdiff[:, :, :], ACT.Exp, scale=-1.0).then_inc(pexp_ok, 1)
                        for k in range(NC_CHUNK):
                            n = NC_CHUNK * l + k + 1
                            a.wait_ge(hinT_ps, n)
                            for half in range(2):
                                ins = a.activation(hinT[:, half * 512:(half + 1) * 512], ps[half][0:D, :], ACT.Copy)
                            ins.then_inc(hinT_sb, 1)
                            layer_norm_scalar(a, y[:, :, :], y2[:, :, :], stats, CT, lnY + (n,))
                            a.wait_ge(z_ok, n)
                            a.activation(y[:, :, :], y[:, :, :], ACT.Relu).then_inc(zr_ok, 1)
                            a.wait_ge(zT_ps, n)
                            for half in range(2):
                                ins = a.activation(zT[:, half * 512:(half + 1) * 512], ps[half][:, :], ACT.Copy)
                            ins.then_inc(zT_sb, 1)
                            layer_norm_scalar(a, hin[:, :, :], ntmp[:, :, :], stats, CT, lnX + (n,))
                            a.wait_ge(hn_ok, n)
                            a.activation(h_cur[:, k * CT:(k + 1) * CT, :], hin[:, :, :], ACT.Relu).then_inc(h_ok, 1)

                @block.vector
                def _(v):
                    v.sem_inc(max_ok, M0)
                    v.sem_inc(sums_ok, S0)
                    STEPS = 6

                    def window(g, w, i, l, b):
                        link = Chain(v, dve_step, g * STEPS)
                        v.wait_ge(l_ok, g + 1 + L0)
                        link(v.tensor_tensor_scan(runmax[:, :], rp[b][:, 0:W], lg[b][:, :], carry[:, 0:1],
                                                  ALU.min, ALU.max))
                        v.tensor_tensor_scan(segmax[:, ::-1], rp[b][:, 1:W + 1][:, ::-1], runmax[:, ::-1], -BIG,
                                             ALU.min, ALU.max).then_inc(max_ok, 1)
                        v.wait_ge(max_ok, g + 1 + M0)
                        v.tensor_scalar(ex[:, 0:1], segmax[:, 0:1], carry[:, 0:1], 0.0, ALU.subtract, ALU.max)
                        v.tensor_copy(wmax[:, bass.ds(w, 1)], segmax[:, 0:1])
                        v.tensor_tensor(ex[:, 1:W + 1], segmax[:, :], lg[b][:, :], ALU.subtract).then_inc(diff_ok, 1)
                        v.wait_ge(diff_ok, g + 1)
                        link(v.tensor_copy(carry[:, 0:1], runmax[:, W - 1:W]))
                        v.wait_ge(ex_ok, g + 1)
                        v.tensor_scalar(start2[:, :], carry[:, 1:3], ex[:, 0:1], None, ALU.mult)
                        link(v.tensor_tensor(uex[:, :], u[b][:, :], ex[:, 1:W + 1], ALU.mult))
                        v.wait_ge(back_ps, BU * (g - 1) + BP0)
                        link(v.tensor_tensor_scan(den[b][:, :], keep[b][:, :], ex[:, 1:W + 1], start2[:, 0:1],
                                                  ALU.mult, ALU.add))
                        v.tensor_tensor_scan(num[b][:, :], keep[b][:, :], uex[:, :], start2[:, 1:2],
                                             ALU.mult, ALU.add).then_inc(sums_ok, 1)
                        v.wait_ge(sums_ok, g + 1 + S0)
                        link(v.tensor_copy(carry[:, 1:2], den[b][:, W - 1:W]))
                        link(v.tensor_copy(carry[:, 2:3], num[b][:, W - 1:W]))

                    PER_LAYER = 5 + NC_CHUNK * 18
                    with v.Fori(0, L) as l:
                        link = Chain(v, node_step, l * PER_LAYER)
                        v.memset(carry[:, 0:1], -BIG)
                        v.memset(carry[:, 1:4], 0.0)
                        v.tensor_copy(W1c[:, :], W1s[:, bass.ds(l, 1), :].rearrange("k l m -> k (l m)"))
                        v.tensor_copy(W2c[:, :], W2s[:, bass.ds(l, 1), :].rearrange("k l m -> k (l m)"))
                        link(v.tensor_copy(tcur[:, 0:1], ts[:, bass.ds(l, 1)]))
                        v.tensor_scalar(tcur[:, 1:2], tcur[:, 0:1], EPS, None, ALU.mult).then_inc(tcur_ok, 1)
                        with v.Fori(0, PAIRS) as i:
                            for b in range(2):
                                window(l * NW + 2 * i + b, 2 * i + b, i, l, b)

                        v.wait_ge(dve_step, (l + 1) * NW * STEPS)
                        v.tensor_tensor_reduce(wjunk[:, :], wmax[:, :], win_hot[:, :], 1.0, 0.0, ALU.mult, ALU.add,
                                               carry[:, 3:4]).then_inc(carry_ok, 1)
                        v.wait_ge(prow_ps, l + 1)
                        link(v.tensor_copy(prow.rearrange("p a d -> p (a d)"), ps[3][0:1, :]))
                        link(v.tensor_scalar(prow[:, 0, 0:D], prow[:, 0, 0:D], cpen[:, 0:1], None, ALU.min))
                        link(v.tensor_tensor(pmax[:, :], prow[:, 0, 0:D], prow[:, 3, D:D2], ALU.max))
                        v.tensor_tensor(pdiff[:, 0, :], pmax[:, :], prow[:, 0, 0:D], ALU.subtract)
                        v.tensor_tensor(pdiff[:, 1, :], pmax[:, :], prow[:, 3, D:D2], ALU.subtract).then_inc(pdiff_ok, 1)
                        v.wait_ge(pexp_ok, l + 1)
                        v.wait_ge(pold_in, 16 * (l + 1))
                        both = [1, 2, D]
                        v.tensor_tensor(ptmp[:, :, :], prow[:, 1:3, 0:D], pdiff[:, 0:1, :].broadcast_to(both), ALU.mult)
                        link(v.tensor_tensor(pnew[:, :, :], pold[:, :, :], pdiff[:, 1:2, :].broadcast_to(both), ALU.mult))
                        v.tensor_tensor(pnew[:, :, :], pnew[:, :, :], ptmp[:, :, :], ALU.add).then_inc(pnew_ok, 1)

                        def per_node(vec, width):
                            return vec.unsqueeze(1).broadcast_to([P, CT, width])

                        for k in range(NC_CHUNK):
                            n = NC_CHUNK * l + k + 1
                            cs = slice(k * CT, (k + 1) * CT)
                            v.wait_ge(dn_in[k], 16 * CT * (l + 1))
                            if k:
                                v.wait_ge(h_ok, n - 1)
                            v.scalar_tensor_tensor(out=hin[:, :, :], in0=dn[:, cs, 0:D], scalar=EPS, in1=dn[:, cs, D:D2],
                                                   op0=ALU.mult, op1=ALU.add)
                            link(v.tensor_scalar(ntmp[:, :, :], dn[:, cs, 0:D], 1e-30, None, ALU.max))
                            link(v.reciprocal(ntmp[:, :, :], ntmp[:, :, :]))
                            link(v.tensor_tensor(hin[:, :, :], hin[:, :, :], ntmp[:, :, :], ALU.mult))
                            v.tensor_tensor(hin[:, :, :], hin[:, :, :], h_cur[:, cs, :], ALU.add).then_inc(hin_ok, 1)
                            v.wait_ge(y_ps, n)
                            for half in range(2):
                                ins = v.tensor_tensor(y2[:, half * GT:(half + 1) * GT, :],
                                                      ps[6 + half].rearrange("p (t d) -> p t d", d=D2),
                                                      b1s[:, bass.ds(l, 1), :].broadcast_to([P, GT, D2]), ALU.add)
                            link(ins)
                            layer_norm(v, link, y[:, :, :], y2[:, :, :], y2[:, :, :], stats, D2, lnY + (n,))
                            link(v.tensor_tensor(y[:, :, :], y[:, :, :], lnGs[:, bass.ds(l, 1), :].broadcast_to([P, CT, D2]), ALU.mult))
                            v.tensor_tensor(y[:, :, :], y[:, :, :], lnBs[:, bass.ds(l, 1), :].broadcast_to([P, CT, D2]), ALU.add
                                            ).then_inc(z_ok, 1)
                            v.wait_ge(o_ps, n)
                            link(v.tensor_tensor(hin[:, :, :], ps[2].rearrange("p (t d) -> p t d", d=D),
                                                 b2s[:, bass.ds(l, 1), :].broadcast_to([P, CT, D]), ALU.add))
                            link(v.tensor_tensor(x_acc[:, cs, :], x_acc[:, cs, :], hin[:, :, :], ALU.add))
                            layer_norm(v, link, hin[:, :, :], x_acc[:, cs, :], ntmp[:, :, :], stats, D, lnX + (n,))
                            link(v.tensor_tensor(hin[:, :, :], hin[:, :, :], nGs[:, bass.ds(l, 1), :].broadcast_to([P, CT, D]), ALU.mult))
                            v.tensor_tensor(hin[:, :, :], hin[:, :, :], nBs[:, bass.ds(l, 1), :].broadcast_to([P, CT, D]), ALU.add
                                            ).then_inc(hn_ok, 1)
                        assert link.n == PER_LAYER, link.n

        with ExitStack() as c:
            TW = 2 * K
            TB = 8
            NB = TW // TB
            gh = [sb(f"gh{i}", [P, TW, D], F32, c) for i in range(2)]
            vm = [sb(f"vm{i}", [P, TW, D], F32, c) for i in range(2)]
            srcB = [sb(f"srcB{i}", [P, 2, W], F32, c) for i in range(2)]
            di = [sb(f"di{i}", [P, TW], I32, c) for i in range(2)]
            si = [sb(f"si{i}", [P, TW], I32, c) for i in range(2)]
            wl = [sb(f"wl{i}", [P, TW], F32, c) for i in range(2)]
            sf = sb("sf", [P, TW], F32, c)
            dup = sb("dup", [P, TW], F32, c)
            move = sb("move", [P, TW], F32, c)
            tgt = [sb(f"tgt{i}", [P, TW], I32, c) for i in range(2)]
            eqw = sb("eqw", [P, 2, TB, P], F32, c)
            tri = sb("tri", [P, P], F32, c)
            djunk = sb("djunk", [P, P], F32, c)
            trash_i = sb("trash_i", [P, 1], I32, c)
            trash = sb("trash", [P, 1], F32, c)
            hT = sb("hT", [D, CT * P], F32, c)
            xin = sb("xin", [P, NT, D], F32, c)
            xtmp = sb("xtmp", [P, NT, D], F32, c)
            tabs = [sb(f"tabs{i}", [P, NT, D], F32, c) for i in range(2)]

            fx_in, fclr, ftri, ftrash, fT_ps, fT_sb, fo_ps, fo_ok, f_step, fh_ok, h2_out = (
                sem(f"f_{n}") for n in ("xin", "clr", "tri", "trash", "Tps", "Tsb", "ops", "ook", "step", "hok", "h2out"))
            ln2 = tuple(sem(f"ln2_{n}") for n in ("centred", "squared", "rooted")) + (1,)
            di_in, ls_in, g_in = ([sem(f"{n}{i}") for i in range(2)] for n in ("di_in", "ls_in", "g_in"))
            set_done = [sem("set_done0"), sem("set_done1")]
            eq_ok, merged_ps, v_sb, tgt_ok, m_step, scat_go, landed = (
                sem(n) for n in ("eq_ok", "merged_ps", "v_sb", "tgt_ok", "m_step", "scat_go", "landed"))
            tab_in, tab_sum, out_ok = [sem("tab_in0"), sem("tab_in1")], sem("tab_sum"), sem("out_ok")
            M0_, V0, T0 = 2 * NB, 2, 2
            SETB = TW // BATCH // 2
            PAIRS = NW // 2

            with nc.Block() as block:
                @block.sync
                def _(sp):
                    def load(w, b):
                        sp.wait_ge(merged_ps, NB * w - NB + M0_)
                        sp.dma_start(di[b][:, :], dst_win[w]).then_inc(di_in[b], 16)
                        sp.wait_ge(tgt_ok, w + 1)
                        sp.dma_start(si[b][:, :], src_win[w]).then_inc(ls_in[b], 16)
                        sp.dma_start(wl[b][:, :], wgt_win[w]).then_inc(ls_in[b], 16)
                        for h in range(2):
                            sp.dma_start(srcB[b][:, h, :], src_flat[bass.ds(h * HALF + w * W, W)]
                                         .partition_broadcast(P)).then_inc(ls_in[b], 16)

                    sp.wait_ge(fclr, 1)
                    sp.dma_start(xin[0:N // NT, :, :].rearrange("p t d -> p (t d)"),
                                 x.rearrange("(p t) d -> p (t d)", t=NT)).then_inc(fx_in, 16)
                    load(0, 0)
                    load(1, 1)
                    sp.wait_ge(fh_ok, 1)
                    sp.dma_start(h_tab.rearrange("(p t) d -> p (t d)", t=NT),
                                 h_cur.rearrange("p t d -> p (t d)")).then_inc(h2_out, 16)
                    with sp.Fori(1, PAIRS) as i:
                        load(2 * i, 0)
                        load(2 * i + 1, 1)
                    for s_ in range(2):
                        sp.wait_ge(set_done[s_], 16 * BATCH * SETB * NW)
                    for i, a in enumerate(acc):
                        if i >= 2:
                            sp.wait_ge(tab_sum, i - 1)
                        sp.dma_start(tabs[i % 2].rearrange("p t d -> p (t d)"),
                                     a[0:NPAD, :].rearrange("(p t) d -> p (t d)", t=NT)).then_inc(tab_in[i % 2], 16)
                    sp.wait_ge(tab_sum, ACCS)
                    sp.dma_start(out.rearrange("(p t) d -> p (t d)", t=NT),
                                 xin[0:N // NT, :, :].rearrange("p t d -> p (t d)")).then_inc(out_ok, 16)
                    sp.wait_ge(out_ok, 16)

                @block.gpsimd
                def _(g_):
                    g_.sem_inc(landed, 1)
                    g_.iota(trash_i[:, :], [[1, 1]], TRASH, 1).then_inc(ftrash, 1)
                    g_.wait_ge(fclr, 2)
                    g_.affine_select(out=tri[:, :], in_=tri[:, :], compare_op=ALU.is_gt, fill=0.0, base=0,
                                     pattern=[[-1, P]], channel_multiplier=1).then_inc(ftri, 1)

                    def gather(w, i, b):
                        g_.wait_ge(merged_ps, NB * w - NB + M0_)
                        g_.sem_inc(scat_go, 1)
                        g_.wait_ge(di_in[b], 16 * (i + 1))
                        g_.sem_inc(scat_go, 1)
                        for t_ in range(TW):
                            g_.indirect_dma_start(gh[b][:, t_, :], None, h_tab[:, :], bass.IndirectOffsetOnAxis(
                                ap=di[b][:, t_:t_ + 1], axis=0)).then_inc(g_in[b], 16)

                    def scatter(w, b, first=False):
                        g_.wait_ge(v_sb, NB * (w + 1) + V0)
                        g_.sem_inc(scat_go, 1)
                        g_.wait_ge(tgt_ok, w + 1 + T0)
                        g_.sem_inc(scat_go, 1)
                        for m in range(TW // BATCH):
                            if not first or m >= 2:
                                g_.wait_ge(set_done[m % 2], 16 * BATCH * (SETB * w + m // 2))
                            g_.sem_inc(landed if m == 1 else scat_go, 1)
                            for q in range(BATCH):
                                t_ = m * BATCH + q
                                g_.indirect_dma_start(acc[BATCH * (m % 2) + q][:, :], bass.IndirectOffsetOnAxis(
                                    ap=tgt[b][:, t_:t_ + 1], axis=0), vm[b][:, t_, :], None,
                                    compute_op=ALU.add).then_inc(set_done[m % 2], 16)

                    g_.wait_ge(h2_out, 16)
                    gather(0, 0, 0)
                    gather(1, 0, 1)
                    scatter(0, 0, first=True)
                    with g_.Fori(1, PAIRS) as i:
                        gather(2 * i, i, 0)
                        scatter(2 * i - 1, 1)
                        gather(2 * i + 1, i, 1)
                        scatter(2 * i, 0)
                    scatter(NW - 1, 1)

                @block.tensor
                def _(pe):
                    pe.sem_inc(merged_ps, M0_)
                    for k in range(NC_CHUNK):
                        if k:
                            pe.wait_ge(fT_sb, k)
                        for j in range(CT):
                            ins = pe.matmul(ps[j // GT][0:D, j % GT * P:(j % GT + 1) * P], h_cur[:, k * CT + j, :],
                                            ident[:, :], start=True, stop=True)
                        ins.then_inc(fT_ps, 1)
                        pe.wait_ge(fT_sb, k + 1)
                        if k:
                            pe.wait_ge(fo_ok, k)
                        for j in range(CT):
                            ins = pe.matmul(ps[2][:, j * D:(j + 1) * D], hT[:, j * P:(j + 1) * P], linWs[:, :],
                                            start=True, stop=True)
                        ins.then_inc(fo_ps, 1)

                    with pe.Fori(0, PAIRS) as i:
                        for b in range(2):
                            w = 2 * i + b
                            pe.wait_ge(g_in[b], 16 * TW * (i + 1))
                            for q in range(NB):
                                slot = (NB * b + q) % 2
                                pe.wait_ge(eq_ok, NB * w + q + 1)
                                pe.wait_ge(v_sb, NB * w + q + 1 - 2 + V0)
                                for j in range(TB):
                                    ins = pe.matmul(ps[4 + slot][:, j * D:(j + 1) * D], eqw[:, slot, j, :],
                                                    gh[b][:, q * TB + j, :], start=True, stop=True)
                                ins.then_inc(merged_ps, 1)

                @block.scalar
                def _(a):
                    a.sem_inc(v_sb, V0)
                    for k in range(NC_CHUNK):
                        a.wait_ge(fT_ps, k + 1)
                        if k:
                            a.wait_ge(fo_ps, k)
                        for half in range(2):
                            ins = a.activation(hT[:, half * 512:(half + 1) * 512], ps[half][0:D, :], ACT.Copy)
                        ins.then_inc(fT_sb, 1)
                    layer_norm_scalar(a, h_cur[:, :, :], xtmp[:, :, :], stats, NT, ln2)
                    with a.Fori(0, PAIRS) as i:
                        for b in range(2):
                            w = 2 * i + b
                            a.wait_ge(landed, w + 1)
                            for q in range(NB):
                                a.wait_ge(merged_ps, NB * w + q + 1 + M0_)
                                a.activation(vm[b].rearrange("p t d -> p (t d)")[:, q * 512:(q + 1) * 512],
                                             ps[4 + (NB * b + q) % 2][:, :], ACT.Copy).then_inc(v_sb, 1)

                @block.vector
                def _(v):
                    v.sem_inc(tgt_ok, T0)
                    v.memset(xin[:, :, :], 0.0).then_inc(fclr, 1)
                    v.memset(tri[:, :], 1.0).then_inc(fclr, 1)
                    link = Chain(v, f_step)
                    v.wait_ge(ftrash, 1)
                    link(v.tensor_copy(trash[:, :], trash_i[:, :]))
                    v.wait_ge(fx_in, 16)
                    for k in range(NC_CHUNK):
                        cs = slice(k * CT, (k + 1) * CT)
                        v.wait_ge(fo_ps, k + 1)
                        v.tensor_tensor(xtmp[:, cs, :], ps[2].rearrange("p (t d) -> p t d", d=D),
                                        linbs.unsqueeze(1).broadcast_to([P, CT, D]), ALU.add).then_inc(fo_ok, 1)
                    v.wait_ge(fo_ok, NC_CHUNK)
                    link(v.tensor_tensor(xin[:, :, :], xin[:, :, :], xtmp[:, :, :], ALU.add))
                    layer_norm(v, link, h_cur[:, :, :], xin[:, :, :], xtmp[:, :, :], stats, D, ln2)
                    v.tensor_scalar(h_cur[:, :, :], h_cur[:, :, :], 0.0, None, ALU.max).then_inc(fh_ok, 1)
                    v.wait_ge(ftri, 1)
                    MS = TW + 5

                    with v.Fori(0, PAIRS) as i:
                        for b in range(2):
                            w = 2 * i + b
                            link = Chain(v, m_step, w * MS)
                            v.wait_ge(ls_in[b], 64 * (i + 1))
                            link(v.tensor_copy(sf[:, :], si[b][:, :]))
                            for t_ in range(TW):
                                slot, q = (NB * b + t_ // TB) % 2, t_ // TB
                                if t_ % TB == 0:
                                    v.wait_ge(merged_ps, NB * w + q + 1 - 2 + M0_)
                                row = srcB[b][:, t_ // K, :].rearrange("p (e k) -> p k e", k=K)[:, t_ % K, :]
                                ins = v.tensor_scalar(eqw[:, slot, t_ % TB, :], row, sf[:, t_:t_ + 1],
                                                      wl[b][:, t_:t_ + 1], ALU.is_equal, ALU.mult)
                                if t_ % TB == TB - 1:
                                    ins.then_inc(eq_ok, 1)
                                link(v.scalar_tensor_tensor(out=djunk[:, :], in0=row, scalar=sf[:, t_:t_ + 1], in1=tri[:, :],
                                                            op0=ALU.is_equal, op1=ALU.mult, accum_out=dup[:, t_:t_ + 1]))
                            v.wait_ge(landed, w + 1)
                            link(v.tensor_scalar(dup[:, :], dup[:, :], 1.0, None, ALU.min))
                            link(v.tensor_scalar(move[:, :], sf[:, :], -1.0, trash[:, 0:1], ALU.mult, ALU.add))
                            link(v.tensor_tensor(move[:, :], move[:, :], dup[:, :], ALU.mult))
                            link(v.tensor_tensor(move[:, :], move[:, :], sf[:, :], ALU.add))
                            v.tensor_copy(tgt[b][:, :], move[:, :]).then_inc(tgt_ok, 1)
                    for i in range(ACCS):
                        v.wait_ge(tab_in[i % 2], 16 * (i // 2 + 1))
                        v.tensor_tensor(xin[:, :, :], xin[:, :, :], tabs[i % 2][:, :, :], ALU.add).then_inc(tab_sum, 1)
                        v.wait_ge(tab_sum, i + 1)


_INS = ['x', 'src', 'dst', 'edge_attr_64', 'edge_weight', 'L0_gnn_encW', 'L0_gnn_encb', 'L0_gnn_eencW', 'L0_gnn_eencb',
        'L0_gnn_convW1', 'L0_gnn_convb1', 'L0_gnn_convLnG', 'L0_gnn_convLnB', 'L0_gnn_convW2', 'L0_gnn_convb2', 'L0_gnn_t',
        'L0_gnn_normG', 'L0_gnn_normB', 'L0_gnn_linW', 'L0_gnn_linb']
_OUTS = [((N, D), 'float32')]


def kernel(**inputs):
    import numpy as _np
    import concourse.bacc as _bacc
    from concourse import mybir as _mybir
    from concourse.bass_utils import run_bass_kernel_spmd as _run

    nc = _bacc.Bacc("TRN2", target_bir_lowering=False, num_devices=1)
    arrays, args = {}, []
    for name in _INS:
        a = _np.ascontiguousarray(inputs[name])
        arrays[f"in_{name}_dram"] = a
        args.append(nc.dram_tensor(f"in_{name}_dram", a.shape, _mybir.dt.from_np(a.dtype), kind="ExternalInput").ap())
    for i, (shape, dtype) in enumerate(_OUTS):
        dt = _mybir.dt.from_np(_np.dtype(dtype))
        args.append(nc.dram_tensor(f"out_{i}_dram", shape, dt, kind="ExternalOutput").ap())
    gnn(nc, *args)
    r = _run(nc, [arrays], core_ids=[0])
    got = tuple(r.results[0][f"out_{i}_dram"] for i in range(len(_OUTS)))
    return got[0]
```

```python
from contextlib import ExitStack

import concourse.bass as bass
from concourse import mybir

F32 = mybir.dt.float32
BF16 = mybir.dt.bfloat16
I32 = mybir.dt.int32
ALU = mybir.AluOpType
ACT = mybir.ActivationFunctionType
AX_X = mybir.AxisListType.X

P = 128
N, D, E, L = 5000, 64, 165000, 4
D2 = 2 * D
NT = N // 125
NPAD = P * NT
K = 12
W = P * K
NW = 54
HALF = NW * W
EPAD = 2 * HALF
GT = 4
NG = K // GT
GC = GT * P
B_REAL = E - HALF - (NW - 1) * W
B_PARTS = B_REAL // K
FLAT = EPAD // P
FLAT_REAL = E - (P - 1) * FLAT
TILES = EPAD // P
BIG = float(2.0 ** 126)
EPS = 1e-7
LN_EPS = 1e-5
NC_CHUNK = 5
CT = NT // NC_CHUNK
ACCS = 8
BATCH = ACCS // 2
ZCOLS = EPAD * D // (P * NW * L)
TRASH = NPAD
assert B_PARTS * K == B_REAL and NPAD == 5120 and FLAT * P == EPAD and ZCOLS * P * NW * L == EPAD * D


class Chain:

    def __init__(self, eng, sem, base=0):
        self.eng, self.sem, self.base, self.n = eng, sem, base, 0

    def __call__(self, ins):
        self.n += 1
        ins.then_inc(self.sem, 1)
        self.eng.wait_ge(self.sem, self.base + self.n)


def layer_norm(v, link, out, x, tmp, stats, width, act_signals):
    n = x.shape[1]
    mean, var, inv = stats[:, 0, 0:n], stats[:, 1, 0:n], stats[:, 2, 0:n]
    centred, squared, rooted, count = act_signals
    link(v.tensor_reduce(mean, x, AX_X, ALU.add))
    link(v.tensor_scalar(mean, mean, 1.0 / width, None, ALU.mult))
    v.tensor_tensor(out, x, mean.unsqueeze(2).broadcast_to([P, n, width]), ALU.subtract).then_inc(centred, 1)
    v.wait_ge(squared, count)
    link(v.tensor_reduce(var, tmp, AX_X, ALU.add))
    v.tensor_scalar(var, var, 1.0 / width, LN_EPS, ALU.mult, ALU.add).then_inc(centred, 1)
    v.wait_ge(rooted, count)
    link(v.reciprocal(inv, var))
    link(v.tensor_tensor(out, out, inv.unsqueeze(2).broadcast_to([P, n, width]), ALU.mult))


def layer_norm_scalar(a, out, tmp, stats, n, act_signals):
    centred, squared, rooted, count = act_signals
    a.wait_ge(centred, 2 * count - 1)
    a.activation(tmp, out, ACT.Square).then_inc(squared, 1)
    a.wait_ge(centred, 2 * count)
    a.activation(stats[:, 1, 0:n], stats[:, 1, 0:n], ACT.Sqrt).then_inc(rooted, 1)


def gnn(nc, x, src, dst, edge_attr, edge_weight, encW, encb, eencW, eencb, W1, b1, lnG, lnB, W2, b2,
        t, normG, normB, linW, linb, out):
    def dram(name, shape, dt=F32):
        return nc.dram_tensor(name, shape, dt).ap()

    src_flat = dram("src_flat", [EPAD])
    wgt_flat = dram("wgt_flat", [EPAD])
    dst_tab = dram("dst_tab", [TILES + 1, P])
    run_pen = dram("run_pen", [EPAD + 16], BF16)
    cnt_tab = dram("cnt_tab", [NPAD])
    h_tab = dram("h_tab", [NPAD, D])
    sums = dram("sums", [EPAD + P, D2])
    run_head = dram("run_head", [EPAD + NPAD, D])
    acc = [dram(f"acc{i}", [NPAD + P, D]) for i in range(ACCS)]
    ZROW = EPAD

    with ExitStack() as whole:
        def sb(name, shape, dt=F32, ctx=whole):
            return ctx.enter_context(nc.sbuf_tensor(name, shape, dt))[tuple([slice(None)] * len(shape))]

        def sem(name):
            return whole.enter_context(nc.semaphore(name))

        ident = sb("ident", [P, P])
        ones = sb("ones", [P, P])
        attrW = sb("attrW", [P, P])
        attrB = sb("attrB", [P, 1])
        last_idx = sb("last_idx", [P, NT], I32)
        first_idx = sb("first_idx", [P, NT], I32)
        win_hot = sb("win_hot", [P, NW])
        patch_i = sb("patch_i", [P, 2], I32)
        cpen = sb("cpen", [1, 1])
        x_acc = sb("x_acc", [P, NT, D])
        h_cur = sb("h_cur", [P, NT, D])
        W1s = sb("W1s", [D + 1, L, D2])
        W2s = sb("W2s", [D2, L, D])
        lnGs = sb("lnGs", [D2, L])
        lnBs = sb("lnBs", [D2, L])
        ln_eps = sb("ln_eps", [P, 1])
        b2s = sb("b2s", [P, L, D])
        nGs = sb("nGs", [P, L, D])
        nBs = sb("nBs", [P, L, D])
        ts = sb("ts", [P, L])
        linWs = sb("linWs", [D, D])
        linbs = sb("linbs", [P, D])
        stats = sb("stats", [P, 3, NT])
        zeros = sb("zeros", [P, ZCOLS])

        ps = [whole.enter_context(nc.psum_tensor(f"ps{i}", [P, 512], F32))[:, :] for i in range(8)]

        with ExitStack() as c:
            wflat = sb("wflat", [P, FLAT], F32, c)
            dflat_i = sb("dflat_i", [P, FLAT], I32, c)
            sflat_i = sb("sflat_i", [P, FLAT], I32, c)
            dflat = sb("dflat", [P, FLAT], F32, c)
            sflat = sb("sflat", [P, FLAT], F32, c)
            dprev = sb("dprev", [P, FLAT], F32, c)
            pen = sb("pen", [P, FLAT], BF16, c)
            padrow = sb("padrow", [1, P], F32, c)
            tlast = sb("tlast", [1, TILES], F32, c)
            tlast_b = sb("tlast_b", [P, TILES], F32, c)
            junk = sb("junk", [P, TILES], F32, c)
            signs = sb("signs", [P, TILES], BF16, c)
            node_h = sb("node_h", [P, NT], F32, c)
            node_i = sb("node_i", [P, NT], I32, c)
            node = sb("node", [P, NT], F32, c)
            cnt_t = sb("cnt_t", [P, NT], F32, c)
            cnt_i = sb("cnt_i", [P, NT], I32, c)
            cnt_r = sb("cnt_r", [P, NT], F32, c)
            before = sb("before", [P, NT], F32, c)
            has = sb("has", [P, NT], F32, c)
            rows = sb("rows", [P, NT, P], F32, c)
            b_first_i = sb("b_first_i", [P, 1], I32, c)
            b_first = sb("b_first", [P, 1], F32, c)
            b_cnt = sb("b_cnt", [P, 1], F32, c)
            b_last = sb("b_last", [P, 2], F32, c)
            win_i = sb("win_i", [P, NW], I32, c)
            win_f = sb("win_f", [P, NW], F32, c)
            win_le = sb("win_le", [P, NW], F32, c)
            pen_end = sb("pen_end", [1, 16], BF16, c)
            cpen_b = sb("cpen_b", [1, 1], BF16, c)
            wmean = sb("wmean", [P, 3, L], F32, c)
            zero = sb("zero", [P, (NT + 1) * D], F32, c)
            encWs = sb("encWs", [D, D], F32, c)
            encbs = sb("encbs", [P, D], F32, c)
            xn = sb("xn", [P, NT, D], F32, c)
            xnT = sb("xnT", [D, 2, 512], F32, c)

            cleared, pool_made, id_made = sem("cleared"), sem("pool_made"), sem("id_made")
            in_dst, in_src, in_wgt, in_par, in_x, in_enc, in_bfirst = (
                sem(f"in_{n}") for n in ("dst", "src", "wgt", "par", "x", "enc", "bfirst"))
            in_prev, in_tlast, in_rows, in_cnt, in_cpen = (
                sem(f"in_{n}") for n in ("prev", "tlast", "rows", "cnt", "cpen"))
            out_wgt, out_dst, out_pen, out_src, out_zero, out_cnt = (
                sem(f"out_{n}") for n in ("wgt", "dst", "pen", "src", "zero", "cnt"))
            dst_f, src_f, pen_f, tlast_ps, bcnt_ok, bcnt_ps, tiles_ok, cnt_ok = (
                sem(f"has_{n}") for n in ("dstf", "srcf", "penf", "tlastps", "bcnt", "bcntps", "tiles", "cnt"))
            tlast_sb, xn_ok, xnT_ps, xnT_sb, enc_ps, enc_sb= (
                sem(f"has_{n}") for n in ("tlastsb", "xn", "xnTps", "xnTsb", "encps", "encsb"))
            ln0 = tuple(sem(f"ln0_{n}") for n in ("centred", "squared", "rooted")) + (1,)
            set_step, in_attrw = sem("set_step"), sem("in_attrw")
            node_ok, signs_ok, in_mlp = sem("node_ok"), sem("signs_ok"), sem("in_mlp")
            N_CLEAR = 10
            SIGNED = range(1, NT, 2)

            with nc.Block() as block:
                @block.sync
                def _(sp):
                    real = (P - 1) * FLAT
                    for n, (dest, flat, done) in enumerate(((dflat_i, dst, in_dst), (sflat_i, src, in_src),
                                                            (wflat, edge_weight, in_wgt))):
                        sp.wait_ge(cleared, n + 1)
                        sp.dma_start(dest[0:P - 1, :], flat[0:real].rearrange("(p i) -> p i", i=FLAT)).then_inc(done, 16)
                        sp.dma_start(dest[P - 1:P, 0:FLAT_REAL], flat[real:E].unsqueeze(0)).then_inc(done, 16)
                        if n == 0:
                            sp.wait_ge(cleared, 4)
                            sp.dma_start(h_cur[0:N // NT, :, :].rearrange("p t d -> p (t d)"),
                                         x.rearrange("(p t) d -> p (t d)", t=NT)).then_inc(in_x, 16)
                    sp.dma_start(encWs[:, :], encW).then_inc(in_enc, 16)
                    sp.dma_start(encbs[:, :], encb.partition_broadcast(P)).then_inc(in_enc, 16)
                    sp.wait_ge(in_wgt, 32)
                    sp.dma_start(wgt_flat.rearrange("(p i) -> p i", i=FLAT), wflat[:, :]).then_inc(out_wgt, 16)
                    sp.wait_ge(cleared, N_CLEAR)
                    sp.dma_start(sums[ZROW:ZROW + P, 0:D], ones[:, 0:D]).then_inc(out_zero, 16)
                    sp.dma_start(sums[ZROW:ZROW + P, D:D2], zero[:, 0:D]).then_inc(out_zero, 16)
                    for a in acc:
                        sp.dma_start(a.rearrange("(p t) d -> p (t d)", p=P), zero[:, :]).then_inc(out_zero, 16)
                    sp.wait_ge(out_wgt, 16)
                    sp.wait_ge(out_zero, 16 * (2 + ACCS))

                @block.gpsimd
                def _(g):
                    g.iota(node_i[:, :], [[1, NT]], 0, NT).then_inc(pool_made, 1)
                    g.iota(win_i[:, :], [[W, NW]], HALF, 0).then_inc(pool_made, 1)
                    g.dma_start(b_first_i[:, :], dst[HALF:HALF + 1].partition_broadcast(P)).then_inc(in_bfirst, 16)
                    g.wait_ge(cleared, N_CLEAR)
                    g.affine_select(out=ident[:, :], in_=ident[:, :], compare_op=ALU.not_equal, fill=1.0, base=0,
                                    pattern=[[-1, P]], channel_multiplier=1).then_inc(id_made, 1)

                    dst_flat = dst_tab.rearrange("a b -> (a b)")
                    g.wait_ge(dst_f, 1)
                    g.dma_start(dst_flat[0:EPAD].rearrange("(p i) -> p i", i=FLAT), dflat[:, :]).then_inc(out_dst, 16)
                    g.dma_start(dst_tab[TILES:TILES + 1, :], padrow[:, :]).then_inc(out_dst, 16)
                    g.wait_ge(out_dst, 32)
                    g.dma_start(dprev[0:1, 1:FLAT], dst_flat[0:FLAT - 1].unsqueeze(0)).then_inc(in_prev, 16)
                    g.dma_start(dprev[1:P, :], dst_flat[FLAT - 1:FLAT - 1 + (P - 1) * FLAT]
                                .rearrange("(p i) -> p i", i=FLAT)).then_inc(in_prev, 16)
                    g.dma_start(tlast[:, :], dst_tab[0:TILES, P - 1:P].rearrange("a b -> b a"),
                                allow_slow_non_contiguous=True).then_inc(in_tlast, 16)
                    g.wait_ge(src_f, 1)
                    g.dma_start(src_flat.rearrange("(p i) -> p i", i=FLAT), sflat[:, :]).then_inc(out_src, 16)
                    g.wait_ge(pen_f, 1)
                    g.dma_start(run_pen[0:EPAD].rearrange("(p i) -> p i", i=FLAT), pen[:, :]).then_inc(out_pen, 16)
                    g.dma_start(run_pen[EPAD:EPAD + 16].unsqueeze(0), pen_end[:, :]).then_inc(out_pen, 16)
                    g.wait_ge(out_pen, 32)
                    g.dma_start(cpen_b[:, :], run_pen[HALF:HALF + 1].unsqueeze(0)).then_inc(in_cpen, 16)

                    g.wait_ge(tiles_ok, 1)
                    for t in range(NT):
                        g.indirect_dma_start(rows[:, t, :], None, dst_tab[:, :], bass.IndirectOffsetOnAxis(
                            ap=cnt_i[:, t:t + 1], axis=0)).then_inc(in_rows, 16)
                    g.wait_ge(cnt_ok, 1)
                    g.dma_start(cnt_tab.rearrange("(p t) -> p t", t=NT), cnt_r[:, :]).then_inc(out_cnt, 16)
                    g.wait_ge(out_cnt, 16)
                    g.dma_start(before[0:1, 1:NT], cnt_tab[0:NT - 1].unsqueeze(0)).then_inc(in_cnt, 16)
                    g.dma_start(before[1:P, :], cnt_tab[NT - 1:NT - 1 + (P - 1) * NT]
                                .rearrange("(p t) -> p t", t=NT)).then_inc(in_cnt, 16)
                    g.wait_ge(out_src, 16)

                @block.scalar
                def _(a):
                    a.wait_ge(cleared, N_CLEAR)
                    a.dma_start(attrW[0:D, 0:D], eencW).then_inc(in_attrw, 16)
                    a.dma_start(attrW[D:D2, D:D2], eencW).then_inc(in_attrw, 16)
                    with nc.allow_non_contiguous_dma("columns of parameters, once"):
                        a.dma_start(attrB[0:D, :], eencb.unsqueeze(1)).then_inc(in_par, 16)
                        a.dma_start(attrB[D:D2, :], eencb.unsqueeze(1)).then_inc(in_par, 16)
                        a.dma_start(lnGs[:, :], lnG.rearrange("l d -> d l")).then_inc(in_par, 16)
                        a.dma_start(lnBs[:, :], lnB.rearrange("l d -> d l")).then_inc(in_par, 16)
                    a.dma_start(W1s[0:D, :, :], W1.rearrange("l k m -> k l m")).then_inc(in_mlp, 16)
                    a.dma_start(W1s[D:D + 1, :, :], b1.unsqueeze(0)).then_inc(in_mlp, 16)
                    a.dma_start(W2s[:, :, :], W2.rearrange("l k m -> k l m")).then_inc(in_mlp, 16)
                    a.dma_start(b2s.rearrange("p l d -> p (l d)"),
                                b2.rearrange("l d -> (l d)").partition_broadcast(P)).then_inc(in_mlp, 16)
                    for dest, v in ((nGs, normG), (nBs, normB)):
                        a.dma_start(dest[:, 0:L - 1, :].rearrange("p l d -> p (l d)"),
                                    v[1:L, :].rearrange("l d -> (l d)").partition_broadcast(P)).then_inc(in_par, 16)
                        a.dma_start(dest[:, L - 1, :], v[0, :].partition_broadcast(P)).then_inc(in_par, 16)
                    a.dma_start(ts[:, :], t.partition_broadcast(P)).then_inc(in_par, 16)
                    a.dma_start(linWs[:, :], linW).then_inc(in_par, 16)
                    a.dma_start(linbs[:, :], linb.partition_broadcast(P)).then_inc(in_par, 16)
                    a.wait_ge(node_ok, 1)
                    a.wait_ge(tlast_sb, 3)
                    for n in SIGNED:
                        ins = a.activation(signs[:, :], tlast_b[:, :], ACT.Sign, bias=node_h[:, n:n + 1], scale=-1.0,
                                           accum_out=cnt_t[:, n:n + 1]).then_inc(signs_ok, 1)
                        a.wait_ge(signs_ok, n // 2 + 1)
                    layer_norm_scalar(a, xn[:, :, :], x_acc[:, :, :], stats, NT, ln0)
                    for k in range(NC_CHUNK):
                        for half in range(2):
                            a.wait_ge(xnT_ps, 2 * k + half + 1)
                            if k and not half:
                                a.wait_ge(enc_ps, k)
                            a.activation(xnT[:, half, :], ps[4 + half][0:D, :], ACT.Copy).then_inc(xnT_sb, 1)
                    a.wait_ge(in_par, 16 * 11)
                    a.wait_ge(in_attrw, 32)

                @block.tensor
                def _(pe):
                    pe.wait_ge(cleared, N_CLEAR)
                    pe.wait_ge(id_made, 1)
                    pe.wait_ge(in_tlast, 16)
                    for i in range(3):
                        cols = slice(i * TILES // 3, (i + 1) * TILES // 3)
                        pe.matmul(ps[1 + i][:, 0:TILES // 3], ones[0:1, :], tlast[:, cols],
                                  start=True, stop=True).then_inc(tlast_ps, 1)
                    pe.wait_ge(bcnt_ok, 1)
                    pe.matmul(ps[0][:, 0:1], ones[:, :], b_cnt[:, :], start=True, stop=True).then_inc(bcnt_ps, 1)
                    pe.wait_ge(xn_ok, 1)
                    pe.wait_ge(in_enc, 32)
                    for k in range(NC_CHUNK):
                        if k:
                            pe.wait_ge(xnT_sb, 2 * k)
                        for i in range(CT):
                            ins = pe.matmul(ps[4 + i // GT][0:D, i % GT * P:(i % GT + 1) * P], xn[:, k * CT + i, :],
                                            ident[:, :], start=True, stop=True)
                            if i % GT == GT - 1:
                                ins.then_inc(xnT_ps, 1)
                        pe.wait_ge(xnT_sb, 2 * k + 2)
                        if k:
                            pe.wait_ge(enc_sb, k)
                        for i in range(CT):
                            ins = pe.matmul(ps[6][:, i * D:(i + 1) * D], xnT[:, i // GT, i % GT * P:(i % GT + 1) * P],
                                            encWs[:, :], start=True, stop=True)
                        ins.then_inc(enc_ps, 1)

                @block.vector
                def _(v):
                    for buf, value in ((dflat_i[:, :], 8191), (sflat_i[:, :], 0), (wflat[:, :], 0.0),
                                       (h_cur[:, :, :], 0.0), (ones[:, :], 1.0), (ident[:, :], 0.0),
                                       (attrW[:, :], 0.0), (dprev[:, :], -1.0), (zeros[:, :], 0.0),
                                       (zero[:, :], 0.0)):
                        v.memset(buf, value).then_inc(cleared, 1)
                    link = Chain(v, set_step)
                    v.memset(padrow[:, :], 8191.0)
                    v.memset(before[:, :], 0.0)
                    link(v.memset(pen_end[:, :], -BIG))
                    v.wait_ge(in_dst, 32)
                    v.wait_ge(cleared, N_CLEAR)
                    v.tensor_copy(dflat[:, :], dflat_i[:, :]).then_inc(dst_f, 1)
                    v.wait_ge(dst_f, 1)
                    v.wait_ge(in_bfirst, 16)
                    link(v.tensor_copy(b_first[:, :], b_first_i[:, :]))
                    v.tensor_scalar(junk[:, :], dflat[:, :], b_first[:, 0:1], None, ALU.is_le, ALU.add,
                                    accum_out=b_cnt[:, :]).then_inc(bcnt_ok, 1)
                    v.wait_ge(in_src, 32)
                    v.tensor_copy(sflat[:, :], sflat_i[:, :]).then_inc(src_f, 1)
                    v.wait_ge(in_prev, 32)
                    v.wait_ge(bcnt_ok, 1)
                    link(v.tensor_tensor(junk[:, :], dflat[:, :], dprev[:, :], ALU.is_equal))
                    v.tensor_scalar(pen[:, :], junk[:, :], -0.5, 2.0 * BIG, ALU.add, ALU.mult).then_inc(pen_f, 1)
                    v.wait_ge(pen_f, 1)

                    for i in range(3):
                        v.wait_ge(tlast_ps, i + 1)
                        v.tensor_copy(tlast_b[:, i * TILES // 3:(i + 1) * TILES // 3], ps[1 + i][:, 0:TILES // 3]
                                      ).then_inc(tlast_sb, 1)
                    v.wait_ge(pool_made, 2)
                    v.tensor_copy(node[:, :], node_i[:, :])
                    link(v.tensor_copy(win_f[:, :], win_i[:, :]))
                    v.tensor_scalar(node_h[:, :], node[:, :], 0.5, None, ALU.add).then_inc(node_ok, 1)
                    v.wait_ge(tlast_sb, 3)
                    for n in range(0, NT, 2):
                        link(v.tensor_scalar(junk[:, :], tlast_b[:, :], node[:, n:n + 1], None, ALU.is_le, ALU.add,
                                             accum_out=cnt_t[:, n:n + 1]))
                    v.wait_ge(signs_ok, len(SIGNED))
                    signed = cnt_t.rearrange("p (n s) -> p n s", s=2)[:, :, 1]
                    link(v.tensor_scalar(signed, signed, 0.5, 0.5 * TILES, ALU.mult, ALU.add))
                    v.tensor_copy(cnt_i[:, :], cnt_t[:, :]).then_inc(tiles_ok, 1)
                    v.wait_ge(in_x, 16)
                    layer_norm(v, link, xn[:, :, :], h_cur[:, :, :], x_acc[:, :, :], stats, D, ln0)
                    v.tensor_scalar(xn[:, :, :], xn[:, :, :], 0.0, None, ALU.max).then_inc(xn_ok, 1)
                    for k in range(NC_CHUNK):
                        v.wait_ge(enc_ps, k + 1)
                        v.tensor_tensor(h_cur[:, k * CT:(k + 1) * CT, :], ps[6].rearrange("p (t d) -> p t d", d=D),
                                        encbs.unsqueeze(1).broadcast_to([P, CT, D]), ALU.add).then_inc(enc_sb, 1)
                    v.wait_ge(enc_sb, NC_CHUNK)
                    v.memset(x_acc[:, :, :], 0.0)
                    v.memset(ln_eps[:, :], LN_EPS)

                    v.wait_ge(in_mlp, 64)
                    for n, (mat, parts, width) in enumerate(((W1s, D + 1, D2), (W2s, D2, D), (b2s, P, D))):
                        mean = wmean[0:parts, n, :]
                        link(v.tensor_reduce(mean, mat[:, :, :], AX_X, ALU.add))
                        link(v.tensor_scalar(mean, mean, 1.0 / width, None, ALU.mult))
                        link(v.tensor_tensor(mat[:, :, :], mat[:, :, :], mean.unsqueeze(2).broadcast_to([parts, L, width]),
                                             ALU.subtract))

                    v.wait_ge(bcnt_ps, 1)
                    v.tensor_scalar(b_last[:, 0:1], ps[0][:, 0:1], -1.0, None, ALU.add)
                    link(v.tensor_scalar(b_last[:, 1:2], ps[0][:, 0:1], -1.0 - W, None, ALU.add))
                    v.tensor_copy(patch_i[:, 0:1], b_last[:, 0:1])
                    v.tensor_copy(patch_i[:, 1:2], b_first[:, 0:1])
                    v.tensor_scalar(win_le[:, :], win_f[:, :], b_last[:, 0:1], None, ALU.is_le)
                    link(v.tensor_scalar(win_hot[:, :], win_f[:, :], b_last[:, 1:2], None, ALU.is_gt))
                    link(v.tensor_tensor(win_hot[:, :], win_hot[:, :], win_le[:, :], ALU.mult))
                    v.wait_ge(in_cpen, 16)
                    link(v.tensor_copy(cpen[:, :], cpen_b[:, :]))

                    v.wait_ge(in_rows, 16 * NT)
                    for n in range(NT):
                        link(v.tensor_scalar(junk[:, 0:P], rows[:, n, :], node[:, n:n + 1], None, ALU.is_le, ALU.add,
                                             accum_out=cnt_r[:, n:n + 1]))
                    v.scalar_tensor_tensor(out=cnt_r[:, :], in0=cnt_t[:, :], scalar=float(P), in1=cnt_r[:, :],
                                           op0=ALU.mult, op1=ALU.add).then_inc(cnt_ok, 1)
                    v.wait_ge(cnt_ok, 1)
                    v.wait_ge(in_cnt, 32)
                    link(v.tensor_tensor(has[:, :], cnt_r[:, :], before[:, :], ALU.is_gt))
                    link(v.tensor_tensor(before[:, :], before[:, :], node[:, :], ALU.subtract))
                    link(v.scalar_tensor_tensor(out=before[:, :], in0=before[:, :], scalar=-float(EPAD), in1=has[:, :],
                                                op0=ALU.add, op1=ALU.mult))
                    link(v.scalar_tensor_tensor(out=before[:, :], in0=before[:, :], scalar=float(EPAD), in1=node[:, :],
                                                op0=ALU.add, op1=ALU.add))
                    link(v.tensor_copy(first_idx[:, :], before[:, :]))
                    link(v.scalar_tensor_tensor(out=cnt_t[:, :], in0=cnt_r[:, :], scalar=-1.0 - ZROW, in1=has[:, :],
                                                op0=ALU.add, op1=ALU.mult))
                    link(v.tensor_scalar(cnt_t[:, :], cnt_t[:, :], float(ZROW), None, ALU.add))
                    link(v.tensor_copy(last_idx[:, :], cnt_t[:, :]))

        with ExitStack() as c:
            xg = [sb(f"xg{i}", [P, K, 2, D], F32, c) for i in range(2)]
            ea = [sb(f"ea{i}", [P, 2, K, D], F32, c) for i in range(2)]
            at = sb("at", [P, NG, GC], F32, c)
            idx = [sb(f"idx{i}", [P, 2, K], I32, c) for i in range(2)]
            rp = [sb(f"rp{i}", [P, W + 1], BF16, c) for i in range(2)]
            keep = [sb(f"keep{i}", [P, W], BF16, c) for i in range(2)]
            u = [sb(f"u{i}", [P, W], F32, c) for i in range(2)]
            lg = [sb(f"lg{i}", [P, W], F32, c) for i in range(2)]
            runmax = sb("runmax", [P, W], F32, c)
            segmax = sb("segmax", [P, W], F32, c)
            ex = sb("ex", [P, W + 1], F32, c)
            uex = sb("uex", [P, W], F32, c)
            den = [sb(f"den{i}", [P, W], F32, c) for i in range(2)]
            num = [sb(f"num{i}", [P, W], F32, c) for i in range(2)]
            st_all = sb("st_all", [P, 2, 2, K, D2], F32, c)
            st = [st_all[:, i, :, :, :] for i in range(2)]
            carry = sb("carry", [P, 4], F32, c)
            start2 = sb("start2", [P, 2], F32, c)
            wmax = sb("wmax", [P, NW], F32, c)
            wjunk = sb("wjunk", [P, NW], F32, c)
            tcur = sb("tcur", [P, 2], F32, c)
            lncur = sb("lncur", [D2, 2], F32, c)
            W1c = sb("W1c", [D + 1, D2], F32, c)
            W2c = sb("W2c", [D2, D], F32, c)
            prow = sb("prow", [1, 4, D2], F32, c)
            pdiff = sb("pdiff", [1, 2, D], F32, c)
            pmax = sb("pmax", [1, D], F32, c)
            pold = sb("pold", [1, 2, D], F32, c)
            pnew = sb("pnew", [1, 2, D], F32, c)
            ptmp = sb("ptmp", [1, 2, D], F32, c)
            dn = st_all.rearrange("p b h k c -> p (b h k) c")[:, 0:NT, :]
            rec = sb("rec", [P, CT, D], F32, c)
            hin = sb("hin", [P, CT, D], F32, c)
            hinT = sb("hinT", [D + 1, CT * P], F32, c)
            y = sb("y", [P, CT, D2], F32, c)
            hn = sb("hn", [P, CT, D], F32, c)
            sqjunk = sb("sqjunk", [P, CT, D2], BF16, c)
            yroot = sb("yroot", [P, CT], F32, c)
            xroot = sb("xroot", [P, CT], F32, c)
            yinv = sb("yinv", [P, CT], F32, c)
            xinv = sb("xinv", [P, CT], F32, c)
            zT = sb("zT", [D2, CT * P], F32, c)

            xg_in = [[sem(f"xg_in{i}_{gr}") for gr in range(NG)] for i in range(2)]
            ea_in, idx_in, rp_in, st_out = (
                [sem(f"{n}{i}") for i in range(2)] for n in ("ea_in", "idx_in", "rp_in", "st_out"))
            z_ps, u_ok, l_ok, diff_ok, ex_ok, max_ok, sums_ok, back_ps, back_sb = (
                sem(n) for n in ("z_ps", "u_ok", "l_ok", "diff_ok", "ex_ok", "max_ok", "sums_ok", "back_ps", "back_sb"))
            dve_step, node_step, tcur_ok, gather_go = (
                sem(n) for n in ("dve_step", "node_step", "tcur_ok", "gather_go"))
            carry_ok, prow_ps, pold_in, pdiff_ok, pexp_ok, pnew_ok, patched = (
                sem(n) for n in ("carry_ok", "prow_ps", "pold_in", "pdiff_ok", "pexp_ok", "pnew_ok", "patched"))
            dn_in = [sem(f"dn_in{i}") for i in range(NC_CHUNK)]
            hin_ok, hinT_ps, hinT_sb, y_ps, ysum_ok, yroot_ok, y_ok, yT_ps, zT_sb, o_ps = (
                sem(n) for n in ("hin_ok", "hinT_ps", "hinT_sb", "y_ps", "ysum_ok", "yroot_ok", "y_ok", "yT_ps", "zT_sb",
                                 "o_ps"))
            x_ok, xsum_ok, xroot_ok, hn_ok, h_ok, tab_out = (
                sem(n) for n in ("x_ok", "xsum_ok", "xroot_ok", "hn_ok", "h_ok", "tab_out"))
            at_ps, at_sb, heads_zero, load_go = sem("at_ps"), sem("at_sb"), sem("heads_zero"), sem("load_go")
            BU = 2 * NG
            Z0, U0, L0, M0, S0, BP0, BS0, A0 = 2 * NG, NG, 2, 2, 2, 2 * BU, 3, 2
            PAIRS = NW // 2

            with nc.Block() as block:
                @block.sync
                def _(sp):
                    last = sp.value_load(patch_i[0:1, 0:1], min_val=HALF, max_val=EPAD - 1)

                    def load(g, w, b, parts=P):
                        sp.wait_ge(z_ps, NG * g + NG - NG * 2 + Z0)
                        for h in range(2):
                            n = parts if h else P
                            piece = bass.ds(h * HALF + w * W, n * K)
                            sp.dma_start(idx[b][0:n, h, :], src[piece].rearrange("(p k) -> p k", k=K)).then_inc(idx_in[b], 16)
                            sp.dma_start(ea[b][0:n, h, :, :], edge_attr[piece, :].rearrange("(p k) f -> p k f", k=K)
                                         ).then_inc(ea_in[b], 16)
                        sp.wait_ge(max_ok, g + 1)
                        sp.wait_ge(l_ok, g + 1)
                        sp.sem_inc(load_go, 1)
                        for h in range(2):
                            sp.dma_start(rp[b][h * D:(h + 1) * D, :], run_pen[bass.ds(h * HALF + w * W, W + 1)]
                                         .partition_broadcast(D)).then_inc(rp_in[b], 16)

                    sums_v = sums[0:EPAD, :].rearrange("(h w p k) c -> h w p (k c)", h=2, w=NW, p=P)

                    def store(g, w, b):
                        sp.wait_ge(back_sb, BU * (g + 1) + BS0)
                        for h in range(2):
                            sp.dma_start(sums_v[h, w], st[b][:, h, :, :].rearrange("p k c -> p (k c)")
                                         ).then_inc(st_out[b], 16)

                    head_pieces = run_head[0:EPAD, :].rearrange("(g p i) d -> g p (i d)", g=L * NW, p=P)

                    def clear(g):
                        sp.dma_start(head_pieces[g], zeros[:, :]).then_inc(heads_zero, 16)

                    def store_nodes(k):
                        sp.dma_start(h_tab.rearrange("(p t) d -> p t d", t=NT)[:, k * CT:(k + 1) * CT, :],
                                     h_cur[:, k * CT:(k + 1) * CT, :]).then_inc(tab_out, 16)

                    for k in range(NC_CHUNK):
                        store_nodes(k)
                    load(0, 0, 0)
                    load(1, 1, 1)
                    with sp.Fori(0, L) as l:
                        with sp.Fori(0, PAIRS - 2) as i:
                            for b in range(2):
                                load(l * NW + 2 * i + 2 + b, 2 * i + 2 + b, b)
                                store(l * NW + 2 * i + b, 2 * i + b, b)
                                clear(l * NW + 2 * i + b)
                        for b in range(2):
                            load(l * NW + NW - 2 + b, NW - 2 + b, b, B_PARTS if b else P)
                            store(l * NW + NW - 4 + b, NW - 4 + b, b)
                            clear(l * NW + NW - 4 + b)
                        for b in range(2):
                            store(l * NW + NW - 2 + b, NW - 2 + b, b)
                            clear(l * NW + NW - 2 + b)
                        for b in range(2):
                            sp.wait_ge(st_out[b], 32 * PAIRS * (l + 1) + 32)
                        sp.dma_start(pold.rearrange("p a d -> p (a d)"), sums[bass.ds(last, 1), :]).then_inc(pold_in, 16)
                        for b in range(2):
                            load((l + 1) * NW + b, b, b)
                        sp.wait_ge(pnew_ok, l + 1)
                        sp.dma_start(sums[bass.ds(last, 1), :], pnew.rearrange("p a d -> p (a d)")).then_inc(patched, 16)
                        for k in range(NC_CHUNK):
                            sp.wait_ge(h_ok, NC_CHUNK * l + k + 1)
                            store_nodes(k)
                    sp.wait_ge(tab_out, 16 * NC_CHUNK * (L + 1))
                    sp.wait_ge(heads_zero, 16 * L * NW)
                    for b in range(2):
                        sp.wait_ge(idx_in[b], 32 * (PAIRS * L + 1))
                        sp.wait_ge(ea_in[b], 32 * (PAIRS * L + 1))
                        sp.wait_ge(rp_in[b], 32 * (PAIRS * L + 1))

                @block.gpsimd
                def _(g_):
                    def window(g, i, l, b):
                        g_.wait_ge(idx_in[b], 32 * (l * PAIRS + i + 1))
                        g_.sem_inc(gather_go, 1)
                        for k in range(K):
                            if k % GT == 0:
                                g_.wait_ge(z_ps, NG * g + k // GT + 1 - NG * 2 + Z0)
                                g_.sem_inc(gather_go, 1)
                            for h in range(2):
                                g_.indirect_dma_start(xg[b][:, k, h, :], None, h_tab[:, :], bass.IndirectOffsetOnAxis(
                                    ap=idx[b][:, h, k:k + 1], axis=0)).then_inc(xg_in[b][k // GT], 16)

                    with g_.Fori(0, L) as l:
                        g_.wait_ge(tab_out, 16 * NC_CHUNK * (l + 1))
                        g_.sem_inc(gather_go, 1)
                        with g_.Fori(0, PAIRS) as i:
                            for b in range(2):
                                window(l * NW + 2 * i + b, i, l, b)
                        g_.wait_ge(patched, 16 * (l + 1))
                        g_.sem_inc(gather_go, 1)
                        for t_ in range(NT):
                            g_.indirect_dma_start(dn[:, t_, :], None, sums[:, :], bass.IndirectOffsetOnAxis(
                                ap=last_idx[:, t_:t_ + 1], axis=0)).then_inc(dn_in[t_ // CT], 16)

                @block.tensor
                def _(pe):
                    pe.sem_inc(z_ps, Z0)
                    pe.sem_inc(back_ps, BP0)

                    def forward(g, i, l, b):
                        pe.wait_ge(ea_in[b], 32 * (l * PAIRS + i + 1))
                        for gr in range(NG):
                            pe.wait_ge(at_sb, NG * g + gr + 1 - 2 + A0)
                            for j in range(GT):
                                for h in range(2):
                                    ins = pe.matmul(ps[6 + (NG * b + gr) % 2][h * D:(h + 1) * D, j * P:(j + 1) * P],
                                                    ea[b][:, h, gr * GT + j, :], ident[:, :], start=True, stop=True)
                            ins.then_inc(at_ps, 1)
                        for gr in range(NG):
                            pe.wait_ge(u_ok, NG * g + gr + 1 - NG + U0)
                            pe.wait_ge(at_sb, NG * g + gr + 1 + A0)
                            pe.matmul(ps[gr][:, :], attrW[:, :], at[:, gr, :], start=True, stop=True)
                            pe.wait_ge(xg_in[b][gr], 32 * GT * (l * PAIRS + i + 1))
                            for j in range(GT):
                                ins = pe.matmul(ps[gr][:, j * P:(j + 1) * P],
                                                xg[b][:, gr * GT + j, :, :].rearrange("p h d -> p (h d)"), ident[:, :],
                                                start=False, stop=True, skip_group_check=True)
                            ins.then_inc(z_ps, 1)

                    def back(g, b):
                        pe.wait_ge(sums_ok, g + 1 + S0)
                        for r in range(BU):
                            gr, s_ = r // 2, r % 2
                            pe.wait_ge(back_sb, BU * g + r + 1 - 3 + BS0)
                            sum_v = (den, num)[s_][b].rearrange("c (p k) -> c k p", k=K)
                            for j in range(GT):
                                ins = pe.matmul(ps[3 + r % 3][:, j * P:(j + 1) * P], sum_v[:, gr * GT + j, :],
                                                ident[:, :], start=True, stop=True)
                            ins.then_inc(back_ps, 1)

                    with pe.Fori(0, L) as l:
                        g0 = l * NW
                        forward(g0, 0, l, 0)
                        with pe.Fori(0, PAIRS - 1) as i:
                            forward(g0 + 2 * i + 1, i, l, 1)
                            back(g0 + 2 * i, 0)
                            forward(g0 + 2 * i + 2, i + 1, l, 0)
                            back(g0 + 2 * i + 1, 1)
                        forward(g0 + NW - 1, PAIRS - 1, l, 1)
                        back(g0 + NW - 2, 0)
                        back(g0 + NW - 1, 1)

                        pe.wait_ge(carry_ok, l + 1)
                        pe.wait_ge(back_sb, BU * (g0 + NW) + BS0)
                        for j in range(4):
                            ins = pe.matmul(ps[3][0:1, j * P:(j + 1) * P], carry[:, j:j + 1], ident[:, :],
                                            start=True, stop=True)
                        ins.then_inc(prow_ps, 1)
                        pe.wait_ge(u_ok, NG * (g0 + NW) + U0)
                        base = NC_CHUNK * l
                        for k in range(NC_CHUNK + 1):
                            if k < NC_CHUNK:
                                pe.wait_ge(hin_ok, base + k + 1)
                                for j in range(CT):
                                    dest = ps[j // GT][0:D, j % GT * P:(j % GT + 1) * P]
                                    pe.matmul(dest, h_cur[:, k * CT + j, :], ident[:, :], start=True, stop=False)
                                    ins = pe.matmul(dest, hin[:, j, :], ident[:, :], start=False, stop=True)
                                ins.then_inc(hinT_ps, 1)
                                pe.wait_ge(hinT_sb, base + k + 1)
                                if k:
                                    pe.wait_ge(y_ok, base + k)
                                for j in range(CT):
                                    ins = pe.matmul(ps[6 + j // GT][:, j % GT * P:(j % GT + 1) * P],
                                                    hinT[:, j * P:(j + 1) * P], W1c[:, :], start=True, stop=True)
                                ins.then_inc(y_ps, 1)
                            if k:
                                pe.wait_ge(y_ok, base + k)
                                for j in range(CT):
                                    ins = pe.matmul(ps[3 + j // GT][:, j % GT * P:(j % GT + 1) * P], y[:, j, :],
                                                    ident[:, :], start=True, stop=True)
                                ins.then_inc(yT_ps, 1)
                                pe.wait_ge(zT_sb, base + k)
                                if k > 1:
                                    pe.wait_ge(x_ok, base + k - 1)
                                for j in range(CT):
                                    ins = pe.matmul(ps[2][:, j * D:(j + 1) * D], zT[:, j * P:(j + 1) * P], W2c[:, :],
                                                    start=True, stop=True)
                                ins.then_inc(o_ps, 1)

                @block.scalar
                def _(a):
                    a.sem_inc(u_ok, U0)
                    a.sem_inc(at_sb, A0)
                    a.sem_inc(l_ok, L0)
                    a.sem_inc(back_sb, BS0)
                    for b in range(2):
                        a.sem_inc(st_out[b], 32)

                    def logits(g, i, l, b):
                        for gr in range(NG):
                            a.wait_ge(z_ps, NG * (g - 1) + gr + 1 + Z0)
                            a.wait_ge(at_ps, NG * g + gr + 1)
                            a.activation(at[:, gr, :], ps[6 + (NG * b + gr) % 2][:, :], ACT.Copy).then_inc(at_sb, 1)
                        a.wait_ge(sums_ok, g + 1 - 2 + S0)
                        a.wait_ge(rp_in[b], 32 * (l * PAIRS + i + 1))
                        a.activation(keep[b][:, :], rp[b][:, 0:W], ACT.Relu, scale=1.0 / BIG)
                        for gr in range(NG):
                            a.wait_ge(z_ps, NG * g + gr + 1 + Z0)
                            a.activation(u[b].rearrange("c (p k) -> c k p", k=K)[:, gr * GT:(gr + 1) * GT, :],
                                         ps[gr].rearrange("c (k p) -> c k p", p=P), ACT.Relu, bias=attrB[:, 0:1]
                                         ).then_inc(u_ok, 1)
                        a.wait_ge(u_ok, NG * (g + 1) + U0)
                        a.activation(lg[b][:, :], u[b][:, :], ACT.Identity, bias=tcur[:, 1:2], scale=tcur[:, 0:1]
                                     ).then_inc(l_ok, 1)

                    def empty(g, i, l, b):
                        a.wait_ge(st_out[b], 32 * (l * PAIRS + i) + 32)
                        for r in range(BU):
                            gr, s_ = r // 2, r % 2
                            a.wait_ge(back_ps, BU * g + r + 1 + BP0)
                            a.activation(st[b].rearrange("p h k c -> p k h c")[:, gr * GT:(gr + 1) * GT, :,
                                                                               s_ * D:(s_ + 1) * D],
                                         ps[3 + r % 3].rearrange("p (k h c) -> p k h c", k=GT, h=2), ACT.Copy
                                         ).then_inc(back_sb, 1)

                    def exponentials(g):
                        a.wait_ge(diff_ok, g + 1)
                        a.activation(ex[:, :], ex[:, :], ACT.Exp, scale=-1.0).then_inc(ex_ok, 1)

                    with a.Fori(0, L) as l:
                        g0 = l * NW
                        a.wait_ge(tcur_ok, l + 1)
                        logits(g0, 0, l, 0)
                        exponentials(g0)
                        with a.Fori(0, PAIRS - 1) as i:
                            logits(g0 + 2 * i + 1, i, l, 1)
                            empty(g0 + 2 * i, i, l, 0)
                            exponentials(g0 + 2 * i + 1)
                            logits(g0 + 2 * i + 2, i + 1, l, 0)
                            empty(g0 + 2 * i + 1, i, l, 1)
                            exponentials(g0 + 2 * i + 2)
                        logits(g0 + NW - 1, PAIRS - 1, l, 1)
                        empty(g0 + NW - 2, PAIRS - 1, l, 0)
                        exponentials(g0 + NW - 1)
                        empty(g0 + NW - 1, PAIRS - 1, l, 1)

                        a.wait_ge(pdiff_ok, l + 1)
                        a.activation(pdiff[:, :, :], pdiff[:, :, :], ACT.Exp, scale=-1.0).then_inc(pexp_ok, 1)
                        base = NC_CHUNK * l
                        for k in range(NC_CHUNK + 2):
                            if k < NC_CHUNK:
                                a.wait_ge(hinT_ps, base + k + 1)
                                for half in range(2):
                                    ins = a.activation(hinT[0:D, half * 512:(half + 1) * 512], ps[half][0:D, :], ACT.Copy)
                                ins.then_inc(hinT_sb, 1)
                            if k > 1:
                                a.wait_ge(x_ok, base + k - 1)
                                for j in range(CT):
                                    ins = a.activation(sqjunk[:, j, 0:D], x_acc[:, (k - 2) * CT + j, :], ACT.Square,
                                                       accum_out=xroot[:, j:j + 1])
                                ins.then_inc(xsum_ok, 1)
                                a.wait_ge(xsum_ok, base + k - 1)
                                a.activation(xroot[:, :], xroot[:, :], ACT.Sqrt, scale=1.0 / D, bias=ln_eps[:, 0:1]
                                             ).then_inc(xroot_ok, 1)
                            if k < NC_CHUNK:
                                a.wait_ge(y_ps, base + k + 1)
                                for j in range(CT):
                                    ins = a.activation(sqjunk[:, j, :], ps[6 + j // GT][:, j % GT * P:(j % GT + 1) * P],
                                                       ACT.Square, accum_out=yroot[:, j:j + 1])
                                ins.then_inc(ysum_ok, 1)
                                a.wait_ge(ysum_ok, base + k + 1)
                                a.activation(yroot[:, :], yroot[:, :], ACT.Sqrt, scale=1.0 / D2, bias=ln_eps[:, 0:1]
                                             ).then_inc(yroot_ok, 1)
                            if 0 < k <= NC_CHUNK:
                                a.wait_ge(yT_ps, base + k)
                                if k > 1:
                                    a.wait_ge(o_ps, base + k - 1)
                                for half in range(2):
                                    ins = a.activation(zT[:, half * 512:(half + 1) * 512], ps[3 + half][:, :], ACT.Relu,
                                                       scale=lncur[:, 0:1], bias=lncur[:, 1:2])
                                ins.then_inc(zT_sb, 1)
                            if k > 1:
                                a.wait_ge(hn_ok, base + k - 1)
                                a.activation(h_cur[:, (k - 2) * CT:(k - 1) * CT, :], hn[:, :, :], ACT.Relu
                                             ).then_inc(h_ok, 1)

                @block.vector
                def _(v):
                    v.sem_inc(max_ok, M0)
                    v.sem_inc(sums_ok, S0)
                    STEPS = 6

                    def window(g, w, i, l, b):
                        link = Chain(v, dve_step, g * STEPS)
                        v.wait_ge(l_ok, g + 1 + L0)
                        link(v.tensor_tensor_scan(runmax[:, :], rp[b][:, 0:W], lg[b][:, :], carry[:, 0:1],
                                                  ALU.min, ALU.max))
                        v.tensor_tensor_scan(segmax[:, ::-1], rp[b][:, 1:W + 1][:, ::-1], runmax[:, ::-1], -BIG,
                                             ALU.min, ALU.max).then_inc(max_ok, 1)
                        v.wait_ge(max_ok, g + 1 + M0)
                        v.tensor_scalar(ex[:, 0:1], segmax[:, 0:1], carry[:, 0:1], 0.0, ALU.subtract, ALU.max)
                        v.tensor_copy(wmax[:, bass.ds(w, 1)], segmax[:, 0:1])
                        v.tensor_tensor(ex[:, 1:W + 1], segmax[:, :], lg[b][:, :], ALU.subtract).then_inc(diff_ok, 1)
                        v.wait_ge(diff_ok, g + 1)
                        link(v.tensor_copy(carry[:, 0:1], runmax[:, W - 1:W]))
                        v.wait_ge(ex_ok, g + 1)
                        v.tensor_scalar(start2[:, :], carry[:, 1:3], ex[:, 0:1], None, ALU.mult)
                        link(v.scalar_tensor_tensor(out=uex[:, :], in0=u[b][:, :], scalar=EPS, in1=ex[:, 1:W + 1],
                                                    op0=ALU.add, op1=ALU.mult))
                        v.wait_ge(back_ps, BU * (g - 1) + BP0)
                        link(v.tensor_tensor_scan(den[b][:, :], keep[b][:, :], ex[:, 1:W + 1], start2[:, 0:1],
                                                  ALU.mult, ALU.add))
                        v.tensor_tensor_scan(num[b][:, :], keep[b][:, :], uex[:, :], start2[:, 1:2],
                                             ALU.mult, ALU.add).then_inc(sums_ok, 1)
                        v.wait_ge(sums_ok, g + 1 + S0)
                        link(v.tensor_copy(carry[:, 1:2], den[b][:, W - 1:W]))
                        link(v.tensor_copy(carry[:, 2:3], num[b][:, W - 1:W]))

                    v.memset(hinT[D:D + 1, :], 1.0)
                    PER_LAYER = 5 + NC_CHUNK * 5
                    with v.Fori(0, L) as l:
                        link = Chain(v, node_step, l * PER_LAYER)
                        v.memset(carry[:, 0:1], -BIG)
                        v.memset(carry[:, 1:4], 0.0)
                        v.tensor_copy(W1c[:, :], W1s[:, bass.ds(l, 1), :].rearrange("k l m -> k (l m)"))
                        v.tensor_copy(W2c[:, :], W2s[:, bass.ds(l, 1), :].rearrange("k l m -> k (l m)"))
                        v.tensor_copy(lncur[:, 0:1], lnGs[:, bass.ds(l, 1)])
                        v.tensor_copy(lncur[:, 1:2], lnBs[:, bass.ds(l, 1)])
                        v.tensor_tensor(x_acc[:, :, :], x_acc[:, :, :], b2s[:, bass.ds(l, 1), :].broadcast_to([P, NT, D]),
                                        ALU.add)
                        link(v.tensor_copy(tcur[:, 0:1], ts[:, bass.ds(l, 1)]))
                        v.tensor_scalar(tcur[:, 1:2], tcur[:, 0:1], EPS, None, ALU.mult).then_inc(tcur_ok, 1)
                        with v.Fori(0, PAIRS) as i:
                            for b in range(2):
                                window(l * NW + 2 * i + b, 2 * i + b, i, l, b)

                        v.wait_ge(dve_step, (l + 1) * NW * STEPS)
                        v.tensor_tensor_reduce(wjunk[:, :], wmax[:, :], win_hot[:, :], 1.0, 0.0, ALU.mult, ALU.add,
                                               carry[:, 3:4]).then_inc(carry_ok, 1)
                        v.wait_ge(prow_ps, l + 1)
                        link(v.tensor_copy(prow.rearrange("p a d -> p (a d)"), ps[3][0:1, :]))
                        link(v.tensor_scalar(prow[:, 0, 0:D], prow[:, 0, 0:D], cpen[:, 0:1], None, ALU.min))
                        link(v.tensor_tensor(pmax[:, :], prow[:, 0, 0:D], prow[:, 3, D:D2], ALU.max))
                        v.tensor_tensor(pdiff[:, 0, :], pmax[:, :], prow[:, 0, 0:D], ALU.subtract)
                        v.tensor_tensor(pdiff[:, 1, :], pmax[:, :], prow[:, 3, D:D2], ALU.subtract).then_inc(pdiff_ok, 1)
                        v.wait_ge(pexp_ok, l + 1)
                        v.wait_ge(pold_in, 16 * (l + 1))
                        both = [1, 2, D]
                        v.tensor_tensor(ptmp[:, :, :], prow[:, 1:3, 0:D], pdiff[:, 0:1, :].broadcast_to(both), ALU.mult)
                        link(v.tensor_tensor(pnew[:, :, :], pold[:, :, :], pdiff[:, 1:2, :].broadcast_to(both), ALU.mult))
                        v.tensor_tensor(pnew[:, :, :], pnew[:, :, :], ptmp[:, :, :], ALU.add).then_inc(pnew_ok, 1)

                        base = NC_CHUNK * l
                        for k in range(NC_CHUNK + 2):
                            if k < NC_CHUNK:
                                cs = slice(k * CT, (k + 1) * CT)
                                v.wait_ge(dn_in[k], 16 * CT * (l + 1))
                                if k:
                                    v.wait_ge(hinT_ps, base + k)
                                link(v.reciprocal(rec[:, :, :], dn[:, cs, 0:D]))
                                v.tensor_tensor(hin[:, :, :], dn[:, cs, D:D2], rec[:, :, :], ALU.mult).then_inc(hin_ok, 1)
                            if k > 1:
                                cs = slice((k - 2) * CT, (k - 1) * CT)
                                v.wait_ge(o_ps, base + k - 1)
                                v.tensor_tensor(x_acc[:, cs, :], x_acc[:, cs, :], ps[2].rearrange("p (t d) -> p t d", d=D),
                                                ALU.add).then_inc(x_ok, 1)
                            if 0 < k <= NC_CHUNK:
                                v.wait_ge(yroot_ok, base + k)
                                if k > 1:
                                    v.wait_ge(yT_ps, base + k - 1)
                                link(v.reciprocal(yinv[:, :], yroot[:, :]))
                                for half in range(2):
                                    ts_ = slice(half * GT, (half + 1) * GT)
                                    ins = v.tensor_tensor(y[:, ts_, :], ps[6 + half].rearrange("p (t d) -> p t d", d=D2),
                                                          yinv[:, ts_].unsqueeze(2).broadcast_to([P, GT, D2]), ALU.mult)
                                ins.then_inc(y_ok, 1)
                            if k > 1:
                                v.wait_ge(xroot_ok, base + k - 1)
                                link(v.reciprocal(xinv[:, :], xroot[:, :]))
                                if k > 2:
                                    v.wait_ge(h_ok, base + k - 2)
                                link(v.tensor_tensor(hn[:, :, :], x_acc[:, cs, :],
                                                     xinv.unsqueeze(2).broadcast_to([P, CT, D]), ALU.mult))
                                link(v.tensor_tensor(hn[:, :, :], hn[:, :, :],
                                                     nGs[:, bass.ds(l, 1), :].broadcast_to([P, CT, D]), ALU.mult))
                                v.tensor_tensor(hn[:, :, :], hn[:, :, :], nBs[:, bass.ds(l, 1), :].broadcast_to([P, CT, D]),
                                                ALU.add).then_inc(hn_ok, 1)
                        assert link.n == PER_LAYER, link.n

        with ExitStack() as c:
            TW = 2 * K
            TB = 8
            NB = TW // TB
            hd = [sb(f"hd{i}", [P, 2, K, D], F32, c) for i in range(2)]
            hdT = [sb(f"hdT{i}", [P, W], F32, c) for i in range(2)]
            hs = [sb(f"hs{i}", [P, W], F32, c) for i in range(2)]
            rp = [sb(f"run{i}", [P, W], BF16, c) for i in range(2)]
            keep = [sb(f"kept{i}", [P, W], BF16, c) for i in range(2)]
            gh = [sb(f"gh{i}", [P, K, 2, D], F32, c) for i in range(2)]
            vm = [sb(f"vm{i}", [P, TW, D], F32, c) for i in range(2)]
            srcB = [sb(f"srcB{i}", [P, 2, W], F32, c) for i in range(2)]
            sf = [sb(f"sf{i}", [P, 2, K], F32, c) for i in range(2)]
            wl = [sb(f"wl{i}", [P, 2, K], F32, c) for i in range(2)]
            flat = sb("flat", [P, K, 2], F32, c)
            dup = sb("dup", [P, TW], F32, c)
            move = sb("move", [P, TW], F32, c)
            tgt = [sb(f"tgt{i}", [P, TW], I32, c) for i in range(2)]
            eqw = sb("eqw", [P, 2, TB, P], F32, c)
            tri = sb("tri", [P, P], F32, c)
            djunk = sb("djunk", [P, P], F32, c)
            trash_i = sb("trash_i", [P, 1], I32, c)
            trash = sb("trash", [P, 1], F32, c)
            hT = sb("hT", [D, CT * P], F32, c)
            xin = sb("xin", [P, NT, D], F32, c)
            xtmp = x_acc
            tabs = [x_acc, h_cur]

            fx_in, fclr, ftri, ftrash, fT_ps, fT_sb, fo_ps, fo_ok, f_step, fh_ok, h2_out, hb_in = (
                sem(f"f_{n}") for n in ("xin", "clr", "tri", "trash", "Tps", "Tsb", "ops", "ook", "step", "hok", "h2out",
                                        "hbin"))
            ln2 = tuple(sem(f"ln2_{n}") for n in ("centred", "squared", "rooted")) + (1,)
            hd_in, ls_in, run_in = ([sem(f"{n}{i}") for i in range(2)] for n in ("hd_in", "ls_in", "run_in"))
            set_done = [sem("set_done0"), sem("set_done1")]
            heads_out, hdT_ps, hdT_sb, scan_ok, gh_ps, gh_sb = (
                sem(n) for n in ("heads_out", "hdT_ps", "hdT_sb", "scan_ok", "gh_ps", "gh_sb"))
            eq_ok, merged_ps, v_sb, tgt_ok, m_step, scat_go, landed = (
                sem(n) for n in ("eq_ok", "merged_ps", "v_sb", "tgt_ok", "m_step", "scat_go", "landed"))
            tab_in, tab_sum, out_ok = [sem("tab_in0"), sem("tab_in1")], sem("tab_sum"), sem("out_ok")
            MP0, V0, T0, HP0, HS0, SC0, GP0, GS0 = 2 * NB, 2, 2, 2 * NG, NG, 2, 2 * NG, NG
            HBANK, GBANK, MBANK = (0, 1, 2), (3, 6, 7), (4, 5)
            SETB = TW // BATCH // 2
            PAIRS = NW // 2

            with nc.Block() as block:
                @block.sync
                def _(sp):
                    split = sp.value_load(patch_i[0:1, 1:2], min_val=0, max_val=N - 1)
                    heads = run_head[0:EPAD, :].rearrange("(h w p k) d -> h w p (k d)", h=2, w=NW, p=P)

                    def load(w, b):
                        sp.wait_ge(hdT_ps, NG * w - NG + HP0)
                        for h in range(2):
                            sp.dma_start(hd[b][:, h, :, :].rearrange("p k d -> p (k d)"), heads[h, w]).then_inc(hd_in[b], 16)
                        sp.wait_ge(scan_ok, w + 1)
                        for h in range(2):
                            sp.dma_start(rp[b][h * D:(h + 1) * D, :], run_pen[bass.ds(h * HALF + w * W, W)]
                                         .partition_broadcast(D)).then_inc(run_in[b], 16)
                        sp.wait_ge(tgt_ok, w + 1)
                        sp.sem_inc(load_go, 1)
                        for h in range(2):
                            piece = bass.ds(h * HALF + w * W, W)
                            for dest, lst in ((sf, src_flat), (wl, wgt_flat)):
                                sp.dma_start(dest[b][:, h, :], lst[piece].rearrange("(p k) -> p k", k=K)).then_inc(ls_in[b], 16)
                            sp.dma_start(srcB[b][:, h, :], src_flat[bass.ds(h * HALF + w * W, W)]
                                         .partition_broadcast(P)).then_inc(ls_in[b], 16)

                    sp.wait_ge(fclr, 1)
                    sp.dma_start(xin[0:N // NT, :, :].rearrange("p t d -> p (t d)"),
                                 x.rearrange("(p t) d -> p (t d)", t=NT)).then_inc(fx_in, 16)
                    sp.wait_ge(fh_ok, 1)
                    sp.dma_start(h_tab.rearrange("(p t) d -> p (t d)", t=NT),
                                 h_cur.rearrange("p t d -> p (t d)")).then_inc(h2_out, 16)
                    sp.wait_ge(h2_out, 16)
                    with nc.allow_non_contiguous_dma("one row, as a column"):
                        sp.dma_start(hs[1][D:D2, W - 1:W], h_tab[bass.ds(split, 1), :].rearrange("a d -> d a")
                                     ).then_inc(hb_in, 16)
                    sp.wait_ge(heads_out, 16 * NT)
                    load(0, 0)
                    load(1, 1)
                    with sp.Fori(1, PAIRS) as i:
                        load(2 * i, 0)
                        load(2 * i + 1, 1)
                    for s_ in range(2):
                        sp.wait_ge(set_done[s_], 16 * BATCH * SETB * NW)
                    for i, a in enumerate(acc):
                        if i >= 2:
                            sp.wait_ge(tab_sum, i - 1)
                        sp.dma_start(tabs[i % 2].rearrange("p t d -> p (t d)"),
                                     a[0:NPAD, :].rearrange("(p t) d -> p (t d)", t=NT)).then_inc(tab_in[i % 2], 16)
                    sp.wait_ge(tab_sum, ACCS)
                    sp.dma_start(out.rearrange("(p t) d -> p (t d)", t=NT),
                                 xin[0:N // NT, :, :].rearrange("p t d -> p (t d)")).then_inc(out_ok, 16)
                    sp.wait_ge(out_ok, 16)

                @block.gpsimd
                def _(g_):
                    g_.sem_inc(landed, 1)
                    g_.iota(trash_i[:, :], [[1, 1]], TRASH, 1).then_inc(ftrash, 1)
                    g_.wait_ge(fclr, 2)
                    g_.affine_select(out=tri[:, :], in_=tri[:, :], compare_op=ALU.is_gt, fill=0.0, base=0,
                                     pattern=[[-1, P]], channel_multiplier=1).then_inc(ftri, 1)
                    g_.wait_ge(fh_ok, 1)
                    for t_ in range(NT):
                        g_.indirect_dma_start(run_head[:, :], bass.IndirectOffsetOnAxis(
                            ap=first_idx[:, t_:t_ + 1], axis=0), h_cur[:, t_, :], None).then_inc(heads_out, 16)

                    def scatter(w, b, first=False):
                        g_.wait_ge(v_sb, NB * (w + 1) + V0)
                        g_.sem_inc(scat_go, 1)
                        g_.wait_ge(tgt_ok, w + 1 + T0)
                        g_.sem_inc(scat_go, 1)
                        for m in range(TW // BATCH):
                            if not first or m >= 2:
                                g_.wait_ge(set_done[m % 2], 16 * BATCH * (SETB * w + m // 2))
                            g_.sem_inc(landed if m == 1 else scat_go, 1)
                            for q in range(BATCH):
                                t_ = m * BATCH + q
                                g_.indirect_dma_start(acc[BATCH * (m % 2) + q][:, :], bass.IndirectOffsetOnAxis(
                                    ap=tgt[b][:, t_:t_ + 1], axis=0), vm[b][:, t_, :], None,
                                    compute_op=ALU.add).then_inc(set_done[m % 2], 16)

                    scatter(0, 0, first=True)
                    with g_.Fori(1, PAIRS) as i:
                        scatter(2 * i - 1, 1)
                        scatter(2 * i, 0)
                    scatter(NW - 1, 1)

                @block.tensor
                def _(pe):
                    pe.sem_inc(merged_ps, MP0)
                    pe.sem_inc(hdT_ps, HP0)
                    pe.sem_inc(gh_ps, GP0)
                    for k in range(NC_CHUNK):
                        if k:
                            pe.wait_ge(fT_sb, k)
                        for j in range(CT):
                            ins = pe.matmul(ps[j // GT][0:D, j % GT * P:(j % GT + 1) * P], h_cur[:, k * CT + j, :],
                                            ident[:, :], start=True, stop=True)
                        ins.then_inc(fT_ps, 1)
                        pe.wait_ge(fT_sb, k + 1)
                        if k:
                            pe.wait_ge(fo_ok, k)
                        for j in range(CT):
                            ins = pe.matmul(ps[2][:, j * D:(j + 1) * D], hT[:, j * P:(j + 1) * P], linWs[:, :],
                                            start=True, stop=True)
                        ins.then_inc(fo_ps, 1)
                    pe.wait_ge(fo_ok, NC_CHUNK)

                    def forward(w, i, b):
                        pe.wait_ge(hd_in[b], 32 * (i + 1))
                        for gr in range(NG):
                            pe.wait_ge(hdT_sb, NG * w + gr + 1 - NG + HS0)
                            for j in range(GT):
                                for h in range(2):
                                    ins = pe.matmul(ps[HBANK[gr]][h * D:(h + 1) * D, j * P:(j + 1) * P],
                                                    hd[b][:, h, gr * GT + j, :], ident[:, :], start=True, stop=True)
                            ins.then_inc(hdT_ps, 1)

                    def merge(w, b):
                        pe.wait_ge(scan_ok, w + 1 + SC0)
                        for gr in range(NG):
                            pe.wait_ge(gh_sb, NG * w + gr + 1 - NG + GS0)
                            for j in range(GT):
                                ins = pe.matmul(ps[GBANK[gr]][:, j * P:(j + 1) * P],
                                                hs[b].rearrange("c (p k) -> c k p", k=K)[:, gr * GT + j, :],
                                                ident[:, :], start=True, stop=True)
                            ins.then_inc(gh_ps, 1)
                        for q in range(NB):
                            slot = (NB * b + q) % 2
                            pe.wait_ge(gh_sb, NG * w + q + 1 + GS0)
                            pe.wait_ge(eq_ok, NB * w + q + 1)
                            pe.wait_ge(v_sb, NB * w + q + 1 - 2 + V0)
                            for j in range(TB):
                                t_ = q * TB + j
                                ins = pe.matmul(ps[MBANK[slot]][:, j * D:(j + 1) * D], eqw[:, slot, j, :],
                                                gh[b][:, t_ // 2, t_ % 2, :], start=True, stop=True)
                            ins.then_inc(merged_ps, 1)

                    forward(0, 0, 0)
                    with pe.Fori(0, PAIRS - 1) as i:
                        forward(2 * i + 1, i, 1)
                        merge(2 * i, 0)
                        forward(2 * i + 2, i + 1, 0)
                        merge(2 * i + 1, 1)
                    forward(NW - 1, PAIRS - 1, 1)
                    merge(NW - 2, 0)
                    merge(NW - 1, 1)

                @block.scalar
                def _(a):
                    a.sem_inc(v_sb, V0)
                    a.sem_inc(hdT_sb, HS0)
                    a.sem_inc(gh_sb, GS0)
                    for k in range(NC_CHUNK):
                        a.wait_ge(fT_ps, k + 1)
                        if k:
                            a.wait_ge(fo_ps, k)
                        for half in range(2):
                            ins = a.activation(hT[:, half * 512:(half + 1) * 512], ps[half][0:D, :], ACT.Copy)
                        ins.then_inc(fT_sb, 1)
                    layer_norm_scalar(a, h_cur[:, :, :], xtmp[:, :, :], stats, NT, ln2)

                    def heads(w, i, b):
                        a.wait_ge(scan_ok, w + 1)
                        a.wait_ge(run_in[b], 32 * (i + 1))
                        a.activation(keep[b][:, :], rp[b][:, :], ACT.Relu, scale=1.0 / BIG)
                        for gr in range(NG):
                            a.wait_ge(hdT_ps, NG * w + gr + 1 + HP0)
                            a.activation(hdT[b].rearrange("c (p k) -> c k p", k=K)[:, gr * GT:(gr + 1) * GT, :],
                                         ps[HBANK[gr]].rearrange("c (k p) -> c k p", p=P), ACT.Copy).then_inc(hdT_sb, 1)

                    def rows(w, b):
                        a.wait_ge(merged_ps, NB * (w - 1) + MP0)
                        for gr in range(NG):
                            a.wait_ge(gh_ps, NG * w + gr + 1 + GP0)
                            a.activation(gh[b].rearrange("p k h d -> p (k h d)")[:, gr * 512:(gr + 1) * 512],
                                         ps[GBANK[gr]][:, :], ACT.Copy).then_inc(gh_sb, 1)
                        a.wait_ge(landed, w + 1)
                        for q in range(NB):
                            a.wait_ge(merged_ps, NB * w + q + 1 + MP0)
                            a.activation(vm[b].rearrange("p t d -> p (t d)")[:, q * 512:(q + 1) * 512],
                                         ps[MBANK[(NB * b + q) % 2]][:, :], ACT.Copy).then_inc(v_sb, 1)

                    heads(0, 0, 0)
                    with a.Fori(0, PAIRS - 1) as i:
                        heads(2 * i + 1, i, 1)
                        rows(2 * i, 0)
                        heads(2 * i + 2, i + 1, 0)
                        rows(2 * i + 1, 1)
                    heads(NW - 1, PAIRS - 1, 1)
                    rows(NW - 2, 0)
                    rows(NW - 1, 1)

                @block.vector
                def _(v):
                    v.sem_inc(tgt_ok, T0)
                    v.sem_inc(scan_ok, SC0)
                    v.memset(xin[:, :, :], 0.0).then_inc(fclr, 1)
                    v.memset(tri[:, :], 1.0).then_inc(fclr, 1)
                    link = Chain(v, f_step)
                    link(v.memset(hs[1][0:D, W - 1:W], 0.0))
                    v.wait_ge(ftrash, 1)
                    link(v.tensor_copy(trash[:, :], trash_i[:, :]))
                    v.wait_ge(fx_in, 16)
                    for k in range(NC_CHUNK):
                        cs = slice(k * CT, (k + 1) * CT)
                        v.wait_ge(fo_ps, k + 1)
                        v.tensor_tensor(xtmp[:, cs, :], ps[2].rearrange("p (t d) -> p t d", d=D),
                                        linbs.unsqueeze(1).broadcast_to([P, CT, D]), ALU.add).then_inc(fo_ok, 1)
                    v.wait_ge(fo_ok, NC_CHUNK)
                    link(v.tensor_tensor(xin[:, :, :], xin[:, :, :], xtmp[:, :, :], ALU.add))
                    layer_norm(v, link, h_cur[:, :, :], xin[:, :, :], xtmp[:, :, :], stats, D, ln2)
                    v.tensor_scalar(h_cur[:, :, :], h_cur[:, :, :], 0.0, None, ALU.max).then_inc(fh_ok, 1)
                    v.wait_ge(ftri, 1)
                    v.wait_ge(hb_in, 16)
                    MS = TW + 4

                    def spread(w, b):
                        v.wait_ge(hdT_sb, NG * (w + 1) + HS0)
                        v.wait_ge(gh_ps, NG * (w - 1) + GP0)
                        v.tensor_tensor_scan(hs[b][:, :], keep[b][:, :], hdT[b][:, :], hs[1 - b][:, W - 1:W],
                                             ALU.mult, ALU.add).then_inc(scan_ok, 1)
                        v.wait_ge(scan_ok, w + 1 + SC0)

                    def targets(w, i, b):
                        link = Chain(v, m_step, w * MS)
                        v.wait_ge(ls_in[b], 96 * (i + 1))
                        for t_ in range(TW):
                            k, h = t_ // 2, t_ % 2
                            slot, q = (NB * b + t_ // TB) % 2, t_ // TB
                            if t_ % TB == 0:
                                v.wait_ge(merged_ps, NB * w + q + 1 - 2 + MP0)
                            row = srcB[b][:, h, :].rearrange("p (e k) -> p k e", k=K)[:, k, :]
                            ins = v.tensor_scalar(eqw[:, slot, t_ % TB, :], row, sf[b][:, h, k:k + 1],
                                                  wl[b][:, h, k:k + 1], ALU.is_equal, ALU.mult)
                            if t_ % TB == TB - 1:
                                ins.then_inc(eq_ok, 1)
                            link(v.scalar_tensor_tensor(out=djunk[:, :], in0=row, scalar=sf[b][:, h, k:k + 1], in1=tri[:, :],
                                                        op0=ALU.is_equal, op1=ALU.mult, accum_out=dup[:, t_:t_ + 1]))
                        v.wait_ge(landed, w + 1)
                        srcs = flat.rearrange("p k h -> p (k h)")
                        v.tensor_copy(flat[:, :, :], sf[b].rearrange("p h k -> p k h"))
                        link(v.tensor_scalar(dup[:, :], dup[:, :], 1.0, None, ALU.min))
                        link(v.tensor_scalar(move[:, :], srcs, -1.0, trash[:, 0:1], ALU.mult, ALU.add))
                        link(v.tensor_tensor(move[:, :], move[:, :], dup[:, :], ALU.mult))
                        link(v.tensor_tensor(move[:, :], move[:, :], srcs, ALU.add))
                        v.tensor_copy(tgt[b][:, :], move[:, :]).then_inc(tgt_ok, 1)

                    spread(0, 0)
                    with v.Fori(0, PAIRS - 1) as i:
                        spread(2 * i + 1, 1)
                        targets(2 * i, i, 0)
                        spread(2 * i + 2, 0)
                        targets(2 * i + 1, i, 1)
                    spread(NW - 1, 1)
                    targets(NW - 2, PAIRS - 1, 0)
                    targets(NW - 1, PAIRS - 1, 1)
                    for i in range(ACCS):
                        v.wait_ge(tab_in[i % 2], 16 * (i // 2 + 1))
                        v.tensor_tensor(xin[:, :, :], xin[:, :, :], tabs[i % 2][:, :, :], ALU.add).then_inc(tab_sum, 1)
                        v.wait_ge(tab_sum, i + 1)


_INS = ['x', 'src', 'dst', 'edge_attr_64', 'edge_weight', 'L0_gnn_encW', 'L0_gnn_encb', 'L0_gnn_eencW', 'L0_gnn_eencb',
        'L0_gnn_convW1', 'L0_gnn_convb1', 'L0_gnn_convLnG', 'L0_gnn_convLnB', 'L0_gnn_convW2', 'L0_gnn_convb2', 'L0_gnn_t',
        'L0_gnn_normG', 'L0_gnn_normB', 'L0_gnn_linW', 'L0_gnn_linb']
_OUTS = [((N, D), 'float32')]


def kernel(**inputs):
    import numpy as _np
    import concourse.bacc as _bacc
    from concourse import mybir as _mybir
    from concourse.bass_utils import run_bass_kernel_spmd as _run

    nc = _bacc.Bacc("TRN2", target_bir_lowering=False, num_devices=1)
    arrays, args = {}, []
    for name in _INS:
        a = _np.ascontiguousarray(inputs[name])
        arrays[f"in_{name}_dram"] = a
        args.append(nc.dram_tensor(f"in_{name}_dram", a.shape, _mybir.dt.from_np(a.dtype), kind="ExternalInput").ap())
    for i, (shape, dtype) in enumerate(_OUTS):
        dt = _mybir.dt.from_np(_np.dtype(dtype))
        args.append(nc.dram_tensor(f"out_{i}_dram", shape, dt, kind="ExternalOutput").ap())
    gnn(nc, *args)
    r = _run(nc, [arrays], core_ids=[0])
    got = tuple(r.results[0][f"out_{i}_dram"] for i in range(len(_OUTS)))
    return got[0]
```

```python
from contextlib import ExitStack

import concourse.bass as bass
from concourse import mybir

F32 = mybir.dt.float32
BF16 = mybir.dt.bfloat16
I32 = mybir.dt.int32
ALU = mybir.AluOpType
ACT = mybir.ActivationFunctionType
AX_X = mybir.AxisListType.X

P = 128
N, D, E, L = 5000, 64, 165000, 4
D2 = 2 * D
NT = N // 125
NPAD = P * NT
K = 12
W = P * K
NW = 54
HALF = NW * W
EPAD = 2 * HALF
GT = 4
NG = K // GT
GC = GT * P
B_REAL = E - HALF - (NW - 1) * W
B_PARTS = B_REAL // K
FLAT = EPAD // P
FLAT_REAL = E - (P - 1) * FLAT
CTILE = 108
CPART = FLAT // CTILE
TILES = P * CPART
BIG = float(2.0 ** 126)
EPS = 1e-7
LN_EPS = 1e-5
NC_CHUNK = 5
CT = NT // NC_CHUNK
MC = 10
MT = NT // MC
ACCS = 8
ZCOLS = EPAD * D // (P * NW * L)
TRASH = NPAD
assert B_PARTS * K == B_REAL and NPAD == 5120 and CPART * CTILE == FLAT and ZCOLS * P * NW * L == EPAD * D


class Chain:

    def __init__(self, eng, sem, base=0):
        self.eng, self.sem, self.base, self.n = eng, sem, base, 0

    def __call__(self, ins):
        self.n += 1
        ins.then_inc(self.sem, 1)
        self.eng.wait_ge(self.sem, self.base + self.n)


def gnn(nc, x, src, dst, edge_attr, edge_weight, encW, encb, eencW, eencb, W1, b1, lnG, lnB, W2, b2,
        t, normG, normB, linW, linb, out):
    def dram(name, shape, dt=F32):
        return nc.dram_tensor(name, shape, dt).ap()

    src_flat = dram("src_flat", [EPAD])
    wgt_flat = dram("wgt_flat", [EPAD])
    dst_tab = dram("dst_tab", [TILES + 1, CTILE])
    run_pen = dram("run_pen", [EPAD + 16], BF16)
    cnt_tab = dram("cnt_tab", [NPAD])
    h_tab = dram("h_tab", [NPAD, D])
    sums = dram("sums", [EPAD + P, D2])
    run_head = dram("run_head", [EPAD + NPAD, D])
    acc = [dram(f"acc{i}", [NPAD + P, D]) for i in range(ACCS)]
    ZROW = EPAD

    with ExitStack() as whole:
        def sb(name, shape, dt=F32, ctx=whole):
            return ctx.enter_context(nc.sbuf_tensor(name, shape, dt))[tuple([slice(None)] * len(shape))]

        def sem(name):
            return whole.enter_context(nc.semaphore(name))

        ident = sb("ident", [P, P])
        ones = sb("ones", [P, P])
        attrW = sb("attrW", [P, P])
        attrB = sb("attrB", [P, 1])
        last_idx = sb("last_idx", [P, NT], I32)
        first_idx = sb("first_idx", [P, NT], I32)
        win_hot = sb("win_hot", [P, NW])
        patch_i = sb("patch_i", [P, 2], I32)
        cpen = sb("cpen", [1, 1])
        x_acc = sb("x_acc", [P, NT, D])
        h_cur = sb("h_cur", [P, NT, D])
        W1s = sb("W1s", [D + 1, L, D2])
        W2s = sb("W2s", [D2, L, D])
        lnGs = sb("lnGs", [D2, L])
        lnBs = sb("lnBs", [D2, L])
        ln_eps = sb("ln_eps", [P, 1])
        b2s = sb("b2s", [P, L, D])
        nGs = sb("nGs", [P, L, D])
        nBs = sb("nBs", [P, L, D])
        ts = sb("ts", [P, L])
        linWs = sb("linWs", [D, D])
        linbs = sb("linbs", [P, D])
        stats = sb("stats", [P, 3, NT])
        zeros = sb("zeros", [P, ZCOLS])

        ps = [whole.enter_context(nc.psum_tensor(f"ps{i}", [P, 512], F32))[:, :] for i in range(8)]

        with ExitStack() as c:
            wflat = sb("wflat", [P, FLAT], F32, c)
            dflat_i = sb("dflat_i", [P, FLAT], I32, c)
            sflat_i = sb("sflat_i", [P, FLAT], I32, c)
            dflat = sb("dflat", [P, FLAT], F32, c)
            sflat = sb("sflat", [P, FLAT], F32, c)
            dprev = sb("dprev", [P, FLAT], F32, c)
            pen = sb("pen", [P, FLAT], BF16, c)
            padrow = sb("padrow", [1, CTILE], F32, c)
            tdiag = sb("tdiag", [P, CPART, P], F32, c)
            tlast_b = sb("tlast_b", [P, TILES], F32, c)
            junk = sb("junk", [P, TILES], F32, c)
            signs = sb("signs", [P, TILES], BF16, c)
            node_h = sb("node_h", [P, NT], F32, c)
            node_i = sb("node_i", [P, NT], I32, c)
            node = sb("node", [P, NT], F32, c)
            cnt_t = sb("cnt_t", [P, NT], F32, c)
            cnt_i = sb("cnt_i", [P, NT], I32, c)
            cnt_r = sb("cnt_r", [P, NT], F32, c)
            before = sb("before", [P, NT], F32, c)
            has = sb("has", [P, NT], F32, c)
            rows = sb("rows", [P, NT, CTILE], F32, c)
            b_first_i = sb("b_first_i", [P, 1], I32, c)
            b_first = sb("b_first", [P, 1], F32, c)
            b_cnt = sb("b_cnt", [P, 1], F32, c)
            b_last = sb("b_last", [P, 2], F32, c)
            win_i = sb("win_i", [P, NW], I32, c)
            win_f = sb("win_f", [P, NW], F32, c)
            win_le = sb("win_le", [P, NW], F32, c)
            pen_end = sb("pen_end", [1, 16], BF16, c)
            cpen_b = sb("cpen_b", [1, 1], BF16, c)
            zero = sb("zero", [P, (NT + 1) * D], F32, c)
            encWs = sb("encWs", [D, D], F32, c)
            encbs = sb("encbs", [P, D], F32, c)
            xn = sb("xn", [P, NT, D], F32, c)
            xnT = sb("xnT", [D, 2, 512], F32, c)

            cleared, pool_made, id_made = sem("cleared"), sem("pool_made"), sem("id_made")
            in_dst, in_src, in_wgt, in_par, in_x, in_enc, in_bfirst = (
                sem(f"in_{n}") for n in ("dst", "src", "wgt", "par", "x", "enc", "bfirst"))
            in_prev, tdiag_ok, in_cnt, in_cpen = (sem(n) for n in ("in_prev", "tdiag_ok", "in_cnt", "in_cpen"))
            assert TILES == 3 * 512
            out_tabs, out_dst, out_pen, out_cnt = (
                sem(f"out_{n}") for n in ("tabs", "dst", "pen", "cnt"))
            dst_f, src_f, pen_f, tlast_ps, bcnt_ok, bcnt_ps, tiles_ok, cnt_ok = (
                sem(f"has_{n}") for n in ("dstf", "srcf", "penf", "tlastps", "bcnt", "bcntps", "tiles", "cnt"))
            tlast_sb, xnT_ps, xnT_sb, enc_ps, enc_sb = (
                sem(f"has_{n}") for n in ("tlastsb", "xnTps", "xnTsb", "encps", "encsb"))
            g_cleared, norm_v, norm_a, norm_g = (sem(n) for n in ("g_cleared", "norm_v", "norm_a", "norm_g"))
            RG = 2
            in_rows = [sem(f"in_rows{i}") for i in range(RG)]
            set_step = sem("set_step")
            node_ok, signs_ok = sem("node_ok"), sem("signs_ok")
            N_CLEAR = 6
            SIGNED = range(17, NT)

            with nc.Block() as block:
                @block.sync
                def _(sp):
                    real = (P - 1) * FLAT
                    for n, (dest, flat, done, pads, count) in enumerate((
                            (dflat_i, dst, in_dst, cleared, 1), (sflat_i, src, in_src, cleared, 2),
                            (wflat, edge_weight, in_wgt, g_cleared, 2))):
                        sp.wait_ge(pads, count)
                        sp.dma_start(dest[0:P - 1, :], flat[0:real].rearrange("(p i) -> p i", i=FLAT)).then_inc(done, 16)
                        sp.dma_start(dest[P - 1:P, 0:FLAT_REAL], flat[real:E].unsqueeze(0)).then_inc(done, 16)
                        if n == 0:
                            sp.wait_ge(g_cleared, 1)
                            sp.dma_start(h_cur[0:N // NT, :, :].rearrange("p t d -> p (t d)"),
                                         x.rearrange("(p t) d -> p (t d)", t=NT)).then_inc(in_x, 16)
                    sp.dma_start(encWs[:, :], encW).then_inc(in_enc, 16)
                    sp.dma_start(encbs[:, :], encb.partition_broadcast(P)).then_inc(in_enc, 16)
                    sp.wait_ge(in_wgt, 32)
                    sp.dma_start(wgt_flat.rearrange("(p i) -> p i", i=FLAT), wflat[:, :]).then_inc(out_tabs, 16)
                    sp.wait_ge(cleared, N_CLEAR)
                    sp.wait_ge(g_cleared, 4)
                    sp.dma_start(sums[ZROW:ZROW + P, 0:D], ones[:, 0:D]).then_inc(out_tabs, 16)
                    sp.dma_start(sums[ZROW:ZROW + P, D:D2], zero[:, 0:D]).then_inc(out_tabs, 16)
                    for a in acc:
                        sp.dma_start(a.rearrange("(p t) d -> p (t d)", p=P), zero[:, :]).then_inc(out_tabs, 16)
                    sp.wait_ge(src_f, 1)
                    sp.dma_start(src_flat.rearrange("(p i) -> p i", i=FLAT), sflat[:, :]).then_inc(out_pen, 16)
                    sp.wait_ge(pen_f, 1)
                    sp.dma_start(run_pen[0:EPAD].rearrange("(p i) -> p i", i=FLAT), pen[:, :]).then_inc(out_pen, 16)
                    sp.dma_start(run_pen[EPAD:EPAD + 16].unsqueeze(0), pen_end[:, :]).then_inc(out_pen, 16)
                    sp.wait_ge(out_pen, 48)
                    sp.dma_start(cpen_b[:, :], run_pen[HALF:HALF + 1].unsqueeze(0)).then_inc(in_cpen, 16)

                    for k in range(NC_CHUNK):
                        sp.wait_ge(enc_sb, k + 1)
                        sp.dma_start(h_tab.rearrange("(p t) d -> p t d", t=NT)[:, k * CT:(k + 1) * CT, :],
                                     h_cur[:, k * CT:(k + 1) * CT, :]).then_inc(out_tabs, 16)
                    sp.wait_ge(cnt_ok, 1)
                    sp.dma_start(cnt_tab.rearrange("(p t) -> p t", t=NT), cnt_r[:, :]).then_inc(out_cnt, 16)
                    sp.wait_ge(out_cnt, 16)
                    sp.dma_start(before[0:1, 1:NT], cnt_tab[0:NT - 1].unsqueeze(0)).then_inc(in_cnt, 16)
                    sp.dma_start(before[1:P, :], cnt_tab[NT - 1:NT - 1 + (P - 1) * NT]
                                .rearrange("(p t) -> p t", t=NT)).then_inc(in_cnt, 16)
                    sp.wait_ge(out_tabs, 16 * (1 + 2 + ACCS + NC_CHUNK))

                @block.gpsimd
                def _(g):
                    g.iota(node_i[:, :], [[1, NT]], 0, NT).then_inc(pool_made, 1)
                    g.iota(win_i[:, :], [[W, NW]], HALF, 0).then_inc(pool_made, 1)
                    g.dma_start(b_first_i[:, :], dst[HALF:HALF + 1].partition_broadcast(P)).then_inc(in_bfirst, 16)
                    g.memset(h_cur[:, :, :], 0.0).then_inc(g_cleared, 1)
                    g.memset(wflat[:, :], 0.0).then_inc(g_cleared, 1)
                    g.wait_ge(cleared, 3)
                    g.affine_select(out=ident[:, :], in_=ident[:, :], compare_op=ALU.not_equal, fill=1.0, base=0,
                                    pattern=[[-1, P]], channel_multiplier=1).then_inc(id_made, 1)

                    dst_flat = dst_tab.rearrange("a b -> (a b)")
                    g.memset(dprev[:, :], -1.0).then_inc(g_cleared, 1)
                    g.memset(zero[:, :], 0.0).then_inc(g_cleared, 1)
                    g.wait_ge(g_cleared, 3)
                    g.wait_ge(dst_f, 1)
                    g.dma_start(dst_flat[0:EPAD].rearrange("(p i) -> p i", i=FLAT), dflat[:, :]).then_inc(out_dst, 16)
                    g.dma_start(dst_tab[TILES:TILES + 1, :], padrow[:, :]).then_inc(out_dst, 16)
                    g.wait_ge(out_dst, 32)
                    g.dma_start(dprev[0:1, 1:FLAT], dst_flat[0:FLAT - 1].unsqueeze(0)).then_inc(in_prev, 16)
                    g.dma_start(dprev[1:P, :], dst_flat[FLAT - 1:FLAT - 1 + (P - 1) * FLAT]
                                .rearrange("(p i) -> p i", i=FLAT)).then_inc(in_prev, 16)
                    g.wait_ge(norm_v, 1)
                    per_node = [P, NT, D]
                    g.tensor_tensor(xn[:, :, :], h_cur[:, :, :], stats[:, 0, :].unsqueeze(2).broadcast_to(per_node),
                                    ALU.subtract).then_inc(norm_g, 1)
                    g.wait_ge(norm_v, 3)
                    g.wait_ge(norm_a, 1)
                    g.tensor_tensor(xn[:, :, :], xn[:, :, :], stats[:, 2, :].unsqueeze(2).broadcast_to(per_node),
                                    ALU.mult).then_inc(norm_g, 1)
                    g.wait_ge(tiles_ok, 1)
                    for t in range(NT):
                        g.indirect_dma_start(rows[:, t, :], None, dst_tab[:, :], bass.IndirectOffsetOnAxis(
                            ap=cnt_i[:, t:t + 1], axis=0)).then_inc(in_rows[t * RG // NT], 16)

                @block.scalar
                def _(a):
                    a.wait_ge(cleared, N_CLEAR)
                    a.dma_start(attrW[0:D, 0:D], eencW).then_inc(in_par, 16)
                    a.dma_start(attrW[D:D2, D:D2], eencW).then_inc(in_par, 16)
                    with nc.allow_non_contiguous_dma("columns of parameters, once"):
                        a.dma_start(attrB[0:D, :], eencb.unsqueeze(1)).then_inc(in_par, 16)
                        a.dma_start(attrB[D:D2, :], eencb.unsqueeze(1)).then_inc(in_par, 16)
                        a.dma_start(lnGs[:, :], lnG.rearrange("l d -> d l")).then_inc(in_par, 16)
                        a.dma_start(lnBs[:, :], lnB.rearrange("l d -> d l")).then_inc(in_par, 16)
                    a.dma_start(W1s[0:D, :, :], W1.rearrange("l k m -> k l m")).then_inc(in_par, 16)
                    a.dma_start(W1s[D:D + 1, :, :], b1.unsqueeze(0)).then_inc(in_par, 16)
                    a.dma_start(W2s[:, :, :], W2.rearrange("l k m -> k l m")).then_inc(in_par, 16)
                    a.dma_start(b2s.rearrange("p l d -> p (l d)"),
                                b2.rearrange("l d -> (l d)").partition_broadcast(P)).then_inc(in_par, 16)
                    for dest, v in ((nGs, normG), (nBs, normB)):
                        a.dma_start(dest[:, 0:L - 1, :].rearrange("p l d -> p (l d)"),
                                    v[1:L, :].rearrange("l d -> (l d)").partition_broadcast(P)).then_inc(in_par, 16)
                        a.dma_start(dest[:, L - 1, :], v[0, :].partition_broadcast(P)).then_inc(in_par, 16)
                    a.dma_start(ts[:, :], t.partition_broadcast(P)).then_inc(in_par, 16)
                    a.dma_start(linWs[:, :], linW).then_inc(in_par, 16)
                    a.dma_start(linbs[:, :], linb.partition_broadcast(P)).then_inc(in_par, 16)
                    a.wait_ge(node_ok, 1)
                    a.wait_ge(tlast_sb, 3)
                    for n in SIGNED:
                        a.activation(signs[:, :], tlast_b[:, :], ACT.Sign, bias=node_h[:, n:n + 1], scale=-1.0,
                                     accum_out=cnt_t[:, n:n + 1]).then_inc(signs_ok, 1)
                        a.wait_ge(signs_ok, n - SIGNED[0] + 1)
                        if n == SIGNED[7]:
                            a.wait_ge(norm_g, 1)
                            a.activation(x_acc[:, :, :], xn[:, :, :], ACT.Square).then_inc(norm_a, 1)
                        if n == SIGNED[14]:
                            a.wait_ge(norm_v, 2)
                            a.activation(stats[:, 1, :], stats[:, 1, :], ACT.Sqrt).then_inc(norm_a, 1)
                    for k in range(NC_CHUNK):
                        for half in range(2):
                            a.wait_ge(xnT_ps, 2 * k + half + 1)
                            if k and not half:
                                a.wait_ge(enc_ps, k)
                            a.activation(xnT[:, half, :], ps[4 + half][0:D, :], ACT.Relu).then_inc(xnT_sb, 1)
                    a.wait_ge(in_par, 16 * 17)

                @block.tensor
                def _(pe):
                    pe.wait_ge(cleared, N_CLEAR)
                    pe.wait_ge(id_made, 1)
                    pe.wait_ge(tdiag_ok, 1)
                    for i in range(3):
                        pe.matmul(ps[1 + i][:, :], ones[:, :],
                                  tdiag.rearrange("p j q -> p (j q)")[:, i * 512:(i + 1) * 512],
                                  start=True, stop=True).then_inc(tlast_ps, 1)
                    pe.wait_ge(norm_g, 2)
                    pe.wait_ge(in_enc, 32)
                    for k in range(NC_CHUNK):
                        if k:
                            pe.wait_ge(xnT_sb, 2 * k)
                        for i in range(CT):
                            ins = pe.transpose(ps[4 + i // GT][0:D, i % GT * P:(i % GT + 1) * P], xn[:, k * CT + i, :],
                                               ident[:, :])
                            if i % GT == GT - 1:
                                ins.then_inc(xnT_ps, 1)
                        pe.wait_ge(xnT_sb, 2 * k + 2)
                        if k:
                            pe.wait_ge(enc_sb, k)
                        for i in range(CT):
                            ins = pe.matmul(ps[6][:, i * D:(i + 1) * D], xnT[:, i // GT, i % GT * P:(i % GT + 1) * P],
                                            encWs[:, :], start=True, stop=True)
                        ins.then_inc(enc_ps, 1)
                    pe.wait_ge(bcnt_ok, 1)
                    pe.matmul(ps[0][:, 0:1], ones[:, :], b_cnt[:, :], start=True, stop=True).then_inc(bcnt_ps, 1)

                @block.vector
                def _(v):
                    for buf, value in ((dflat_i[:, :], 8191), (sflat_i[:, :], 0), (ident[:, :], 0.0),
                                       (ones[:, :], 1.0), (attrW[:, :], 0.0), (zeros[:, :], 0.0)):
                        v.memset(buf, value).then_inc(cleared, 1)
                    link = Chain(v, set_step)
                    v.memset(padrow[:, :], 8191.0)
                    v.memset(before[:, :], 0.0)
                    link(v.memset(pen_end[:, :], -BIG))
                    v.wait_ge(in_dst, 32)
                    v.wait_ge(cleared, N_CLEAR)
                    v.tensor_copy(dflat[:, :], dflat_i[:, :]).then_inc(dst_f, 1)
                    v.wait_ge(dst_f, 1)
                    v.wait_ge(id_made, 1)
                    ends = dflat.rearrange("p (j e) -> p j e", e=CTILE)[:, :, CTILE - 1:CTILE]
                    v.tensor_tensor(tdiag[:, :, :], ends.broadcast_to([P, CPART, P]),
                                    ident.unsqueeze(1).broadcast_to([P, CPART, P]), ALU.mult).then_inc(tdiag_ok, 1)
                    for i in range(3):
                        v.wait_ge(tlast_ps, i + 1)
                        v.tensor_copy(tlast_b[:, i * 512:(i + 1) * 512], ps[1 + i][:, :]).then_inc(tlast_sb, 1)
                    v.wait_ge(pool_made, 2)
                    v.tensor_copy(node[:, :], node_i[:, :])
                    link(v.tensor_copy(win_f[:, :], win_i[:, :]))
                    v.tensor_scalar(node_h[:, :], node[:, :], 0.5, None, ALU.add).then_inc(node_ok, 1)
                    v.wait_ge(tlast_sb, 3)
                    for n in range(SIGNED[0]):
                        link(v.tensor_scalar(junk[:, :], tlast_b[:, :], node[:, n:n + 1], None, ALU.is_le, ALU.add,
                                             accum_out=cnt_t[:, n:n + 1]))
                        if n == 0:
                            v.wait_ge(in_x, 16)
                            link(v.tensor_reduce(stats[:, 0, :], h_cur[:, :, :], AX_X, ALU.add))
                            v.tensor_scalar(stats[:, 0, :], stats[:, 0, :], 1.0 / D, None, ALU.mult).then_inc(norm_v, 1)
                        if n == 7:
                            v.wait_ge(norm_a, 1)
                            link(v.tensor_reduce(stats[:, 1, :], x_acc[:, :, :], AX_X, ALU.add))
                            v.tensor_scalar(stats[:, 1, :], stats[:, 1, :], 1.0 / D, LN_EPS, ALU.mult, ALU.add
                                            ).then_inc(norm_v, 1)
                        if n == 12:
                            v.wait_ge(norm_a, 2)
                            v.reciprocal(stats[:, 2, :], stats[:, 1, :]).then_inc(norm_v, 1)
                    v.wait_ge(signs_ok, len(SIGNED))
                    signed = cnt_t[:, SIGNED[0]:NT]
                    link(v.tensor_scalar(signed, signed, 0.5, 0.5 * TILES, ALU.mult, ALU.add))
                    v.tensor_copy(cnt_i[:, :], cnt_t[:, :]).then_inc(tiles_ok, 1)

                    v.wait_ge(in_bfirst, 16)
                    link(v.tensor_copy(b_first[:, :], b_first_i[:, :]))
                    v.tensor_scalar(junk[:, 0:FLAT], dflat[:, :], b_first[:, 0:1], None, ALU.is_le, ALU.add,
                                    accum_out=b_cnt[:, :]).then_inc(bcnt_ok, 1)
                    v.wait_ge(in_src, 32)
                    v.tensor_copy(sflat[:, :], sflat_i[:, :]).then_inc(src_f, 1)
                    v.wait_ge(in_prev, 32)
                    v.wait_ge(bcnt_ok, 1)
                    link(v.tensor_tensor(junk[:, 0:FLAT], dflat[:, :], dprev[:, :], ALU.is_equal))
                    v.tensor_scalar(pen[:, :], junk[:, 0:FLAT], -0.5, 2.0 * BIG, ALU.add, ALU.mult).then_inc(pen_f, 1)
                    v.wait_ge(pen_f, 1)

                    for k in range(NC_CHUNK):
                        v.wait_ge(enc_ps, k + 1)
                        v.tensor_tensor(h_cur[:, k * CT:(k + 1) * CT, :], ps[6].rearrange("p (t d) -> p t d", d=D),
                                        encbs.unsqueeze(1).broadcast_to([P, CT, D]), ALU.add).then_inc(enc_sb, 1)
                    v.wait_ge(enc_sb, NC_CHUNK)

                    v.wait_ge(bcnt_ps, 1)
                    v.tensor_scalar(b_last[:, 0:1], ps[0][:, 0:1], -1.0, None, ALU.add)
                    link(v.tensor_scalar(b_last[:, 1:2], ps[0][:, 0:1], -1.0 - W, None, ALU.add))
                    v.tensor_copy(patch_i[:, 0:1], b_last[:, 0:1])
                    v.tensor_copy(patch_i[:, 1:2], b_first[:, 0:1])
                    v.tensor_scalar(win_le[:, :], win_f[:, :], b_last[:, 0:1], None, ALU.is_le)
                    link(v.tensor_scalar(win_hot[:, :], win_f[:, :], b_last[:, 1:2], None, ALU.is_gt))
                    link(v.tensor_tensor(win_hot[:, :], win_hot[:, :], win_le[:, :], ALU.mult))
                    v.wait_ge(in_cpen, 16)
                    link(v.tensor_copy(cpen[:, :], cpen_b[:, :]))

                    for n in range(NT):
                        if n % (NT // RG) == 0:
                            v.wait_ge(in_rows[n * RG // NT], 16 * NT // RG)
                        link(v.tensor_scalar(junk[:, 0:CTILE], rows[:, n, :], node[:, n:n + 1], None, ALU.is_le, ALU.add,
                                             accum_out=cnt_r[:, n:n + 1]))
                    v.scalar_tensor_tensor(out=cnt_r[:, :], in0=cnt_t[:, :], scalar=float(CTILE), in1=cnt_r[:, :],
                                           op0=ALU.mult, op1=ALU.add).then_inc(cnt_ok, 1)
                    v.wait_ge(cnt_ok, 1)
                    v.wait_ge(in_cnt, 32)
                    link(v.tensor_tensor(has[:, :], cnt_r[:, :], before[:, :], ALU.is_gt))
                    link(v.tensor_tensor(before[:, :], before[:, :], node[:, :], ALU.subtract))
                    link(v.scalar_tensor_tensor(out=before[:, :], in0=before[:, :], scalar=-float(EPAD), in1=has[:, :],
                                                op0=ALU.add, op1=ALU.mult))
                    link(v.scalar_tensor_tensor(out=before[:, :], in0=before[:, :], scalar=float(EPAD), in1=node[:, :],
                                                op0=ALU.add, op1=ALU.add))
                    link(v.tensor_copy(first_idx[:, :], before[:, :]))
                    link(v.scalar_tensor_tensor(out=cnt_t[:, :], in0=cnt_r[:, :], scalar=-1.0 - ZROW, in1=has[:, :],
                                                op0=ALU.add, op1=ALU.mult))
                    link(v.tensor_scalar(cnt_t[:, :], cnt_t[:, :], float(ZROW), None, ALU.add))
                    link(v.tensor_copy(last_idx[:, :], cnt_t[:, :]))

        with ExitStack() as c:
            xg = [sb(f"xg{i}", [P, K, 2, D], F32, c) for i in range(2)]
            ea = [sb(f"ea{i}", [P, 2, K, D], F32, c) for i in range(2)]
            at = sb("at", [P, NG, GC], F32, c)
            idx = [sb(f"idx{i}", [P, 2, K], I32, c) for i in range(2)]
            rp = [sb(f"rp{i}", [P, W + 1], BF16, c) for i in range(2)]
            keep = [sb(f"keep{i}", [P, W], BF16, c) for i in range(2)]
            u = [sb(f"u{i}", [P, W], F32, c) for i in range(2)]
            lg = [sb(f"lg{i}", [P, W], F32, c) for i in range(2)]
            runmax = sb("runmax", [P, W], F32, c)
            segmax = sb("segmax", [P, W], F32, c)
            ex = sb("ex", [P, W + 1], F32, c)
            uex = sb("uex", [P, W], F32, c)
            den = [sb(f"den{i}", [P, W], F32, c) for i in range(2)]
            num = [sb(f"num{i}", [P, W], F32, c) for i in range(2)]
            st_all = sb("st_all", [P, 2, 2, K, D2], F32, c)
            st = [st_all[:, i, :, :, :] for i in range(2)]
            carry = sb("carry", [P, 4], F32, c)
            start2 = sb("start2", [P, 2], F32, c)
            wmax = sb("wmax", [P, NW], F32, c)
            wjunk = sb("wjunk", [P, NW], F32, c)
            wmean = sb("wmean", [P, 3, L], F32, c)
            tcur = sb("tcur", [P, 2], F32, c)
            ncur = sb("ncur", [P, 2, D], F32, c)
            lncur = sb("lncur", [D2, 2], F32, c)
            W1c = sb("W1c", [D + 1, D2], F32, c)
            W2c = sb("W2c", [D2, D], F32, c)
            prow = sb("prow", [1, 4, D2], F32, c)
            pdiff = sb("pdiff", [1, 2, D], F32, c)
            pmax = sb("pmax", [1, D], F32, c)
            pold = sb("pold", [1, 2, D], F32, c)
            pnew = sb("pnew", [1, 2, D], F32, c)
            ptmp = sb("ptmp", [1, 2, D], F32, c)
            dn = st_all.rearrange("p b h k c -> p (b h k) c")[:, 0:NT, :]
            rec = sb("rec", [P, MT, D], F32, c)
            hin = sb("hin", [P, MT, D], F32, c)
            hinT = sb("hinT", [D + 1, MT * P], F32, c)
            y = sb("y", [P, MT, D2], F32, c)
            sqjunk = sb("sqjunk", [P, MT, D2], BF16, c)
            yroot = sb("yroot", [P, 2, MT], F32, c)
            xroot = sb("xroot", [P, 2, MT], F32, c)
            yinv = sb("yinv", [P, MT], F32, c)
            xinv = sb("xinv", [P, MT], F32, c)
            zT = sb("zT", [D2, MT * P], F32, c)

            xg_in = [[sem(f"xg_in{i}_{gr}") for gr in range(NG)] for i in range(2)]
            ea_in, idx_in, rp_in, st_out = (
                [sem(f"{n}{i}") for i in range(2)] for n in ("ea_in", "idx_in", "rp_in", "st_out"))
            z_ps, u_ok, l_ok, diff_ok, ex_ok, max_ok, sums_ok, back_ps, back_sb = (
                sem(n) for n in ("z_ps", "u_ok", "l_ok", "diff_ok", "ex_ok", "max_ok", "sums_ok", "back_ps", "back_sb"))
            dve_step, node_step, centre_step, den_ok, tcur_ok, gather_go = (
                sem(n) for n in ("dve_step", "node_step", "centre_step", "den_ok", "tcur_ok", "gather_go"))
            carry_ok, prow_ps, pold_in, pdiff_ok, pexp_ok, pnew_ok, patched = (
                sem(n) for n in ("carry_ok", "prow_ps", "pold_in", "pdiff_ok", "pexp_ok", "pnew_ok", "patched"))
            dn_in = [sem(f"dn_in{i}") for i in range(MC)]
            hin_ok, hinT_ps, hinT_sb, y_ps, ysum_ok, yroot_ok, y_ok, yT_ps, zT_sb, o_ps = (
                sem(n) for n in ("hin_ok", "hinT_ps", "hinT_sb", "y_ps", "ysum_ok", "yroot_ok", "y_ok", "yT_ps", "zT_sb",
                                 "o_ps"))
            x_ok, xsum_ok, xroot_ok, hn_ok, ha_ok, gain_ok, h_ok, tab_out = (
                sem(n) for n in ("x_ok", "xsum_ok", "xroot_ok", "hn_ok", "ha_ok", "gain_ok", "h_ok", "tab_out"))
            at_ps, at_sb, heads_zero, load_go = sem("at_ps"), sem("at_sb"), sem("heads_zero"), sem("load_go")
            BU = 2 * NG
            Z0, U0, L0, M0, S0, BP0, BS0, A0 = 2 * NG, NG, 2, 2, 2, 2 * BU, 3, 2
            PAIRS = NW // 2

            with nc.Block() as block:
                @block.sync
                def _(sp):
                    last = sp.value_load(patch_i[0:1, 0:1], min_val=HALF, max_val=EPAD - 1)

                    def load(g, w, b, parts=P):
                        sp.wait_ge(z_ps, NG * g + NG - NG * 2 + Z0)
                        for h in range(2):
                            n = parts if h else P
                            piece = bass.ds(h * HALF + w * W, n * K)
                            sp.dma_start(idx[b][0:n, h, :], src[piece].rearrange("(p k) -> p k", k=K)).then_inc(idx_in[b], 16)
                            sp.dma_start(ea[b][0:n, h, :, :], edge_attr[piece, :].rearrange("(p k) f -> p k f", k=K)
                                         ).then_inc(ea_in[b], 16)
                        sp.wait_ge(max_ok, g + 1)
                        sp.wait_ge(l_ok, g + 1)
                        sp.sem_inc(load_go, 1)
                        for h in range(2):
                            sp.dma_start(rp[b][h * D:(h + 1) * D, :], run_pen[bass.ds(h * HALF + w * W, W + 1)]
                                         .partition_broadcast(D)).then_inc(rp_in[b], 16)

                    sums_v = sums[0:EPAD, :].rearrange("(h w p k) c -> h w p (k c)", h=2, w=NW, p=P)

                    def store(g, w, b):
                        sp.wait_ge(back_sb, BU * (g + 1) + BS0)
                        for h in range(2):
                            sp.dma_start(sums_v[h, w], st[b][:, h, :, :].rearrange("p k c -> p (k c)")
                                         ).then_inc(st_out[b], 16)

                    head_pieces = run_head[0:EPAD, :].rearrange("(g p i) d -> g p (i d)", g=L * NW, p=P)

                    def clear(g):
                        sp.dma_start(head_pieces[g], zeros[:, :]).then_inc(heads_zero, 16)

                    def store_nodes(k):
                        sp.dma_start(h_tab.rearrange("(p t) d -> p t d", t=NT)[:, k * MT:(k + 1) * MT, :],
                                     h_cur[:, k * MT:(k + 1) * MT, :]).then_inc(tab_out, 16)

                    sp.sem_inc(tab_out, 16)
                    load(0, 0, 0)
                    load(1, 1, 1)
                    with sp.Fori(0, L) as l:
                        with sp.Fori(0, PAIRS - 2) as i:
                            for b in range(2):
                                load(l * NW + 2 * i + 2 + b, 2 * i + 2 + b, b)
                                store(l * NW + 2 * i + b, 2 * i + b, b)
                                clear(l * NW + 2 * i + b)
                        for b in range(2):
                            load(l * NW + NW - 2 + b, NW - 2 + b, b, B_PARTS if b else P)
                            store(l * NW + NW - 4 + b, NW - 4 + b, b)
                            clear(l * NW + NW - 4 + b)
                        for b in range(2):
                            store(l * NW + NW - 2 + b, NW - 2 + b, b)
                            clear(l * NW + NW - 2 + b)
                        for b in range(2):
                            sp.wait_ge(st_out[b], 32 * PAIRS * (l + 1) + 32)
                        sp.dma_start(pold.rearrange("p a d -> p (a d)"), sums[bass.ds(last, 1), :]).then_inc(pold_in, 16)
                        for b in range(2):
                            load((l + 1) * NW + b, b, b)
                        sp.wait_ge(pnew_ok, l + 1)
                        sp.dma_start(sums[bass.ds(last, 1), :], pnew.rearrange("p a d -> p (a d)")).then_inc(patched, 16)
                        for k in range(MC):
                            sp.wait_ge(h_ok, MC * l + k + 1)
                            store_nodes(k)
                    sp.wait_ge(tab_out, 16 * MC * L + 16)
                    sp.wait_ge(heads_zero, 16 * L * NW)
                    for b in range(2):
                        sp.wait_ge(idx_in[b], 32 * (PAIRS * L + 1))
                        sp.wait_ge(ea_in[b], 32 * (PAIRS * L + 1))
                        sp.wait_ge(rp_in[b], 32 * (PAIRS * L + 1))

                @block.gpsimd
                def _(g_):
                    def window(g, i, l, b):
                        g_.wait_ge(idx_in[b], 32 * (l * PAIRS + i + 1))
                        g_.sem_inc(gather_go, 1)
                        for k in range(K):
                            if k % GT == 0:
                                g_.wait_ge(z_ps, NG * g + k // GT + 1 - NG * 2 + Z0)
                                g_.sem_inc(gather_go, 1)
                            for h in range(2):
                                g_.indirect_dma_start(xg[b][:, k, h, :], None, h_tab[:, :], bass.IndirectOffsetOnAxis(
                                    ap=idx[b][:, h, k:k + 1], axis=0)).then_inc(xg_in[b][k // GT], 16)

                    g_.sem_inc(ha_ok, 1)
                    with g_.Fori(0, L) as l:
                        g_.wait_ge(tab_out, 16 * MC * l + 16)
                        g_.sem_inc(gather_go, 1)
                        with g_.Fori(0, PAIRS) as i:
                            for b in range(2):
                                window(l * NW + 2 * i + b, i, l, b)
                        g_.wait_ge(patched, 16 * (l + 1))
                        g_.sem_inc(gather_go, 1)
                        for t_ in range(NT):
                            g_.indirect_dma_start(dn[:, t_, :], None, sums[:, :], bass.IndirectOffsetOnAxis(
                                ap=last_idx[:, t_:t_ + 1], axis=0)).then_inc(dn_in[t_ // MT], 16)
                        for k in range(MC):
                            cs = slice(k * MT, (k + 1) * MT)
                            g_.wait_ge(hn_ok, MC * l + k + 1)
                            g_.sem_inc(gather_go, 1)
                            g_.tensor_tensor(h_cur[:, cs, :], h_cur[:, cs, :],
                                             ncur[:, 0:1, :].broadcast_to([P, MT, D]), ALU.mult
                                             ).then_inc(gain_ok, 1)
                            g_.wait_ge(gain_ok, MC * l + k + 1)
                            g_.sem_inc(gather_go, 1)
                            g_.tensor_tensor(h_cur[:, cs, :], h_cur[:, cs, :],
                                             ncur[:, 1:2, :].broadcast_to([P, MT, D]), ALU.add
                                             ).then_inc(ha_ok, 1)

                @block.tensor
                def _(pe):
                    pe.sem_inc(z_ps, Z0)
                    pe.sem_inc(back_ps, BP0)

                    def forward(g, i, l, b):
                        pe.wait_ge(ea_in[b], 32 * (l * PAIRS + i + 1))
                        for gr in range(NG):
                            pe.wait_ge(at_sb, NG * g + gr + 1 - 2 + A0)
                            for j in range(GT):
                                for h in range(2):
                                    ins = pe.matmul(ps[6 + (NG * b + gr) % 2][h * D:(h + 1) * D, j * P:(j + 1) * P],
                                                    ea[b][:, h, gr * GT + j, :], ident[:, :], start=True, stop=True)
                            ins.then_inc(at_ps, 1)
                        for gr in range(NG):
                            pe.wait_ge(u_ok, NG * g + gr + 1 - NG + U0)
                            pe.wait_ge(at_sb, NG * g + gr + 1 + A0)
                            pe.matmul(ps[gr][:, :], attrW[:, :], at[:, gr, :], start=True, stop=True)
                            pe.wait_ge(xg_in[b][gr], 32 * GT * (l * PAIRS + i + 1))
                            for j in range(GT):
                                ins = pe.matmul(ps[gr][:, j * P:(j + 1) * P],
                                                xg[b][:, gr * GT + j, :, :].rearrange("p h d -> p (h d)"), ident[:, :],
                                                start=False, stop=True, skip_group_check=True)
                            ins.then_inc(z_ps, 1)

                    def back(g, b):
                        for r in range(BU):
                            gr, s_ = r % NG, r // NG
                            if r == 0:
                                pe.wait_ge(den_ok, g + 1)
                            if r == NG:
                                pe.wait_ge(sums_ok, g + 1 + S0)
                            pe.wait_ge(back_sb, BU * g + r + 1 - 3 + BS0)
                            sum_v = (den, num)[s_][b].rearrange("c (p k) -> c k p", k=K)
                            for j in range(GT):
                                ins = pe.transpose(ps[3 + r % 3][:, j * P:(j + 1) * P], sum_v[:, gr * GT + j, :],
                                                   ident[:, :])
                            ins.then_inc(back_ps, 1)

                    with pe.Fori(0, L) as l:
                        g0 = l * NW
                        forward(g0, 0, l, 0)
                        with pe.Fori(0, PAIRS - 1) as i:
                            forward(g0 + 2 * i + 1, i, l, 1)
                            back(g0 + 2 * i, 0)
                            forward(g0 + 2 * i + 2, i + 1, l, 0)
                            back(g0 + 2 * i + 1, 1)
                        forward(g0 + NW - 1, PAIRS - 1, l, 1)
                        back(g0 + NW - 2, 0)
                        back(g0 + NW - 1, 1)

                        pe.wait_ge(carry_ok, l + 1)
                        pe.wait_ge(back_sb, BU * (g0 + NW) + BS0)
                        for j in range(4):
                            ins = pe.matmul(ps[3][0:1, j * P:(j + 1) * P], carry[:, j:j + 1], ident[:, :],
                                            start=True, stop=True)
                        ins.then_inc(prow_ps, 1)
                        pe.wait_ge(u_ok, NG * (g0 + NW) + U0)
                        base = MC * l
                        for k in range(MC + 1):
                            if k < MC:
                                pe.wait_ge(hin_ok, base + k + 1)
                                for j in range(MT):
                                    dest = ps[0][0:D, j * P:(j + 1) * P]
                                    pe.matmul(dest, h_cur[:, k * MT + j, :], ident[:, :], start=True, stop=False)
                                    ins = pe.matmul(dest, hin[:, j, :], ident[:, :], start=False, stop=True)
                                ins.then_inc(hinT_ps, 1)
                            if k:
                                pe.wait_ge(y_ok, base + k)
                                for j in range(MT):
                                    ins = pe.transpose(ps[3][:, j * P:(j + 1) * P], y[:, j, :], ident[:, :])
                                ins.then_inc(yT_ps, 1)
                            if k < MC:
                                pe.wait_ge(hinT_sb, base + k + 1)
                                for j in range(MT):
                                    ins = pe.matmul(ps[6 + k % 2][:, j * P:(j + 1) * P],
                                                    hinT[:, j * P:(j + 1) * P], W1c[:, :], start=True, stop=True)
                                ins.then_inc(y_ps, 1)
                            if k:
                                pe.wait_ge(zT_sb, base + k)
                                if k > 1:
                                    pe.wait_ge(x_ok, base + k - 1)
                                for j in range(MT):
                                    ins = pe.matmul(ps[2][:, j * D:(j + 1) * D], zT[:, j * P:(j + 1) * P], W2c[:, :],
                                                    start=True, stop=True)
                                ins.then_inc(o_ps, 1)

                @block.scalar
                def _(a):
                    a.sem_inc(u_ok, U0)
                    a.sem_inc(at_sb, A0)
                    a.sem_inc(l_ok, L0)
                    a.sem_inc(back_sb, BS0)
                    for b in range(2):
                        a.sem_inc(st_out[b], 32)

                    def logits(g, i, l, b):
                        for gr in range(NG):
                            a.wait_ge(z_ps, NG * (g - 1) + gr + 1 + Z0)
                            a.wait_ge(at_ps, NG * g + gr + 1)
                            a.activation(at[:, gr, :], ps[6 + (NG * b + gr) % 2][:, :], ACT.Copy).then_inc(at_sb, 1)
                        a.wait_ge(sums_ok, g + 1 - 2 + S0)
                        a.wait_ge(rp_in[b], 32 * (l * PAIRS + i + 1))
                        a.activation(keep[b][:, :], rp[b][:, 0:W], ACT.Relu, scale=1.0 / BIG)
                        for gr in range(NG):
                            a.wait_ge(z_ps, NG * g + gr + 1 + Z0)
                            a.activation(u[b].rearrange("c (p k) -> c k p", k=K)[:, gr * GT:(gr + 1) * GT, :],
                                         ps[gr].rearrange("c (k p) -> c k p", p=P), ACT.Relu, bias=attrB[:, 0:1]
                                         ).then_inc(u_ok, 1)
                        a.wait_ge(u_ok, NG * (g + 1) + U0)
                        a.activation(lg[b][:, :], u[b][:, :], ACT.Identity, bias=tcur[:, 1:2], scale=tcur[:, 0:1]
                                     ).then_inc(l_ok, 1)

                    def empty(g, i, l, b):
                        a.wait_ge(st_out[b], 32 * (l * PAIRS + i) + 32)
                        for r in range(BU):
                            gr, s_ = r % NG, r // NG
                            a.wait_ge(back_ps, BU * g + r + 1 + BP0)
                            a.activation(st[b].rearrange("p h k c -> p k h c")[:, gr * GT:(gr + 1) * GT, :,
                                                                               s_ * D:(s_ + 1) * D],
                                         ps[3 + r % 3].rearrange("p (k h c) -> p k h c", k=GT, h=2), ACT.Copy
                                         ).then_inc(back_sb, 1)

                    def exponentials(g):
                        a.wait_ge(diff_ok, g + 1)
                        a.activation(ex[:, :], ex[:, :], ACT.Exp, scale=-1.0).then_inc(ex_ok, 1)

                    with a.Fori(0, L) as l:
                        g0 = l * NW
                        a.wait_ge(tcur_ok, l + 1)
                        logits(g0, 0, l, 0)
                        exponentials(g0)
                        with a.Fori(0, PAIRS - 1) as i:
                            logits(g0 + 2 * i + 1, i, l, 1)
                            empty(g0 + 2 * i, i, l, 0)
                            exponentials(g0 + 2 * i + 1)
                            logits(g0 + 2 * i + 2, i + 1, l, 0)
                            empty(g0 + 2 * i + 1, i, l, 1)
                            exponentials(g0 + 2 * i + 2)
                        logits(g0 + NW - 1, PAIRS - 1, l, 1)
                        empty(g0 + NW - 2, PAIRS - 1, l, 0)
                        exponentials(g0 + NW - 1)
                        empty(g0 + NW - 1, PAIRS - 1, l, 1)

                        a.wait_ge(pdiff_ok, l + 1)
                        a.activation(pdiff[:, :, :], pdiff[:, :, :], ACT.Exp, scale=-1.0).then_inc(pexp_ok, 1)
                        base = MC * l
                        for k in range(MC + 3):
                            if k < MC:
                                a.wait_ge(hinT_ps, base + k + 1)
                                a.activation(hinT[0:D, :], ps[0][0:D, :], ACT.Copy).then_inc(hinT_sb, 1)
                            if 0 < k <= MC:
                                a.wait_ge(yT_ps, base + k)
                                if k > 1:
                                    a.wait_ge(o_ps, base + k - 1)
                                a.activation(zT[:, :], ps[3][:, :], ACT.Relu, scale=lncur[:, 0:1], bias=lncur[:, 1:2]
                                             ).then_inc(zT_sb, 1)
                            if k < MC:
                                a.wait_ge(y_ps, base + k + 1)
                                for j in range(MT):
                                    ins = a.activation(sqjunk[:, j, :], ps[6 + k % 2][:, j * P:(j + 1) * P], ACT.Square,
                                                       accum_out=yroot[:, k % 2, j:j + 1])
                                ins.then_inc(ysum_ok, 1)
                                a.wait_ge(ysum_ok, base + k + 1)
                                a.activation(yroot[:, k % 2, :], yroot[:, k % 2, :], ACT.Sqrt, scale=1.0 / D2, bias=ln_eps[:, 0:1]
                                             ).then_inc(yroot_ok, 1)
                            if 1 < k < MC + 2:
                                a.wait_ge(x_ok, base + k - 1)
                                for j in range(MT):
                                    ins = a.activation(sqjunk[:, j, 0:D], x_acc[:, (k - 2) * MT + j, :], ACT.Square,
                                                       accum_out=xroot[:, k % 2, j:j + 1])
                                ins.then_inc(xsum_ok, 1)
                                a.wait_ge(xsum_ok, base + k - 1)
                                a.activation(xroot[:, k % 2, :], xroot[:, k % 2, :], ACT.Sqrt, scale=1.0 / D, bias=ln_eps[:, 0:1]
                                             ).then_inc(xroot_ok, 1)
                            if k > 2:
                                cs = slice((k - 3) * MT, (k - 2) * MT)
                                a.wait_ge(ha_ok, base + k - 2 + 1)
                                a.activation(h_cur[:, cs, :], h_cur[:, cs, :], ACT.Relu).then_inc(h_ok, 1)

                @block.vector
                def _(v):
                    v.sem_inc(max_ok, M0)
                    v.sem_inc(sums_ok, S0)
                    STEPS = 6

                    def window(g, w, i, l, b):
                        link = Chain(v, dve_step, g * STEPS)
                        v.wait_ge(l_ok, g + 1 + L0)
                        link(v.tensor_tensor_scan(runmax[:, :], rp[b][:, 0:W], lg[b][:, :], carry[:, 0:1],
                                                  ALU.min, ALU.max))
                        v.tensor_tensor_scan(segmax[:, ::-1], rp[b][:, 1:W + 1][:, ::-1], runmax[:, ::-1], -BIG,
                                             ALU.min, ALU.max).then_inc(max_ok, 1)
                        v.wait_ge(max_ok, g + 1 + M0)
                        v.tensor_scalar(ex[:, 0:1], segmax[:, 0:1], carry[:, 0:1], 0.0, ALU.subtract, ALU.max)
                        v.tensor_copy(wmax[:, bass.ds(w, 1)], segmax[:, 0:1])
                        v.tensor_tensor(ex[:, 1:W + 1], segmax[:, :], lg[b][:, :], ALU.subtract).then_inc(diff_ok, 1)
                        v.wait_ge(diff_ok, g + 1)
                        link(v.tensor_copy(carry[:, 0:1], runmax[:, W - 1:W]))
                        v.wait_ge(ex_ok, g + 1)
                        link(v.tensor_scalar(start2[:, :], carry[:, 1:3], ex[:, 0:1], None, ALU.mult))
                        v.wait_ge(back_ps, BU * (g - 1) + BP0)
                        v.tensor_tensor_scan(den[b][:, :], keep[b][:, :], ex[:, 1:W + 1], start2[:, 0:1],
                                             ALU.mult, ALU.add).then_inc(den_ok, 1)
                        link(v.scalar_tensor_tensor(out=uex[:, :], in0=u[b][:, :], scalar=EPS, in1=ex[:, 1:W + 1],
                                                    op0=ALU.add, op1=ALU.mult))
                        v.tensor_tensor_scan(num[b][:, :], keep[b][:, :], uex[:, :], start2[:, 1:2],
                                             ALU.mult, ALU.add).then_inc(sums_ok, 1)
                        v.wait_ge(sums_ok, g + 1 + S0)
                        link(v.tensor_copy(carry[:, 1:2], den[b][:, W - 1:W]))
                        link(v.tensor_copy(carry[:, 2:3], num[b][:, W - 1:W]))

                    v.memset(x_acc[:, :, :], 0.0)
                    v.memset(ln_eps[:, :], LN_EPS)

                    link = Chain(v, centre_step)
                    for n, (mat, parts, width) in enumerate(((W1s, D + 1, D2), (W2s, D2, D), (b2s, P, D))):
                        mean = wmean[0:parts, n, :]
                        link(v.tensor_reduce(mean, mat[:, :, :], AX_X, ALU.add))
                        link(v.tensor_scalar(mean, mean, 1.0 / width, None, ALU.mult))
                        link(v.tensor_tensor(mat[:, :, :], mat[:, :, :], mean.unsqueeze(2).broadcast_to([parts, L, width]),
                                             ALU.subtract))
                    v.memset(hinT[D:D + 1, :], 1.0)
                    PER_LAYER = 5 + MC * 3
                    with v.Fori(0, L) as l:
                        link = Chain(v, node_step, l * PER_LAYER)
                        v.memset(carry[:, 0:1], -BIG)
                        v.memset(carry[:, 1:4], 0.0)
                        v.tensor_copy(W1c[:, :], W1s[:, bass.ds(l, 1), :].rearrange("k l m -> k (l m)"))
                        v.tensor_copy(W2c[:, :], W2s[:, bass.ds(l, 1), :].rearrange("k l m -> k (l m)"))
                        v.wait_ge(ha_ok, MC * l + 1)
                        v.tensor_copy(ncur[:, 0:1, :], nGs[:, bass.ds(l, 1), :])
                        v.tensor_copy(ncur[:, 1:2, :], nBs[:, bass.ds(l, 1), :])
                        v.tensor_copy(lncur[:, 0:1], lnGs[:, bass.ds(l, 1)])
                        v.tensor_copy(lncur[:, 1:2], lnBs[:, bass.ds(l, 1)])
                        v.tensor_tensor(x_acc[:, :, :], x_acc[:, :, :], b2s[:, bass.ds(l, 1), :].broadcast_to([P, NT, D]),
                                        ALU.add)
                        link(v.tensor_copy(tcur[:, 0:1], ts[:, bass.ds(l, 1)]))
                        v.tensor_scalar(tcur[:, 1:2], tcur[:, 0:1], EPS, None, ALU.mult).then_inc(tcur_ok, 1)
                        with v.Fori(0, PAIRS) as i:
                            for b in range(2):
                                window(l * NW + 2 * i + b, 2 * i + b, i, l, b)

                        v.wait_ge(dve_step, (l + 1) * NW * STEPS)
                        v.tensor_tensor_reduce(wjunk[:, :], wmax[:, :], win_hot[:, :], 1.0, 0.0, ALU.mult, ALU.add,
                                               carry[:, 3:4]).then_inc(carry_ok, 1)
                        v.wait_ge(prow_ps, l + 1)
                        link(v.tensor_copy(prow.rearrange("p a d -> p (a d)"), ps[3][0:1, :]))
                        link(v.tensor_scalar(prow[:, 0, 0:D], prow[:, 0, 0:D], cpen[:, 0:1], None, ALU.min))
                        link(v.tensor_tensor(pmax[:, :], prow[:, 0, 0:D], prow[:, 3, D:D2], ALU.max))
                        v.tensor_tensor(pdiff[:, 0, :], pmax[:, :], prow[:, 0, 0:D], ALU.subtract)
                        v.tensor_tensor(pdiff[:, 1, :], pmax[:, :], prow[:, 3, D:D2], ALU.subtract).then_inc(pdiff_ok, 1)
                        v.wait_ge(pexp_ok, l + 1)
                        v.wait_ge(pold_in, 16 * (l + 1))
                        both = [1, 2, D]
                        v.tensor_tensor(ptmp[:, :, :], prow[:, 1:3, 0:D], pdiff[:, 0:1, :].broadcast_to(both), ALU.mult)
                        link(v.tensor_tensor(pnew[:, :, :], pold[:, :, :], pdiff[:, 1:2, :].broadcast_to(both), ALU.mult))
                        v.tensor_tensor(pnew[:, :, :], pnew[:, :, :], ptmp[:, :, :], ALU.add).then_inc(pnew_ok, 1)

                        base = MC * l
                        for k in range(MC + 3):
                            if k < MC:
                                cs = slice(k * MT, (k + 1) * MT)
                                v.wait_ge(dn_in[k], 16 * MT * (l + 1))
                                if k:
                                    v.wait_ge(hinT_ps, base + k)
                                link(v.reciprocal(rec[:, :, :], dn[:, cs, 0:D]))
                                v.tensor_tensor(hin[:, :, :], dn[:, cs, D:D2], rec[:, :, :], ALU.mult).then_inc(hin_ok, 1)
                            if 1 < k < MC + 2:
                                cs = slice((k - 2) * MT, (k - 1) * MT)
                                v.wait_ge(o_ps, base + k - 1)
                                v.tensor_tensor(x_acc[:, cs, :], x_acc[:, cs, :], ps[2][:, 0:MT * D].rearrange("p (t d) -> p t d", d=D),
                                                ALU.add).then_inc(x_ok, 1)
                            if 0 < k <= MC:
                                v.wait_ge(yroot_ok, base + k)
                                if k > 1:
                                    v.wait_ge(yT_ps, base + k - 1)
                                link(v.reciprocal(yinv[:, :], yroot[:, (k - 1) % 2, :]))
                                v.tensor_tensor(y[:, :, :], ps[6 + (k - 1) % 2].rearrange("p (t d) -> p t d", d=D2),
                                                yinv.unsqueeze(2).broadcast_to([P, MT, D2]), ALU.mult).then_inc(y_ok, 1)
                            if k > 2:
                                cs = slice((k - 3) * MT, (k - 2) * MT)
                                v.wait_ge(xroot_ok, base + k - 2)
                                if k > 3:
                                    v.wait_ge(hn_ok, base + k - 3)
                                link(v.reciprocal(xinv[:, :], xroot[:, (k - 3) % 2, :]))
                                v.tensor_tensor(h_cur[:, cs, :], x_acc[:, cs, :],
                                                xinv.unsqueeze(2).broadcast_to([P, MT, D]), ALU.mult).then_inc(hn_ok, 1)
                        assert link.n == PER_LAYER, link.n

        with ExitStack() as c:
            TW = 2 * K
            TB = 8
            NB = TW // TB
            hd = [sb(f"hd{i}", [P, 2, K, D], F32, c) for i in range(2)]
            hdT = [sb(f"hdT{i}", [P, W], F32, c) for i in range(2)]
            hs = [sb(f"hs{i}", [P, W], F32, c) for i in range(2)]
            rp = [sb(f"run{i}", [P, W], BF16, c) for i in range(2)]
            keep = [sb(f"kept{i}", [P, W], BF16, c) for i in range(2)]
            gh = [sb(f"gh{i}", [P, K, 2, D], F32, c) for i in range(2)]
            vm = [sb(f"vm{i}", [P, TW, D], F32, c) for i in range(2)]
            srcB = [sb(f"srcB{i}", [P, 2, W], F32, c) for i in range(2)]
            sf = [sb(f"sf{i}", [P, 2, K], F32, c) for i in range(2)]
            wl = [sb(f"wl{i}", [P, 2, K], F32, c) for i in range(2)]
            flat = sb("flat", [P, K, 2], F32, c)
            dup = sb("dup", [P, TW], F32, c)
            move = sb("move", [P, TW], F32, c)
            tgt = [sb(f"tgt{i}", [P, TW], I32, c) for i in range(2)]
            eqw = sb("eqw", [P, NB, TB, P], F32, c)
            tri = sb("tri", [P, P], F32, c)
            djunk = sb("djunk", [P, P], F32, c)
            trash_i = sb("trash_i", [P, 1], I32, c)
            trash = sb("trash", [P, 1], F32, c)
            hT = sb("hT", [D, 2, MT * P], F32, c)
            squares = sb("squares", [P, MT, D], BF16, c)
            froot = sb("froot", [P, 2, MT], F32, c)
            fmean = sb("fmean", [P, MT], F32, c)
            finv = sb("finv", [P, MT], F32, c)
            xin = sb("xin", [P, NT, D], F32, c)
            tabs = [x_acc, h_cur]

            fx_in, fclr, ftri, ftrash, fT_ps, fT_sb, fo_ps, fo_ok, f_step, fh_ok, h2_out, hb_in = (
                sem(f"f_{n}") for n in ("xin", "clr", "tri", "trash", "Tps", "Tsb", "ops", "ook", "step", "hok", "h2out",
                                        "hbin"))
            lin_ok, fc_ok, fsum_ok, froot_ok = (sem(f"f_{n}") for n in ("lin", "centred", "sum", "root"))
            hd_in, ls_in, run_in = ([sem(f"{n}{i}") for i in range(2)] for n in ("hd_in", "ls_in", "run_in"))
            added = [sem(f"added{i}") for i in range(ACCS)]
            heads_out, hdT_ps, hdT_sb, scan_ok, gh_ps, gh_sb = (
                sem(n) for n in ("heads_out", "hdT_ps", "hdT_sb", "scan_ok", "gh_ps", "gh_sb"))
            eq_ok, merged_ps, v_sb, tgt_ok, m_step, scat_go, landed = (
                sem(n) for n in ("eq_ok", "merged_ps", "v_sb", "tgt_ok", "m_step", "scat_go", "landed"))
            tab_in, tab_sum, out_ok = [sem("tab_in0"), sem("tab_in1")], sem("tab_sum"), sem("out_ok")
            MP0, V0, T0, HP0, HS0, SC0, GP0, GS0 = 2 * NB, 2, 2, 2 * NG, NG, 2, 2 * NG, NG
            HBANK, GBANK, MBANK = (0, 1, 2), (3, 6, 7), (4, 5)
            ROUNDS = TW // ACCS
            PAIRS = NW // 2

            with nc.Block() as block:
                @block.sync
                def _(sp):
                    split = sp.value_load(patch_i[0:1, 1:2], min_val=0, max_val=N - 1)
                    heads = run_head[0:EPAD, :].rearrange("(h w p k) d -> h w p (k d)", h=2, w=NW, p=P)

                    def load_heads(w, b):
                        sp.wait_ge(hdT_ps, NG * w - NG + HP0)
                        for h in range(2):
                            sp.dma_start(hd[b][:, h, :, :].rearrange("p k d -> p (k d)"), heads[h, w]).then_inc(hd_in[b], 16)

                    def load_lists(w, b):
                        sp.wait_ge(scan_ok, w + 1)
                        for h in range(2):
                            sp.dma_start(rp[b][h * D:(h + 1) * D, :], run_pen[bass.ds(h * HALF + w * W, W)]
                                         .partition_broadcast(D)).then_inc(run_in[b], 16)
                        sp.wait_ge(tgt_ok, w + 1)
                        sp.sem_inc(load_go, 1)
                        for h in range(2):
                            piece = bass.ds(h * HALF + w * W, W)
                            for dest, lst in ((sf, src_flat), (wl, wgt_flat)):
                                sp.dma_start(dest[b][:, h, :], lst[piece].rearrange("(p k) -> p k", k=K)).then_inc(ls_in[b], 16)
                            sp.dma_start(srcB[b][:, h, :], src_flat[bass.ds(h * HALF + w * W, W)]
                                         .partition_broadcast(P)).then_inc(ls_in[b], 16)

                    sp.wait_ge(fclr, 1)
                    sp.dma_start(xin[0:N // NT, :, :].rearrange("p t d -> p (t d)"),
                                 x.rearrange("(p t) d -> p (t d)", t=NT)).then_inc(fx_in, 16)
                    for b in range(2):
                        load_lists(b, b)
                    sp.wait_ge(fh_ok, MC)
                    sp.dma_start(h_tab.rearrange("(p t) d -> p (t d)", t=NT),
                                 h_cur.rearrange("p t d -> p (t d)")).then_inc(h2_out, 16)
                    sp.wait_ge(h2_out, 16)
                    with nc.allow_non_contiguous_dma("one row, as a column"):
                        sp.dma_start(hs[1][D:D2, W - 1:W], h_tab[bass.ds(split, 1), :].rearrange("a d -> d a")
                                     ).then_inc(hb_in, 16)
                    sp.wait_ge(heads_out, 16 * NT)
                    load_heads(0, 0)
                    load_heads(1, 1)
                    with sp.Fori(1, PAIRS) as i:
                        for b in range(2):
                            load_heads(2 * i + b, b)
                            load_lists(2 * i + b, b)
                    for i, a in enumerate(acc):
                        sp.wait_ge(added[i], 16 * ROUNDS * NW)
                        if i >= 2:
                            sp.wait_ge(tab_sum, i - 1)
                        sp.dma_start(tabs[i % 2].rearrange("p t d -> p (t d)"),
                                     a[0:NPAD, :].rearrange("(p t) d -> p (t d)", t=NT)).then_inc(tab_in[i % 2], 16)
                    sp.wait_ge(tab_sum, ACCS)
                    sp.dma_start(out.rearrange("(p t) d -> p (t d)", t=NT),
                                 xin[0:N // NT, :, :].rearrange("p t d -> p (t d)")).then_inc(out_ok, 16)
                    sp.wait_ge(out_ok, 16)

                @block.gpsimd
                def _(g_):
                    g_.sem_inc(landed, 1)
                    g_.iota(trash_i[:, :], [[1, 1]], TRASH, 1).then_inc(ftrash, 1)
                    g_.wait_ge(fclr, 2)
                    g_.affine_select(out=tri[:, :], in_=tri[:, :], compare_op=ALU.is_gt, fill=0.0, base=0,
                                     pattern=[[-1, P]], channel_multiplier=1).then_inc(ftri, 1)
                    for t_ in range(NT):
                        if t_ % MT == 0:
                            g_.wait_ge(fh_ok, t_ // MT + 1)
                        g_.indirect_dma_start(run_head[:, :], bass.IndirectOffsetOnAxis(
                            ap=first_idx[:, t_:t_ + 1], axis=0), h_cur[:, t_, :], None).then_inc(heads_out, 16)

                    def scatter(w, b, first=False):
                        g_.wait_ge(v_sb, NB * (w + 1) + V0)
                        g_.sem_inc(scat_go, 1)
                        g_.wait_ge(tgt_ok, w + 1 + T0)
                        g_.sem_inc(scat_go, 1)
                        for t_ in range(TW):
                            i, r = t_ % ACCS, t_ // ACCS
                            if not first or r:
                                g_.wait_ge(added[i], 16 * (ROUNDS * w + r))
                                g_.sem_inc(landed if t_ == ACCS - 1 else scat_go, 1)
                            elif t_ == ACCS - 1:
                                g_.sem_inc(landed, 1)
                            g_.indirect_dma_start(acc[i][:, :], bass.IndirectOffsetOnAxis(
                                ap=tgt[b][:, t_:t_ + 1], axis=0), vm[b][:, t_, :], None,
                                compute_op=ALU.add).then_inc(added[i], 16)

                    scatter(0, 0, first=True)
                    with g_.Fori(1, PAIRS) as i:
                        scatter(2 * i - 1, 1)
                        scatter(2 * i, 0)
                    scatter(NW - 1, 1)

                @block.tensor
                def _(pe):
                    pe.sem_inc(merged_ps, MP0)
                    pe.sem_inc(hdT_ps, HP0)
                    pe.sem_inc(gh_ps, GP0)
                    for k in range(MC):
                        s_ = k % 2
                        if k > 1:
                            pe.wait_ge(fT_sb, k - 1)
                        for j in range(MT):
                            ins = pe.transpose(ps[s_][0:D, j * P:(j + 1) * P], h_cur[:, k * MT + j, :], ident[:, :])
                        ins.then_inc(fT_ps, 1)
                        pe.wait_ge(fT_sb, k + 1)
                        if k > 1:
                            pe.wait_ge(fo_ok, k - 1)
                        for j in range(MT):
                            ins = pe.matmul(ps[2 + s_][:, j * D:(j + 1) * D], hT[:, s_, j * P:(j + 1) * P], linWs[:, :],
                                            start=True, stop=True)
                        ins.then_inc(fo_ps, 1)
                    pe.wait_ge(fo_ok, MC)

                    def forward(w, i, b):
                        pe.wait_ge(hd_in[b], 32 * (i + 1))
                        for gr in range(NG):
                            pe.wait_ge(hdT_sb, NG * w + gr + 1 - NG + HS0)
                            for j in range(GT):
                                for h in range(2):
                                    ins = pe.matmul(ps[HBANK[gr]][h * D:(h + 1) * D, j * P:(j + 1) * P],
                                                    hd[b][:, h, gr * GT + j, :], ident[:, :], start=True, stop=True)
                            ins.then_inc(hdT_ps, 1)

                    def merge(w, b):
                        pe.wait_ge(scan_ok, w + 1 + SC0)
                        for gr in range(NG):
                            pe.wait_ge(gh_sb, NG * w + gr + 1 - NG + GS0)
                            for j in range(GT):
                                ins = pe.transpose(ps[GBANK[gr]][:, j * P:(j + 1) * P],
                                                   hs[b].rearrange("c (p k) -> c k p", k=K)[:, gr * GT + j, :],
                                                   ident[:, :])
                            ins.then_inc(gh_ps, 1)
                        for q in range(NB):
                            slot = (NB * b + q) % 2
                            pe.wait_ge(gh_sb, NG * w + q + 1 + GS0)
                            pe.wait_ge(eq_ok, NB * w + q + 1)
                            pe.wait_ge(v_sb, NB * w + q + 1 - 2 + V0)
                            for j in range(TB):
                                t_ = q * TB + j
                                ins = pe.matmul(ps[MBANK[slot]][:, j * D:(j + 1) * D], eqw[:, q, j, :],
                                                gh[b][:, t_ // 2, t_ % 2, :], start=True, stop=True)
                            ins.then_inc(merged_ps, 1)

                    forward(0, 0, 0)
                    with pe.Fori(0, PAIRS - 1) as i:
                        forward(2 * i + 1, i, 1)
                        merge(2 * i, 0)
                        forward(2 * i + 2, i + 1, 0)
                        merge(2 * i + 1, 1)
                    forward(NW - 1, PAIRS - 1, 1)
                    merge(NW - 2, 0)
                    merge(NW - 1, 1)

                @block.scalar
                def _(a):
                    a.sem_inc(v_sb, V0)
                    a.sem_inc(hdT_sb, HS0)
                    a.sem_inc(gh_sb, GS0)
                    for k in range(MC + 1):
                        if k < MC:
                            a.wait_ge(fT_ps, k + 1)
                            if k > 1:
                                a.wait_ge(fo_ps, k - 1)
                            a.activation(hT[:, k % 2, :], ps[k % 2][0:D, :], ACT.Copy).then_inc(fT_sb, 1)
                        if k:
                            a.wait_ge(fc_ok, k)
                            for j in range(MT):
                                ins = a.activation(squares[:, j, :], h_cur[:, (k - 1) * MT + j, :], ACT.Square,
                                                   accum_out=froot[:, (k - 1) % 2, j:j + 1])
                            ins.then_inc(fsum_ok, 1)
                            a.wait_ge(fsum_ok, k)
                            root = froot[:, (k - 1) % 2, :]
                            a.activation(root, root, ACT.Sqrt, scale=1.0 / D, bias=ln_eps[:, 0:1]).then_inc(froot_ok, 1)

                    def heads(w, i, b):
                        a.wait_ge(scan_ok, w + 1)
                        a.wait_ge(run_in[b], 32 * (i + 1))
                        a.activation(keep[b][:, :], rp[b][:, :], ACT.Relu, scale=1.0 / BIG)
                        for gr in range(NG):
                            a.wait_ge(hdT_ps, NG * w + gr + 1 + HP0)
                            a.activation(hdT[b].rearrange("c (p k) -> c k p", k=K)[:, gr * GT:(gr + 1) * GT, :],
                                         ps[HBANK[gr]].rearrange("c (k p) -> c k p", p=P), ACT.Copy).then_inc(hdT_sb, 1)

                    def rows(w, b):
                        a.wait_ge(merged_ps, NB * (w - 1) + MP0)
                        for gr in range(NG):
                            a.wait_ge(gh_ps, NG * w + gr + 1 + GP0)
                            a.activation(gh[b].rearrange("p k h d -> p (k h d)")[:, gr * 512:(gr + 1) * 512],
                                         ps[GBANK[gr]][:, :], ACT.Copy).then_inc(gh_sb, 1)
                        a.wait_ge(landed, w + 1)
                        for q in range(NB):
                            a.wait_ge(merged_ps, NB * w + q + 1 + MP0)
                            a.activation(vm[b].rearrange("p t d -> p (t d)")[:, q * 512:(q + 1) * 512],
                                         ps[MBANK[(NB * b + q) % 2]][:, :], ACT.Copy).then_inc(v_sb, 1)

                    heads(0, 0, 0)
                    with a.Fori(0, PAIRS - 1) as i:
                        heads(2 * i + 1, i, 1)
                        rows(2 * i, 0)
                        heads(2 * i + 2, i + 1, 0)
                        rows(2 * i + 1, 1)
                    heads(NW - 1, PAIRS - 1, 1)
                    rows(NW - 2, 0)
                    rows(NW - 1, 1)

                @block.vector
                def _(v):
                    v.sem_inc(tgt_ok, T0)
                    v.sem_inc(scan_ok, SC0)
                    v.memset(xin[:, :, :], 0.0).then_inc(fclr, 1)
                    v.memset(tri[:, :], 1.0).then_inc(fclr, 1)
                    link = Chain(v, f_step)
                    link(v.memset(hs[1][0:D, W - 1:W], 0.0))
                    v.wait_ge(ftrash, 1)
                    link(v.tensor_copy(trash[:, :], trash_i[:, :]))
                    v.wait_ge(fx_in, 16)
                    v.tensor_tensor(xin[:, :, :], xin[:, :, :], linbs.unsqueeze(1).broadcast_to([P, NT, D]), ALU.add
                                    ).then_inc(lin_ok, 1)
                    v.wait_ge(lin_ok, 1)
                    for k in range(MC + 1):
                        if k:
                            v.wait_ge(fc_ok, k)
                        if k < MC:
                            cs = slice(k * MT, (k + 1) * MT)
                            v.wait_ge(fo_ps, k + 1)
                            v.tensor_tensor(xin[:, cs, :], xin[:, cs, :],
                                            ps[2 + k % 2][:, 0:MT * D].rearrange("p (t d) -> p t d", d=D), ALU.add
                                            ).then_inc(fo_ok, 1)
                            v.wait_ge(fo_ok, k + 1)
                            link(v.tensor_reduce(fmean[:, :], xin[:, cs, :], AX_X, ALU.add))
                            link(v.tensor_scalar(fmean[:, :], fmean[:, :], 1.0 / D, None, ALU.mult))
                            v.tensor_tensor(h_cur[:, cs, :], xin[:, cs, :], fmean.unsqueeze(2).broadcast_to([P, MT, D]),
                                            ALU.subtract).then_inc(fc_ok, 1)
                        if k:
                            cs = slice((k - 1) * MT, k * MT)
                            v.wait_ge(froot_ok, k)
                            link(v.reciprocal(finv[:, :], froot[:, (k - 1) % 2, :]))
                            link(v.tensor_tensor(h_cur[:, cs, :], h_cur[:, cs, :],
                                                 finv.unsqueeze(2).broadcast_to([P, MT, D]), ALU.mult))
                            v.tensor_scalar(h_cur[:, cs, :], h_cur[:, cs, :], 0.0, None, ALU.max).then_inc(fh_ok, 1)
                    v.wait_ge(ftri, 1)
                    MS = TW + 4

                    def spread(w, b):
                        v.wait_ge(hdT_sb, NG * (w + 1) + HS0)
                        v.wait_ge(gh_ps, NG * (w - 1) + GP0)
                        v.tensor_tensor_scan(hs[b][:, :], keep[b][:, :], hdT[b][:, :], hs[1 - b][:, W - 1:W],
                                             ALU.mult, ALU.add).then_inc(scan_ok, 1)
                        v.wait_ge(scan_ok, w + 1 + SC0)

                    def targets(w, i, b):
                        link = Chain(v, m_step, w * MS)
                        v.wait_ge(ls_in[b], 96 * (i + 1))
                        for t_ in range(TW):
                            k, h = t_ // 2, t_ % 2
                            q = t_ // TB
                            if t_ % TB == 0:
                                v.wait_ge(merged_ps, NB * (w - 1) + q + 1 + MP0)
                            row = srcB[b][:, h, :].rearrange("p (e k) -> p k e", k=K)[:, k, :]
                            ins = v.tensor_scalar(eqw[:, q, t_ % TB, :], row, sf[b][:, h, k:k + 1],
                                                  wl[b][:, h, k:k + 1], ALU.is_equal, ALU.mult)
                            if t_ % TB == TB - 1:
                                ins.then_inc(eq_ok, 1)
                            link(v.scalar_tensor_tensor(out=djunk[:, :], in0=row, scalar=sf[b][:, h, k:k + 1], in1=tri[:, :],
                                                        op0=ALU.is_equal, op1=ALU.mult, accum_out=dup[:, t_:t_ + 1]))
                        v.wait_ge(landed, w + 1)
                        srcs = flat.rearrange("p k h -> p (k h)")
                        v.tensor_copy(flat[:, :, :], sf[b].rearrange("p h k -> p k h"))
                        link(v.tensor_scalar(dup[:, :], dup[:, :], 1.0, None, ALU.min))
                        link(v.tensor_scalar(move[:, :], srcs, -1.0, trash[:, 0:1], ALU.mult, ALU.add))
                        link(v.tensor_tensor(move[:, :], move[:, :], dup[:, :], ALU.mult))
                        link(v.tensor_tensor(move[:, :], move[:, :], srcs, ALU.add))
                        v.tensor_copy(tgt[b][:, :], move[:, :]).then_inc(tgt_ok, 1)

                    targets(0, 0, 0)
                    v.wait_ge(hb_in, 16)
                    spread(0, 0)
                    spread(1, 1)
                    targets(1, 0, 1)
                    with v.Fori(1, PAIRS) as i:
                        spread(2 * i, 0)
                        targets(2 * i, i, 0)
                        spread(2 * i + 1, 1)
                        targets(2 * i + 1, i, 1)
                    for i in range(ACCS):
                        v.wait_ge(tab_in[i % 2], 16 * (i // 2 + 1))
                        v.tensor_tensor(xin[:, :, :], xin[:, :, :], tabs[i % 2][:, :, :], ALU.add).then_inc(tab_sum, 1)
                        v.wait_ge(tab_sum, i + 1)


_INS = ['x', 'src', 'dst', 'edge_attr_64', 'edge_weight', 'L0_gnn_encW', 'L0_gnn_encb', 'L0_gnn_eencW', 'L0_gnn_eencb',
        'L0_gnn_convW1', 'L0_gnn_convb1', 'L0_gnn_convLnG', 'L0_gnn_convLnB', 'L0_gnn_convW2', 'L0_gnn_convb2', 'L0_gnn_t',
        'L0_gnn_normG', 'L0_gnn_normB', 'L0_gnn_linW', 'L0_gnn_linb']
_OUTS = [((N, D), 'float32')]


def kernel(**inputs):
    import numpy as _np
    import concourse.bacc as _bacc
    from concourse import mybir as _mybir
    from concourse.bass_utils import run_bass_kernel_spmd as _run

    nc = _bacc.Bacc("TRN2", target_bir_lowering=False, num_devices=1)
    arrays, args = {}, []
    for name in _INS:
        a = _np.ascontiguousarray(inputs[name])
        arrays[f"in_{name}_dram"] = a
        args.append(nc.dram_tensor(f"in_{name}_dram", a.shape, _mybir.dt.from_np(a.dtype), kind="ExternalInput").ap())
    for i, (shape, dtype) in enumerate(_OUTS):
        dt = _mybir.dt.from_np(_np.dtype(dtype))
        args.append(nc.dram_tensor(f"out_{i}_dram", shape, dt, kind="ExternalOutput").ap())
    gnn(nc, *args)
    r = _run(nc, [arrays], core_ids=[0])
    got = tuple(r.results[0][f"out_{i}_dram"] for i in range(len(_OUTS)))
    return got[0]
```
